# Optimizing a Trainium2 kernel written in Bass

```python
import numpy as np
import jax
import jax.numpy as jnp

def _softmax(x, axis=-1):
    return jax.nn.softmax(x, axis=axis)

def _gelu(x):
    return jax.nn.gelu(x, approximate=True)

def _silu(x):
    return jax.nn.silu(x)

def _sigmoid(x):
    return jax.nn.sigmoid(x)

def _layernorm(x, axis=-1, eps=1e-05):
    m = jnp.mean(x, axis=axis, keepdims=True)
    v = jnp.var(x, axis=axis, keepdims=True)
    return (x - m) / jnp.sqrt(v + eps)

def _scatter_add(tgt, idx, src, axis=0):
    return tgt.at[idx].add(src)

def _segment_sum(src, seg, n):
    return jax.ops.segment_sum(src, seg, n)
kernel_name = 'mk_xattn_ffn_d2_seqx_r4_d37f6e'

def setup_inputs(seed: int=0):
    np.random.seed(seed)
    _w = jnp.asarray

    def _rec_inputs():
        import jax
        import jax.numpy as jnp
        _rk = jax.random.key(seed)
        x = -0.0002928 + 1 * jax.random.normal(jax.random.fold_in(_rk, 1), (8, 512, 256), jnp.float32)
        _lenS = 512 - jax.random.randint(jax.random.fold_in(_rk, 7), (8,), 0, max(1, 512 // 4) + 1, jnp.int32)
        _lenS2 = 512 - jax.random.randint(jax.random.fold_in(_rk, 8), (8,), 0, max(1, 512 // 4) + 1, jnp.int32)
        _ctx_1024P = jax.random.normal(jax.random.fold_in(_rk, 11), (8, 16, 256), jnp.float32)
        _ctx_1024c = jax.random.dirichlet(jax.random.fold_in(_rk, 511), 0.3 * jnp.ones((16,), jnp.float32), (8, 512))
        _ctx_1024t = jnp.einsum('bsk,bkd->bsd', _ctx_1024c, _ctx_1024P)
        _ctx_1024t = _ctx_1024t * jax.lax.rsqrt(jnp.mean(jnp.square(_ctx_1024t)) + 1e-12) * 0.953939
        ctx_1024 = -1.39393e-06 + 0.999914 * (_ctx_1024t + 0.3 * jax.random.normal(jax.random.fold_in(_rk, 611), (8, 512, 256), jnp.float32))
        return (x, ctx_1024)
    x, ctx_1024 = _rec_inputs()

    def _L0_xattn_setup():
        import jax, jax.numpy as jnp
        import numpy as np
        EPS_BACKEND = 1e-06
        NORM_EPS = 1e-06
        NUM_HEADS = 4

        def _mlstm_forward(q, k, v, ig_kernel, ig_bias, fg_kernel, fg_bias, outnorm_weight):
            B, S, E = q.shape
            NH = ig_bias.shape[0]
            DH = E // NH
            gate_input = jnp.concatenate([q, k, v], axis=-1)
            igate = gate_input @ ig_kernel + ig_bias
            fgate = gate_input @ fg_kernel + fg_bias
            qh = q.reshape(B, S, NH, DH).transpose(0, 2, 1, 3)
            kh = k.reshape(B, S, NH, DH).transpose(0, 2, 1, 3)
            vh = v.reshape(B, S, NH, DH).transpose(0, 2, 1, 3)
            ig = igate.transpose(0, 2, 1)
            fg = fgate.transpose(0, 2, 1)
            log_fg = jax.nn.log_sigmoid(fg)
            cums = jnp.concatenate([jnp.zeros((B, NH, 1), log_fg.dtype), jnp.cumsum(log_fg, axis=-1)], axis=-1)
            fg_mat = cums[..., :, None] - cums[..., None, :]
            mask = jnp.tril(jnp.ones((S + 1, S + 1), bool))
            fg_mat = jnp.where(mask, fg_mat, -jnp.inf)[..., 1:, 1:]
            log_D = fg_mat + ig[..., None, :]
            max_log_D = jnp.max(log_D, axis=-1, keepdims=True)
            D = jnp.exp(log_D - max_log_D)
            qk = jnp.einsum('bnsd,bntd->bnst', qh, kh) / jnp.sqrt(jnp.float32(DH))
            C = qk * D
            normalizer = jnp.maximum(jnp.abs(C.sum(-1, keepdims=True)), jnp.exp(-max_log_D))
            h = jnp.einsum('bnst,bntd->bnsd', C / (normalizer + EPS_BACKEND), vh)
            h = h.transpose(0, 2, 1, 3)
            mean = h.mean(-1, keepdims=True)
            var = h.var(-1, keepdims=True)
            hn = (h - mean) * jax.lax.rsqrt(var + NORM_EPS) * outnorm_weight
            return hn.reshape(B, S, E)
        key = jax.random.key(seed)
        ks = jax.random.split(key, 8)
        B, S, E, NH = (2, 512, 256, NUM_HEADS)
        DH = E // NH
        q = jax.random.normal(ks[0], (B, S, E), jnp.float32)
        k = jax.random.normal(ks[1], (B, S, E), jnp.float32)
        v = jax.random.normal(ks[2], (B, S, E), jnp.float32)
        ig_kernel = jax.random.normal(ks[3], (3 * E, NH), jnp.float32) * 0.02
        fg_kernel = jax.random.normal(ks[4], (3 * E, NH), jnp.float32) * 0.02
        ig_bias = jax.random.normal(ks[5], (NH,), jnp.float32) * 0.1
        fg_bias = jnp.linspace(3.0, 6.0, NH, dtype=jnp.float32)
        outnorm_weight = jnp.ones((NH, DH), jnp.float32)
        return {'q': q, 'k': k, 'v': v, 'ig_kernel': ig_kernel, 'ig_bias': ig_bias, 'fg_kernel': fg_kernel, 'fg_bias': fg_bias, 'outnorm_weight': outnorm_weight}
    _L0_xattn_all = _L0_xattn_setup()
    _L0_xattn_in = {k: v for k, v in _L0_xattn_all.items() if k in ('ig_kernel', 'ig_bias', 'fg_kernel', 'fg_bias', 'outnorm_weight')}
    del _L0_xattn_all

    def _L0_ffn_setup():
        import jax, jax.numpy as jnp
        import numpy as np
        N_EMBD = 256
        N_STATE = 1024
        key = jax.random.key(seed)
        k_x, k_w1, k_b1, k_w2, k_b2 = jax.random.split(key, 5)
        x = jax.random.normal(k_x, (4, 512, N_EMBD), dtype=jnp.float32)
        w1 = jax.random.normal(k_w1, (N_EMBD, N_STATE), dtype=jnp.float32) * (1.0 / np.sqrt(N_EMBD))
        b1 = jax.random.normal(k_b1, (N_STATE,), dtype=jnp.float32) * 0.02
        w2 = jax.random.normal(k_w2, (N_STATE, N_EMBD), dtype=jnp.float32) * (1.0 / np.sqrt(N_STATE))
        b2 = jax.random.normal(k_b2, (N_EMBD,), dtype=jnp.float32) * 0.02
        return {'x': x, 'w1': w1, 'b1': b1, 'w2': w2, 'b2': b2}
    _L0_ffn_all = _L0_ffn_setup()
    _L0_ffn_in = {k: v for k, v in _L0_ffn_all.items() if k in ('w1', 'b1', 'w2', 'b2')}
    del _L0_ffn_all

    def _L1_xattn_setup():
        import jax, jax.numpy as jnp
        import numpy as np
        HEAD_NUM = 16
        KEY_DIM = 64
        EMBED = 256
        KV_OUT = HEAD_NUM * KEY_DIM
        key = jax.random.key(seed)
        ks = jax.random.split(key, 11)
        B, L, E = (2, 512, EMBED)
        scale = 0.02
        return {'query': jax.random.normal(ks[0], (B, L, E), jnp.float32), 'key': jax.random.normal(ks[1], (B, L, E), jnp.float32), 'value': jax.random.normal(ks[2], (B, L, E), jnp.float32), 'W_Query': jax.random.normal(ks[3], (E, KV_OUT), jnp.float32) * scale, 'W_Key': jax.random.normal(ks[4], (E, KV_OUT), jnp.float32) * scale, 'W_Value': jax.random.normal(ks[5], (E, KV_OUT), jnp.float32) * scale, 'W_Output': jax.random.normal(ks[6], (KV_OUT, E), jnp.float32) * scale, 'B_Query': jnp.zeros((KV_OUT,), jnp.float32), 'B_Key': jnp.zeros((KV_OUT,), jnp.float32), 'B_Value': jnp.zeros((KV_OUT,), jnp.float32), 'B_Output': jnp.zeros((E,), jnp.float32)}
    _L1_xattn_all = _L1_xattn_setup()
    _L1_xattn_in = {k: v for k, v in _L1_xattn_all.items() if k in ('W_Query', 'W_Key', 'W_Value', 'W_Output', 'B_Query', 'B_Key', 'B_Value', 'B_Output')}
    del _L1_xattn_all

    def _L1_ffn_setup():
        import math
        import jax, jax.numpy as jnp
        import numpy as np
        D_MODEL = 256
        NUM_EXPERTS = 8
        D_FF_EXPERT = max(64, int(D_MODEL * 4 * 0.25))
        THRESHOLD = 0.9
        CAP_FACTOR = 1.0
        INIT_STD = 0.02

        def _xmoe_route(probs):
            N, E = probs.shape
            order = jnp.argsort(-probs, axis=-1)
            p_sorted = jnp.take_along_axis(probs, order, axis=-1)
            csum = jnp.cumsum(p_sorted, axis=-1)
            reached = (csum >= THRESHOLD).at[:, -1].set(True)
            k_idx = jnp.argmax(reached, axis=-1)
            select_prefix = jnp.arange(E)[None, :] <= k_idx[:, None]
            rows = jnp.arange(N)[:, None]
            assign_mask = jnp.zeros((N, E), dtype=bool).at[rows, order].set(select_prefix)
            rank = jnp.arange(1, E + 1, dtype=probs.dtype)[None, :]
            R_sorted = jnp.where(select_prefix, p_sorted - rank, jnp.full_like(p_sorted, -1000000000.0))
            R = jnp.zeros((N, E), dtype=probs.dtype).at[rows, order].set(R_sorted)
            capacity = int(math.ceil(N / E) * CAP_FACTOR)
            C = min(capacity, N)
            tok_order = jnp.argsort(-R, axis=0)
            topC = tok_order[:C, :]
            keep = jnp.zeros((N, E), dtype=bool).at[topC, jnp.arange(E)[None, :]].set(True)
            final_mask = assign_mask & keep
            return jnp.where(final_mask, probs, jnp.zeros_like(probs))
        key = jax.random.key(seed)
        k_x, k_g, k_w1, k_w2 = jax.random.split(key, 4)
        B, T = (4, 512)
        x = jax.random.normal(k_x, (B, T, D_MODEL), dtype=jnp.float32)
        bound = 1.0 / math.sqrt(D_MODEL)
        gate_w = jax.random.uniform(k_g, (NUM_EXPERTS, D_MODEL), minval=-bound, maxval=bound, dtype=jnp.float32)
        w1 = INIT_STD * jax.random.normal(k_w1, (NUM_EXPERTS, D_FF_EXPERT, D_MODEL), dtype=jnp.float32)
        w2 = INIT_STD * jax.random.normal(k_w2, (NUM_EXPERTS, D_MODEL, D_FF_EXPERT), dtype=jnp.float32)
        return {'x': x, 'gate_w': gate_w, 'w1': w1, 'w2': w2}
    _L1_ffn_all = _L1_ffn_setup()
    _L1_ffn_in = {k: v for k, v in _L1_ffn_all.items() if k in ('gate_w', 'w1', 'w2')}
    del _L1_ffn_all
    return {'x': x, 'ctx_1024': ctx_1024, 'L0_xattn_ig_kernel': _L0_xattn_in['ig_kernel'], 'L0_xattn_ig_bias': _L0_xattn_in['ig_bias'], 'L0_xattn_fg_kernel': _L0_xattn_in['fg_kernel'], 'L0_xattn_fg_bias': _L0_xattn_in['fg_bias'], 'L0_xattn_outnorm_weight': _L0_xattn_in['outnorm_weight'], 'L0_ffn_w1': _L0_ffn_in['w1'], 'L0_ffn_b1': _L0_ffn_in['b1'], 'L0_ffn_w2': _L0_ffn_in['w2'], 'L0_ffn_b2': _L0_ffn_in['b2'], 'L1_xattn_W_Query': _L1_xattn_in['W_Query'], 'L1_xattn_W_Key': _L1_xattn_in['W_Key'], 'L1_xattn_W_Value': _L1_xattn_in['W_Value'], 'L1_xattn_W_Output': _L1_xattn_in['W_Output'], 'L1_xattn_B_Query': _L1_xattn_in['B_Query'], 'L1_xattn_B_Key': _L1_xattn_in['B_Key'], 'L1_xattn_B_Value': _L1_xattn_in['B_Value'], 'L1_xattn_B_Output': _L1_xattn_in['B_Output'], 'L1_ffn_gate_w': _L1_ffn_in['gate_w'], 'L1_ffn_w1': _L1_ffn_in['w1'], 'L1_ffn_w2': _L1_ffn_in['w2']}

def reference(x, ctx_1024, L0_xattn_ig_kernel, L0_xattn_ig_bias, L0_xattn_fg_kernel, L0_xattn_fg_bias, L0_xattn_outnorm_weight, L0_ffn_w1, L0_ffn_b1, L0_ffn_w2, L0_ffn_b2, L1_xattn_W_Query, L1_xattn_W_Key, L1_xattn_W_Value, L1_xattn_W_Output, L1_xattn_B_Query, L1_xattn_B_Key, L1_xattn_B_Value, L1_xattn_B_Output, L1_ffn_gate_w, L1_ffn_w1, L1_ffn_w2):
    import jax
    import jax.numpy as jnp

    def _L0_xattn_ref(q, k, v, ig_kernel, ig_bias, fg_kernel, fg_bias, outnorm_weight):
        import jax, jax.numpy as jnp
        import numpy as np
        EPS_BACKEND = 1e-06
        NORM_EPS = 1e-06
        NUM_HEADS = 4

        def _mlstm_forward(q, k, v, ig_kernel, ig_bias, fg_kernel, fg_bias, outnorm_weight):
            B, S, E = q.shape
            NH = ig_bias.shape[0]
            DH = E // NH
            gate_input = jnp.concatenate([q, k, v], axis=-1)
            igate = gate_input @ ig_kernel + ig_bias
            fgate = gate_input @ fg_kernel + fg_bias
            qh = q.reshape(B, S, NH, DH).transpose(0, 2, 1, 3)
            kh = k.reshape(B, S, NH, DH).transpose(0, 2, 1, 3)
            vh = v.reshape(B, S, NH, DH).transpose(0, 2, 1, 3)
            ig = igate.transpose(0, 2, 1)
            fg = fgate.transpose(0, 2, 1)
            log_fg = jax.nn.log_sigmoid(fg)
            cums = jnp.concatenate([jnp.zeros((B, NH, 1), log_fg.dtype), jnp.cumsum(log_fg, axis=-1)], axis=-1)
            fg_mat = cums[..., :, None] - cums[..., None, :]
            mask = jnp.tril(jnp.ones((S + 1, S + 1), bool))
            fg_mat = jnp.where(mask, fg_mat, -jnp.inf)[..., 1:, 1:]
            log_D = fg_mat + ig[..., None, :]
            max_log_D = jnp.max(log_D, axis=-1, keepdims=True)
            D = jnp.exp(log_D - max_log_D)
            qk = jnp.einsum('bnsd,bntd->bnst', qh, kh) / jnp.sqrt(jnp.float32(DH))
            C = qk * D
            normalizer = jnp.maximum(jnp.abs(C.sum(-1, keepdims=True)), jnp.exp(-max_log_D))
            h = jnp.einsum('bnst,bntd->bnsd', C / (normalizer + EPS_BACKEND), vh)
            h = h.transpose(0, 2, 1, 3)
            mean = h.mean(-1, keepdims=True)
            var = h.var(-1, keepdims=True)
            hn = (h - mean) * jax.lax.rsqrt(var + NORM_EPS) * outnorm_weight
            return hn.reshape(B, S, E)
        return _mlstm_forward(q, k, v, ig_kernel, ig_bias, fg_kernel, fg_bias, outnorm_weight)

    def _L0_ffn_ref(x, w1, b1, w2, b2):
        import jax, jax.numpy as jnp
        import numpy as np
        N_EMBD = 256
        N_STATE = 1024
        h = jax.nn.gelu(jnp.einsum('bse,eh->bsh', x, w1) + b1, approximate=False)
        return jnp.einsum('bsh,he->bse', h, w2) + b2

    def _L1_xattn_ref(query, key, value, W_Query, W_Key, W_Value, W_Output, B_Query, B_Key, B_Value, B_Output):
        import jax, jax.numpy as jnp
        import numpy as np
        HEAD_NUM = 16
        KEY_DIM = 64
        EMBED = 256
        KV_OUT = HEAD_NUM * KEY_DIM
        B, Lq, E = query.shape
        Lk = key.shape[1]
        H, D = (HEAD_NUM, KEY_DIM)
        q = query @ W_Query + B_Query
        k = key @ W_Key + B_Key
        v = value @ W_Value + B_Value
        q = q.reshape(B, Lq, H, D)
        k = k.reshape(B, Lk, H, D)
        v = v.reshape(B, Lk, H, D)
        scores = jnp.einsum('bqhd,bkhd->bhqk', q, k) / D ** 0.5
        probs = jax.nn.softmax(scores, axis=-1)
        out = jnp.einsum('bhqk,bkhd->bqhd', probs, v)
        out = out.reshape(B, Lq, H * D)
        return out @ W_Output + B_Output

    def _L1_ffn_ref(x, gate_w, w1, w2):
        import math
        import jax, jax.numpy as jnp
        import numpy as np
        D_MODEL = 256
        NUM_EXPERTS = 8
        D_FF_EXPERT = max(64, int(D_MODEL * 4 * 0.25))
        THRESHOLD = 0.9
        CAP_FACTOR = 1.0
        INIT_STD = 0.02

        def _xmoe_route(probs):
            N, E = probs.shape
            order = jnp.argsort(-probs, axis=-1)
            p_sorted = jnp.take_along_axis(probs, order, axis=-1)
            csum = jnp.cumsum(p_sorted, axis=-1)
            reached = (csum >= THRESHOLD).at[:, -1].set(True)
            k_idx = jnp.argmax(reached, axis=-1)
            select_prefix = jnp.arange(E)[None, :] <= k_idx[:, None]
            rows = jnp.arange(N)[:, None]
            assign_mask = jnp.zeros((N, E), dtype=bool).at[rows, order].set(select_prefix)
            rank = jnp.arange(1, E + 1, dtype=probs.dtype)[None, :]
            R_sorted = jnp.where(select_prefix, p_sorted - rank, jnp.full_like(p_sorted, -1000000000.0))
            R = jnp.zeros((N, E), dtype=probs.dtype).at[rows, order].set(R_sorted)
            capacity = int(math.ceil(N / E) * CAP_FACTOR)
            C = min(capacity, N)
            tok_order = jnp.argsort(-R, axis=0)
            topC = tok_order[:C, :]
            keep = jnp.zeros((N, E), dtype=bool).at[topC, jnp.arange(E)[None, :]].set(True)
            final_mask = assign_mask & keep
            return jnp.where(final_mask, probs, jnp.zeros_like(probs))
        B, T, D = x.shape
        N = B * T
        xf = x.reshape(N, D)
        probs = jax.nn.softmax(xf @ gate_w.T, axis=-1)
        scores_sel = _xmoe_route(probs)
        h = jax.nn.gelu(jnp.einsum('nd,efd->enf', xf, w1), approximate=False)
        y_e = jnp.einsum('enf,edf->end', h, w2)
        y = jnp.einsum('ne,end->nd', scores_sel, y_e)
        return y.reshape(B, T, D)
    x = x + _L0_xattn_ref(_layernorm(x, axis=-1), ctx_1024, ctx_1024, L0_xattn_ig_kernel, L0_xattn_ig_bias, L0_xattn_fg_kernel, L0_xattn_fg_bias, L0_xattn_outnorm_weight)
    x = x + _L0_ffn_ref(_layernorm(x, axis=-1), L0_ffn_w1, L0_ffn_b1, L0_ffn_w2, L0_ffn_b2)
    x = x + _L1_xattn_ref(_layernorm(x, axis=-1), ctx_1024, ctx_1024, L1_xattn_W_Query, L1_xattn_W_Key, L1_xattn_W_Value, L1_xattn_W_Output, L1_xattn_B_Query, L1_xattn_B_Key, L1_xattn_B_Value, L1_xattn_B_Output)
    x = x + _L1_ffn_ref(_layernorm(x, axis=-1), L1_ffn_gate_w, L1_ffn_w1, L1_ffn_w2)
    return x

_drawn_inputs = setup_inputs


def setup_inputs(seed=0):
    import zlib

    import numpy as np

    out = dict(_drawn_inputs(seed))
    spreads = {'L0_xattn_outnorm_weight': (1.0, 0.2),
     'L1_xattn_B_Query': (0.0, 0.8),
     'L1_xattn_B_Key': (0.0, 0.8),
     'L1_xattn_B_Value': (0.0, 0.1),
     'L1_xattn_B_Output': (0.0, 0.1)}
    factors = {'L0_xattn_ig_bias': 8.0,
     'L0_ffn_b1': 7.675,
     'L0_ffn_b2': 5.275,
     'L1_xattn_W_Query': 8.0,
     'L1_xattn_W_Key': 8.0,
     'L1_ffn_gate_w': 7.268,
     'L1_ffn_w1': 7.054,
     'L1_ffn_w2': 6.832}
    for name, (base, spread) in spreads.items():
        noise = np.random.default_rng([zlib.crc32(name.encode()), seed]).standard_normal(out[name].shape)
        drawn = base * np.exp(spread * noise) if base else spread * noise
        out[name] = jnp.asarray(drawn.astype(out[name].dtype))
    for name, factor in factors.items():
        out[name] = (out[name] * factor).astype(out[name].dtype)
    return out
```

```python
from contextlib import ExitStack

import concourse.bass as bass
from concourse import mybir

F32 = mybir.dt.float32
BF16 = mybir.dt.bfloat16
I32 = mybir.dt.int32
U32 = mybir.dt.uint32
ALU = mybir.AluOpType
ACT = mybir.ActivationFunctionType
AX = mybir.AxisListType
ds = bass.ds

P = 128
B, S, D = 8, 512, 256
N = B * S
TPB = S // P
NT = N // P
DC = D // P
MH, MD = 4, 64
F = 1024
FC = F // P
AH, AD = 16, 64
HP = AH // 2
E, EF = 8, 256
CAP = N // E
CT = CAP // P
ROW = D + E
SPARE = P
LN_EPS = 1e-5
MIX_EPS = 1e-6
FAR = 1e9


def sems(ctx, nc, phase, names):
    return {n: ctx.enter_context(nc.semaphore(f"{phase}_{n}")) for n in names.split()}


def wait_apart(eng, sem, value):
    eng.wait_ge(sem, value)
    eng.nop(nofuse=True)


def norm_batch_dve(dve, s, i, x_all, tmp, wait_free):
    for t in range(TPB):
        ins = dve.bn_stats(tmp["stats"][:, t, :], x_all[:, ds(i * TPB + t, 1), :].rearrange("p a d -> p (a d)"))
    ins.then_inc(s["stats"], 1)
    wait_apart(dve, s["stats"], i + 1)
    for t in range(TPB):
        ins = dve.bn_aggr(tmp["mv"][:, t, :], tmp["stats"][:, t, :])
    ins.then_inc(s["mv"], 1)
    dve.wait_ge(s["mv"], i + 1)
    dve.tensor_scalar(tmp["ve"][:, :], tmp["mv"][:, :, 1], LN_EPS, None, ALU.add).then_inc(s["ve"], 1)
    wait_free()
    dve.wait_ge(s["rstd"], i + 1)
    for t in range(TPB):
        ins = dve.tensor_scalar(tmp["xn"][:, t, :], x_all[:, ds(i * TPB + t, 1), :].rearrange("p a d -> p (a d)"),
                                tmp["mv"][:, t, 0:1], tmp["rstd"][:, t:t + 1], ALU.subtract, ALU.mult)
    ins.then_inc(s["xn"], 1)


def norm_batch_pool(pool, s, i, tmp, minus_half):
    wait_apart(pool, s["ve"], i + 1)
    pool.tensor_tensor(tmp["rstd"][:, :], tmp["ve"][:, :], minus_half[:, 0:TPB], ALU.pow).then_inc(s["rstd"], 1)


def norm_tmp(sb):
    return {"stats": sb("stats", [P, TPB, 6], F32), "mv": sb("mv", [P, TPB, 2], F32),
            "ve": sb("ve", [P, TPB], F32), "rstd": sb("rstd", [P, TPB], F32), "xn": sb("xn", [P, TPB, D], F32)}


def allocator(ctx, nc, phase):
    def sb(name, shape, dt):
        return ctx.enter_context(nc.sbuf_tensor(f"{phase}_{name}", shape, dt))
    return sb


def setup(nc, c, x, x_all):
    with ExitStack() as ctx:
        s = sems(ctx, nc, "st", "x zero fill")
        with nc.Block() as block:
            @block.sync
            def _(sp):
                xv = x.rearrange("b (t p) d -> p (b t) d", p=P)
                for i in range(B):
                    sp.dma_start(x_all[:, i * TPB:(i + 1) * TPB, :], xv[:, i * TPB:(i + 1) * TPB, :]).then_inc(s["x"], 16)
                sp.wait_ge(s["x"], 16 * B)

            @block.gpsimd
            def _(pool):
                pool.memset(c["ident"][:, :], 0.0)
                pool.memset(c["sel"][:, :, :], 0.0)
                pool.memset(c["lower"][:, :], 1.0)
                pool.memset(c["ones_row"][:, :], 1.0)
                pool.memset(c["ones_bf"][:, :], 1.0)
                pool.memset(c["minus_half"][:, :], -0.5)
                pool.memset(c["earlier"][:, :, :], 1.0).then_inc(s["zero"], 1)
                pool.wait_ge(s["zero"], 1)
                pool.affine_select(out=c["ident"][:, :], in_=c["ident"][:, :], compare_op=ALU.not_equal, fill=1.0,
                                   base=0, pattern=[[-1, P]], channel_multiplier=1)
                pool.affine_select(out=c["sel"][:, :, :], in_=c["sel"][:, :, :], compare_op=ALU.not_equal, fill=1.0,
                                   base=0, pattern=[[-1, MH], [0, P]], channel_multiplier=1)
                pool.affine_select(out=c["lower"][:, :], in_=c["lower"][:, :], compare_op=ALU.is_gt, fill=0.0,
                                   base=0, pattern=[[1, P]], channel_multiplier=-1)
                pool.affine_select(out=c["earlier"][:, :, :], in_=c["earlier"][:, :, :], compare_op=ALU.is_gt,
                                   fill=0.0, base=0, pattern=[[1, E], [-1, E]], channel_multiplier=0)
                pool.iota(c["slot"][:, :], pattern=[[1, P]], base=0, channel_multiplier=0,
                          allow_small_or_imprecise_dtypes=True)
                pool.iota(c["part"][:, :], pattern=[[0, 1]], base=0, channel_multiplier=1,
                          allow_small_or_imprecise_dtypes=True)
                pool.iota(c["tile_no"][:, :], pattern=[[1, NT]], base=0, channel_multiplier=0,
                          allow_small_or_imprecise_dtypes=True).then_inc(s["fill"], 1)
                pool.wait_ge(s["fill"], 1)


def mlstm(nc, c, x_all, ctxT_all, ctx_in, ig_kernel, ig_bias, fg_kernel, fg_bias, outnorm):
    OFF = [0, 512, 896, 1152]
    LEN = [S - P * t for t in range(TPB)]
    PACK = sum(LEN)
    GW = 36
    with ExitStack() as ctx:
        sb = allocator(ctx, nc, "ml")
        tmp = norm_tmp(sb)
        ctx_s = sb("ctx", [P, TPB, D], F32)
        qT = sb("qT", [P, DC, S], F32)
        kT = sb("kT", [P, DC, S], F32)
        vaug = sb("vaug", [P, TPB, MH, MD + 1], F32)
        gk_in = sb("gk_in", [P, 3 * DC, 2 * MH], F32)
        gate_w = sb("gate_w", [P, 2 * DC, GW], F32)
        gbias = sb("gbias", [GW, 1], F32)
        w_row = sb("w_row", [P, D], F32)
        ig = sb("ig", [MH, S], F32)
        fg = sb("fg", [MH, S], F32)
        absf = sb("absf", [MH, S], F32)
        efg = sb("efg", [MH, S], F32)
        lfg = sb("lfg", [MH, S], F32)
        cums = sb("cums", [MH, S], F32)
        g = sb("g", [MH, S], F32)
        gmax = sb("gmax", [MH, S], F32)
        logmax = sb("logmax", [MH, S], F32)
        floor = sb("floor", [MH, S], F32)
        cols = sb("cols", [P, 2, TPB, MH], F32)
        Dm = sb("Dm", [P, 2, PACK], F32)
        C = sb("C", [P, PACK], F32)
        hT = sb("hT", [MD + 1, S], F32)
        hs = sb("hs", [P, MH, TPB, MD + 1], F32)
        nrm = sb("nrm", [P, 8, MH * TPB], F32)
        hw = sb("hw", [P, MH * TPB, MD], F32)
        sq = sb("sq", [P, MH * TPB, MD], F32)
        ps = ctx.enter_context(nc.psum_tensor("ml_ps", [P, 8, 512], F32))
        C_BANK, M_BANK, H_BANK, ROW_BANK, TURN_BANK = 0, 3, 4, 5, 6
        s = sems(ctx, nc, "ml", "w wset gw ctx vaug stats mv ve rstd xn xn_turned ctx_turned qT kT ctxT gates rows "
                 "act_rows cols_ps cols m_ps d_in d_exp d_masked c_ps c pv hT h_turned hs fin fin_pow")
        ident = c["ident"]
        cv = ctx_in.rearrange("b (t p) d -> b p t d", p=P)
        TR = (MH + 1 - 1)

        FREE_AT_START = "pv cols d_in c hT hs c_ps ctxT cols_ps h_turned xn_turned".split()
        with nc.Block() as block:
            @block.sync
            def _(sp):
                sp.dma_start(ctx_s[:, :, :], cv[0]).then_inc(s["ctx"], 16)
                sp.dma_start(gk_in[:, :, 0:MH], ig_kernel.rearrange("(c p) h -> p c h", p=P)).then_inc(s["w"], 16)
                sp.dma_start(gk_in[:, :, MH:2 * MH], fg_kernel.rearrange("(c p) h -> p c h", p=P)).then_inc(s["w"], 16)
                sp.wait_ge(s["wset"], 1)
                sp.dma_start(gbias[0:MH, :], ig_bias.rearrange("(h a) -> h a", a=1)).then_inc(s["w"], 16)
                sp.dma_start(gbias[32:32 + MH, :], fg_bias.rearrange("(h a) -> h a", a=1)).then_inc(s["w"], 16)
                row = outnorm.rearrange("h d -> (h d)").rearrange("(a n) -> a n", a=1)
                sp.dma_start(w_row[:, :], row.broadcast_to([P, D])).then_inc(s["w"], 16)
                with sp.Fori(1, B) as i:
                    sp.wait_ge(s["ctx_turned"], i)
                    sp.wait_ge(s["vaug"], i)
                    sp.dma_start(ctx_s[:, :, :], cv[ds(i, 1)].rearrange("a p t d -> p (a t) d")).then_inc(s["ctx"], 16)

            @block.gpsimd
            def _(pool):
                pool.memset(gbias[:, :], 0.0).then_inc(s["wset"], 1)
                pool.memset(vaug[:, :, :, MD:MD + 1], 1.0)
                with pool.Fori(0, B) as i:
                    norm_batch_pool(pool, s, i, tmp, c["minus_half"])
                    wait_apart(pool, s["ctx"], 16 * i + 16)
                    wait_apart(pool, s["pv"], MH * i + 1)
                    pool.tensor_copy(vaug[:, :, :, 0:MD],
                                     ctx_s[:, :, :].rearrange("p t (h d) -> p t h d", h=MH)).then_inc(s["vaug"], 1)
                    wait_apart(pool, s["kT"], i + 1)
                    pool.tensor_copy(ctxT_all[:, :, ds(i * S, S)], kT[:, :, :]).then_inc(s["ctxT"], 1)
                    for h in range(MH):
                        wait_apart(pool, s["d_exp"], MH * i + h + 1)
                        for t in range(TPB):
                            diag = Dm[:, h % 2, OFF[t]:OFF[t] + P]
                            pool.affine_select(out=diag, in_=diag, compare_op=ALU.is_ge, fill=0.0, base=0,
                                               pattern=[[1, P]], channel_multiplier=-1).then_inc(s["d_masked"], 1)
                    wait_apart(pool, s["fin"], 14 * i + 11)
                    pool.tensor_tensor(nrm[:, 7, :], nrm[:, 6, :], c["minus_half"][:, 0:MH * TPB],
                                       ALU.pow).then_inc(s["fin_pow"], 1)

            @block.tensor
            def _(pe):
                def gate_maps(i):
                    pe.wait_ge(s["cols"], i + 1)
                    pe.wait_ge(s["qT"], i + 1)
                    pe.wait_ge(s["kT"], i + 1)
                    for k in range(2 * DC):
                        rhs = qT[:, k, :] if k < DC else kT[:, k - DC, :]
                        ins = pe.matmul(ps[0:GW, ROW_BANK, :], gate_w[:, k, :], rhs, start=k == 0, stop=k == 2 * DC - 1)
                    ins.then_inc(s["gates"], 1)

                def spread_max(i, h):
                    pe.wait_ge(s["rows"], 8 * i + 7)
                    pe.wait_ge(s["d_in"], MH * i + h + 1)
                    pe.matmul(ps[:, M_BANK, :], c["sel"][:, h, :], gmax[:, :], start=True, stop=True).then_inc(s["m_ps"], 1)

                def scores(i, h):
                    pe.wait_ge(s["c"], MH * i + h + 1)
                    lo = MD * (h % 2)
                    for t in range(TPB):
                        bank, at = (t, 0) if t < 3 else (2, LEN[2])
                        ins = pe.matmul(ps[:, C_BANK + bank, at:at + LEN[t]], kT[lo:lo + MD, h // 2, P * t:P * t + P],
                                        qT[lo:lo + MD, h // 2, P * t:S], start=True, stop=True)
                    ins.then_inc(s["c_ps"], 1)

                def values(i, h):
                    pe.wait_ge(s["c"], MH * i + h + 2)
                    pe.wait_ge(s["hT"], MH * i + h + 1)
                    for t in range(TPB):
                        ins = pe.matmul(ps[0:MD + 1, H_BANK, P * t:S], vaug[:, t, h, :], C[:, OFF[t]:OFF[t] + LEN[t]],
                                        start=t == 0, stop=t == TPB - 1, skip_group_check=True)
                    ins.then_inc(s["pv"], 1)

                def turn_head(i, h):
                    pe.wait_ge(s["hT"], MH * i + h + 2)
                    wait_apart(pe, s["hs"], MH * i + h + 1)
                    for t in range(TPB):
                        ins = pe.transpose(ps[:, TURN_BANK + 1, (MD + 1) * t:(MD + 1) * (t + 1)],
                                           hT[:, P * t:P * t + P], ident[0:MD + 1, 0:MD + 1])
                    ins.then_inc(s["h_turned"], 1)

                pe.wait_ge(s["gw"], 6)
                with pe.Fori(0, B) as i:
                    pe.wait_ge(s["xn"], i + 1)
                    pe.wait_ge(s["hs"], MH * i + 1)
                    for k in range(DC):
                        for t in range(TPB):
                            ins = pe.transpose(ps[:, TURN_BANK + k, P * t:P * t + P], tmp["xn"][:, t, P * k:P * k + P],
                                               ident[:, :])
                    ins.then_inc(s["xn_turned"], 1)
                    pe.wait_ge(s["ctx"], 16 * i + 16)
                    pe.wait_ge(s["hT"], MH * i + 1)
                    pe.wait_ge(s["cols"], i + 1)
                    for k in range(DC):
                        for t in range(TPB):
                            ins = pe.transpose(ps[:, H_BANK + k, P * t:P * t + P], ctx_s[:, t, P * k:P * k + P],
                                               ident[:, :])
                    ins.then_inc(s["ctx_turned"], 1)
                    gate_maps(i)
                    scores(i, 0)
                    wait_apart(pe, s["rows"], 8 * i + 6)
                    for t in range(TPB):
                        pe.transpose(ps[:, ROW_BANK, MH * t:MH * t + MH], g[:, P * t:P * t + P], ident[0:MH, 0:MH])
                    wait_apart(pe, s["act_rows"], 3 * i + 3)
                    for t in range(TPB):
                        ins = pe.transpose(ps[:, ROW_BANK, MH * (TPB + t):MH * (TPB + t + 1)],
                                           floor[:, P * t:P * t + P], ident[0:MH, 0:MH])
                    ins.then_inc(s["cols_ps"], 1)
                    spread_max(i, 0)
                    for h in range(MH):
                        if h:
                            scores(i, h)
                        if h + 1 < MH:
                            spread_max(i, h + 1)
                        if h:
                            turn_head(i, h - 1)
                        pe.wait_ge(s["vaug"], i + 1)
                        values(i, h)
                    turn_head(i, MH - 1)

            @block.scalar
            def _(act):
                with act.Fori(0, B) as i:
                    act.wait_ge(s["c_ps"], MH * i + 1)
                    act.wait_ge(s["xn_turned"], i + 2)
                    for k in range(DC):
                        ins = act.copy(qT[:, k, :], ps[:, TURN_BANK + k, :])
                    ins.then_inc(s["qT"], 1)
                    act.wait_ge(s["ctxT"], i + 1)
                    act.wait_ge(s["ctx_turned"], i + 1)
                    for k in range(DC):
                        ins = act.copy(kT[:, k, :], ps[:, H_BANK + k, :])
                    ins.then_inc(s["kT"], 1)
                    act.wait_ge(s["rows"], 8 * i + 3)
                    act.activation(efg[:, :], absf[:, :], ACT.Exp, scale=-1.0).then_inc(s["act_rows"], 1)
                    act.wait_ge(s["act_rows"], 3 * i + 1)
                    act.activation(lfg[:, :], efg[:, :], ACT.Ln, bias=1.0).then_inc(s["act_rows"], 1)
                    act.wait_ge(s["rows"], 8 * i + 8)
                    act.wait_ge(s["cols_ps"], i + 1)
                    act.activation(floor[:, :], logmax[:, :], ACT.Exp, scale=-1.0).then_inc(s["act_rows"], 1)
                    for h in range(MH + 1):
                        if h < MH:
                            act.wait_ge(s["d_in"], MH * i + h + 2)
                            act.activation(Dm[:, h % 2, :], Dm[:, h % 2, :], ACT.Exp, scale=-1.0).then_inc(s["d_exp"], 1)
                        if h:
                            act.wait_ge(s["pv"], MH * i + h + 1)
                            act.wait_ge(s["h_turned"], MH * i + h)
                            act.copy(hT[:, :], ps[0:MD + 1, H_BANK, :]).then_inc(s["hT"], 1)

            @block.vector
            def _(dve):
                for name in FREE_AT_START:
                    dve.sem_inc(s[name], 1)
                dve.memset(gate_w[:, :, :], 0.0).then_inc(s["gw"], 1)
                dve.wait_ge(s["gw"], 1)
                dve.wait_ge(s["w"], 16 * 5)
                for half in range(2):
                    src = gk_in[:, :, MH * half:MH * half + MH]
                    dst = gate_w[:, :, 32 * half:32 * half + MH]
                    dve.tensor_copy(dst[:, 0:DC, :], src[:, 0:DC, :]).then_inc(s["gw"], 1)
                    dve.tensor_tensor(dst[:, DC:2 * DC, :], src[:, DC:2 * DC, :], src[:, 2 * DC:3 * DC, :],
                                      ALU.add).then_inc(s["gw"], 1)
                dve.memset(nrm[:, :, :], 1.0).then_inc(s["gw"], 1)
                ones_row = c["ones_row"][0:MH, :]

                def decay_in(i, h):
                    dve.wait_ge(s["m_ps"], MH * i + h + 1)
                    for t in range(TPB):
                        ins = dve.tensor_scalar(Dm[:, h % 2, OFF[t]:OFF[t] + LEN[t]], ps[:, M_BANK, P * t:S],
                                                cols[:, 0, t, h:h + 1], 0.0, ALU.subtract, ALU.max)
                    ins.then_inc(s["d_in"], 1)

                def weigh(i, h):
                    dve.wait_ge(s["c_ps"], MH * i + h + 2)
                    dve.wait_ge(s["d_masked"], TPB * (MH * i + h + 1))
                    dve.wait_ge(s["pv"], MH * i + h + 1)
                    for bank in range(3):
                        lo, n = OFF[bank], (LEN[bank] if bank < 2 else LEN[2] + LEN[3])
                        ins = dve.scalar_tensor_tensor(out=C[:, lo:lo + n], in0=ps[:, C_BANK + bank, 0:n],
                                                       scalar=MD ** -0.5, in1=Dm[:, h % 2, lo:lo + n],
                                                       op0=ALU.mult, op1=ALU.mult)
                    ins.then_inc(s["c"], 1)

                def keep_head(i, h):
                    dve.wait_ge(s["h_turned"], MH * i + h + 2)
                    dve.tensor_copy(hs[:, h, :, :], ps[:, TURN_BANK + 1, 0:TPB * (MD + 1)].rearrange(
                        "p (t d) -> p t d", t=TPB)).then_inc(s["hs"], 1)

                with dve.Fori(0, B) as i:
                    norm_batch_dve(dve, s, i, x_all, tmp, lambda: dve.wait_ge(s["xn_turned"], i + 1))

                    def row(ins, k):
                        ins.then_inc(s["rows"], 1)
                        dve.wait_ge(s["rows"], 8 * i + k)

                    dve.wait_ge(s["gates"], i + 1)
                    row(dve.tensor_scalar(ig[:, :], ps[0:MH, ROW_BANK, :], gbias[0:MH, :], None, ALU.add), 1)
                    row(dve.tensor_scalar(fg[:, :], ps[32:32 + MH, ROW_BANK, :], gbias[32:32 + MH, :], None, ALU.add), 2)
                    row(dve.scalar_tensor_tensor(out=absf[:, :], in0=fg[:, :], scalar=-1.0, in1=fg[:, :],
                                                 op0=ALU.mult, op1=ALU.max), 3)
                    dve.wait_ge(s["act_rows"], 3 * i + 2)
                    row(dve.scalar_tensor_tensor(out=fg[:, :], in0=fg[:, :], scalar=0.0, in1=lfg[:, :],
                                                 op0=ALU.min, op1=ALU.subtract), 4)
                    row(dve.tensor_tensor_scan(cums[:, :], ones_row, fg[:, :], 0.0, ALU.mult, ALU.add), 5)
                    row(dve.tensor_tensor(g[:, :], ig[:, :], cums[:, :], ALU.subtract), 6)
                    row(dve.tensor_tensor_scan(gmax[:, :], g[:, :], g[:, :], -3.0e38, ALU.max, ALU.max), 7)
                    row(dve.tensor_tensor(logmax[:, :], cums[:, :], gmax[:, :], ALU.add), 8)
                    dve.wait_ge(s["cols_ps"], i + 2)
                    dve.tensor_copy(cols[:, :, :, :], ps[:, ROW_BANK, 0:2 * TPB * MH].rearrange(
                        "p (a t h) -> p a t h", a=2, t=TPB)).then_inc(s["cols"], 1)
                    dve.wait_ge(s["cols"], i + 2)
                    decay_in(i, 0)
                    for h in range(MH):
                        if h + 1 < MH:
                            decay_in(i, h + 1)
                        weigh(i, h)
                        if h:
                            keep_head(i, h - 1)
                    keep_head(i, MH - 1)

                    def fin(ins, k):
                        ins.then_inc(s["fin"], 1)
                        dve.wait_ge(s["fin"], 14 * i + k)

                    def wide(k):
                        return nrm[:, k, :].rearrange("p (g a) -> p g a", a=1).broadcast_to([P, MH * TPB, MD])

                    dve.wait_ge(s["hs"], MH * i + MH + 1)
                    hv = hs[:, :, :, 0:MD].rearrange("p h t d -> p (h t) d")
                    total = hs[:, :, :, MD:MD + 1].rearrange("p h t a -> p (h t a)")
                    n0 = nrm[:, 0, :].rearrange("p (h t) -> p h t", h=MH)
                    fin(dve.scalar_tensor_tensor(out=nrm[:, 0, :], in0=total, scalar=-1.0, in1=total, op0=ALU.mult,
                                                 op1=ALU.max), 1)
                    fin(dve.tensor_tensor(n0, n0, cols[:, 1, :, :].rearrange("p t h -> p h t"), ALU.max), 2)
                    fin(dve.tensor_scalar(nrm[:, 1, :], nrm[:, 0, :], MIX_EPS, None, ALU.add), 3)
                    fin(dve.reciprocal(nrm[:, 2, :], nrm[:, 1, :]), 4)
                    fin(dve.tensor_tensor(hw[:, :, :], hv, wide(2), ALU.mult), 5)
                    fin(dve.tensor_reduce(nrm[:, 3, :], hw[:, :, :], AX.X, ALU.add), 6)
                    fin(dve.tensor_scalar(nrm[:, 4, :], nrm[:, 3, :], 1.0 / MD, None, ALU.mult), 7)
                    fin(dve.tensor_tensor(hw[:, :, :], hw[:, :, :], wide(4), ALU.subtract), 8)
                    fin(dve.tensor_tensor(sq[:, :, :], hw[:, :, :], hw[:, :, :], ALU.mult), 9)
                    fin(dve.tensor_reduce(nrm[:, 5, :], sq[:, :, :], AX.X, ALU.add), 10)
                    fin(dve.tensor_scalar(nrm[:, 6, :], nrm[:, 5, :], 1.0 / MD, MIX_EPS, ALU.mult, ALU.add), 11)
                    dve.wait_ge(s["fin_pow"], i + 1)
                    fin(dve.tensor_tensor(hw[:, :, :], hw[:, :, :], wide(7), ALU.mult), 12)
                    for h in range(MH):
                        ins = dve.tensor_tensor(
                            hw[:, h * TPB:(h + 1) * TPB, :], hw[:, h * TPB:(h + 1) * TPB, :],
                            w_row[:, MD * h:MD * h + MD].rearrange("p (a d) -> p a d", a=1).broadcast_to([P, TPB, MD]),
                            ALU.mult)
                    fin(ins, 13)
                    for h in range(MH):
                        xv = x_all[:, ds(i * TPB, TPB), MD * h:MD * h + MD]
                        ins = dve.tensor_tensor(xv, xv, hw[:, h * TPB:(h + 1) * TPB, :], ALU.add)
                    fin(ins, 14)


def norm_and_turn(nc, c, phase, x_all, xnT_all, rows=None):
    with ExitStack() as ctx:
        sb = allocator(ctx, nc, phase)
        tmp = norm_tmp(sb)
        ps = ctx.enter_context(nc.psum_tensor(f"{phase}_ps", [P, DC, 512], F32))
        s = sems(ctx, nc, phase, "stats mv ve rstd xn turned out stored")
        FREE_AT_START = "turned stored out".split()
        with nc.Block() as block:
            @block.gpsimd
            def _(pool):
                with pool.Fori(0, B) as i:
                    norm_batch_pool(pool, s, i, tmp, c["minus_half"])

            @block.vector
            def _(dve):
                for name in FREE_AT_START:
                    dve.sem_inc(s[name], 1)
                with dve.Fori(0, B) as i:
                    def wait_free():
                        dve.wait_ge(s["turned"], i + 1)
                        if rows is not None:
                            dve.wait_ge(s["stored"], 16 * i + 1)
                    norm_batch_dve(dve, s, i, x_all, tmp, wait_free)

            @block.tensor
            def _(pe):
                with pe.Fori(0, B) as i:
                    pe.wait_ge(s["xn"], i + 1)
                    pe.wait_ge(s["out"], i + 1)
                    for k in range(DC):
                        for t in range(TPB):
                            ins = pe.transpose(ps[:, k, P * t:P * t + P], tmp["xn"][:, t, P * k:P * k + P],
                                               c["ident"][:, :])
                    ins.then_inc(s["turned"], 1)

            @block.scalar
            def _(act):
                with act.Fori(0, B) as i:
                    act.wait_ge(s["turned"], i + 2)
                    for k in range(DC):
                        ins = act.copy(xnT_all[:, k, ds(i * S, S)], ps[:, k, :])
                    ins.then_inc(s["out"], 1)

            if rows is not None:
                @block.sync
                def _(sp):
                    rv = rows.rearrange("(b t p) d -> b p t d", p=P, t=TPB)
                    with sp.Fori(0, B) as i:
                        sp.wait_ge(s["xn"], i + 1)
                        sp.dma_start(rv[ds(i, 1), :, :, 0:D].rearrange("a p t d -> p (a t) d"),
                                     tmp["xn"][:, :, :]).then_inc(s["stored"], 16)
                    sp.wait_ge(s["stored"], 16 * B + 1)


def mlp(nc, c, x_all, xnT_all, w1, b1, w2, b2):
    with ExitStack() as ctx:
        sb = allocator(ctx, nc, "mlp")
        w1_s = sb("w1", [P, DC, F], F32)
        w2_s = sb("w2", [P, FC, D], F32)
        b1_s = sb("b1", [P, FC], F32)
        b2_s = sb("b2", [P, D], F32)
        hT = sb("hT", [P, FC, S], F32)
        ps = ctx.enter_context(nc.psum_tensor("mlp_ps", [P, 8, 512], F32))
        s = sems(ctx, nc, "mlp", "w h_ps hT y_ps y b")
        FREE_AT_START = "y y_ps".split()
        with nc.Block() as block:
            @block.sync
            def _(sp):
                sp.dma_start(w1_s[:, :, :], w1.rearrange("(c p) f -> p c f", p=P)).then_inc(s["w"], 16)
                sp.dma_start(w2_s[:, :, :], w2.rearrange("(c p) d -> p c d", p=P)).then_inc(s["w"], 16)
                sp.dma_start(b1_s[:, :], b1.rearrange("(c p) -> p c", p=P), allow_slow_non_contiguous=True).then_inc(s["w"], 16)
                sp.dma_start(b2_s[:, :], b2.rearrange("(a d) -> a d", a=1).broadcast_to([P, D])).then_inc(s["w"], 16)

            @block.tensor
            def _(pe):
                pe.wait_ge(s["w"], 64)
                with pe.Fori(0, B) as i:
                    for f in range(FC):
                        if f >= 4:
                            pe.wait_ge(s["hT"], FC * i + f - 3)
                        for k in range(DC):
                            ins = pe.matmul(ps[:, f % 4, :], w1_s[:, k, P * f:P * f + P], xnT_all[:, k, ds(i * S, S)],
                                            start=k == 0, stop=k == DC - 1)
                        ins.then_inc(s["h_ps"], 1)
                    pe.wait_ge(s["y"], TPB * i + 1)
                    pe.wait_ge(s["hT"], FC * i + FC)
                    for t in range(TPB):
                        for f in range(FC):
                            ins = pe.matmul(ps[:, 4 + t, 0:D], hT[:, f, P * t:P * t + P], w2_s[:, f, :],
                                            start=f == 0, stop=f == FC - 1)
                        ins.then_inc(s["y_ps"], 1)

            @block.scalar
            def _(act):
                act.wait_ge(s["w"], 64)
                with act.Fori(0, B) as i:
                    act.wait_ge(s["y_ps"], TPB * i + 1)
                    for f in range(FC):
                        act.wait_ge(s["h_ps"], FC * i + f + 1)
                        act.activation(hT[:, f, :], ps[:, f % 4, :], ACT.Gelu, bias=b1_s[:, f:f + 1]).then_inc(s["hT"], 1)

            @block.vector
            def _(dve):
                for name in FREE_AT_START:
                    dve.sem_inc(s[name], 1)
                dve.wait_ge(s["w"], 64)
                with dve.Fori(0, B) as i:
                    for t in range(TPB):
                        dve.wait_ge(s["y_ps"], TPB * i + t + 2)
                        xv = x_all[:, ds(i * TPB + t, 1), :].rearrange("p a d -> p (a d)")
                        dve.tensor_tensor(xv, ps[:, 4 + t, 0:D], xv, ALU.add).then_inc(s["y"], 1)
                    dve.wait_ge(s["y"], TPB * i + TPB + 1)
                    for t in range(TPB):
                        xv = x_all[:, ds(i * TPB + t, 1), :].rearrange("p a d -> p (a d)")
                        ins = dve.tensor_tensor(xv, xv, b2_s[:, :], ALU.add)
                    ins.then_inc(s["b"], 1)


def attention(nc, c, x_all, xnT_all, ctxT_all, Wq, Wk, Wv, Wo, Bq, Bk, Bv, Bo):
    U = HP * B
    NBL = 2 * TPB
    with ExitStack() as ctx:
        sb = allocator(ctx, nc, "at")
        w_s = sb("w", [P, 3, DC, P], F32)
        b_s = sb("b", [P, 3], F32)
        wo_s = sb("wo", [P, D], F32)
        bo_s = sb("bo", [P, D], F32)
        qT = sb("qT", [P, 2, S], F32)
        kT = sb("kT", [P, 2, S], F32)
        vT = sb("vT", [P, S], F32)
        V = sb("V", [P, 2, TPB, P], F32)
        Pr = sb("Pr", [P, 4, S], F32)
        PT = sb("PT", [P, 2, TPB, S], F32)
        oT = sb("oT", [P, S], F32)
        nmax = sb("nmax", [P, 4], F32)
        rsum = sb("rsum", [P, 4], F32)
        rinv = sb("rinv", [P, 4], F32)
        ps = ctx.enter_context(nc.psum_tensor("at_ps", [P, 8, 512], F32))
        S_BANK, T_BANK, A_BANK, O_BANK, Y_BANK = 0, 3, 5, 6, 7
        s = sems(ctx, nc, "at", "w wo bo q_ps qT k_ps kT v_ps vT vturned V s_ps nmax exp rinv pn t_ps pt pv oT y_ps x bo_add")
        w_dram = [W.rearrange("(c p) n -> p c n", p=P) for W in (Wq, Wk, Wv)]
        b_dram = [b.rearrange("(a p) -> p a", p=P) for b in (Bq, Bk, Bv)]
        wo_dram = Wo.rearrange("(a p) d -> a p d", p=P)
        LOADS = 6

        def every_unit(eng, body):
            body(0, 0, first=True)
            with eng.Fori(0, (U - 2) // 2) as pair:
                body(pair * 2 + 1, 1)
                body(pair * 2 + 2, 0)
            body(U - 1, 1, last=True)

        with nc.Block() as block:
            @block.sync
            def _(sp):
                def load_qkv(hp):
                    for k in range(3):
                        sp.dma_start(w_s[:, k, :, :], w_dram[k][:, :, ds(hp * P, P)]).then_inc(s["w"], 16)
                        sp.dma_start(b_s[:, k:k + 1], b_dram[k][:, ds(hp, 1)], allow_slow_non_contiguous=True).then_inc(s["w"], 16)

                def load_o(hp):
                    sp.dma_start(wo_s[:, :], wo_dram[ds(hp, 1)].rearrange("a p d -> (a p) d")).then_inc(s["wo"], 16)

                load_qkv(0)
                load_o(0)
                sp.dma_start(bo_s[:, :], Bo.rearrange("(a d) -> a d", a=1).broadcast_to([P, D])).then_inc(s["bo"], 16)
                with sp.Fori(1, HP) as hp:
                    sp.wait_ge(s["vT"], hp * B)
                    sp.wait_ge(s["kT"], hp * B)
                    sp.wait_ge(s["qT"], hp * B)
                    load_qkv(hp)
                    sp.wait_ge(s["y_ps"], hp * B)
                    load_o(hp)

            @block.tensor
            def _(pe):
                def project(u, k):
                    src = xnT_all if k == 0 else ctxT_all
                    b = u % B
                    if k == 0:
                        pe.wait_ge(s["w"], 16 * LOADS * (u // B + 1))
                        pe.wait_ge(s["V"], u)
                    else:
                        pe.wait_ge(s["qT" if k == 1 else "kT"], u + 1)
                    for d in range(DC):
                        ins = pe.matmul(ps[:, A_BANK, :], w_s[:, k, d, :], src[:, d, ds(b * S, S)],
                                        start=d == 0, stop=d == DC - 1)
                    ins.then_inc(s[("q_ps", "k_ps", "v_ps")[k]], 1)

                def turn_values(u):
                    pe.wait_ge(s["vT"], u + 1)
                    for t in range(TPB):
                        ins = pe.transpose(ps[:, A_BANK, P * t:P * t + P], vT[:, P * t:P * t + P], c["ident"][:, :])
                    ins.then_inc(s["vturned"], 1)

                def score(u, par, j):
                    if j >= 3:
                        pe.wait_ge(s["exp"], NBL * u + j - 2)
                    if j == 0:
                        pe.wait_ge(s["qT"], u + 1)
                        pe.wait_ge(s["kT"], u + 1)
                    lo, q = AD * (j // TPB), P * (j % TPB)
                    pe.matmul(ps[:, S_BANK + j % 3, :], qT[lo:lo + AD, par, q:q + P], kT[lo:lo + AD, par, :],
                              start=True, stop=True).then_inc(s["s_ps"], 1)

                def turn(u, j):
                    pe.wait_ge(s["pn"], NBL * u + j + 1)
                    if j >= 2:
                        pe.wait_ge(s["pt"], NBL * u + j - 1)
                    for t in range(TPB):
                        ins = pe.transpose(ps[:, T_BANK + j % 2, P * t:P * t + P], Pr[:, j % 4, P * t:P * t + P],
                                           c["ident"][:, :])
                    ins.then_inc(s["t_ps"], 1)

                def body(u, par, first=False, last=False):
                    for j in range(NBL):
                        score(u, par, j)
                        if j >= 2:
                            turn(u, j - 2)
                    for k in range(2):
                        if not last:
                            project(u + 1, k)
                        turn(u, NBL - 2 + k)
                    if not last:
                        project(u + 1, 2)
                    pe.wait_ge(s["pt"], NBL * u + NBL)
                    pe.wait_ge(s["V"], u + 1)
                    pe.wait_ge(s["x"], u)
                    for t in range(TPB):
                        for h in range(2):
                            ins = pe.matmul(ps[AD * h:AD * h + AD, O_BANK, :], V[:, par, t, AD * h:AD * h + AD],
                                            PT[:, h, t, :], start=t == 0, stop=t == TPB - 1)
                    ins.then_inc(s["pv"], 1)
                    if not last:
                        turn_values(u + 1)
                    pe.wait_ge(s["oT"], u + 1)
                    pe.wait_ge(s["wo"], 16 * (u // B + 1))
                    for t in range(TPB):
                        ins = pe.matmul(ps[:, Y_BANK - t // 2, D * (t % 2):D * (t % 2) + D], oT[:, P * t:P * t + P],
                                        wo_s[:, :], start=True, stop=True)
                    ins.then_inc(s["y_ps"], 1)

                for k in range(3):
                    project(0, k)
                turn_values(0)
                every_unit(pe, body)

            @block.scalar
            def _(act):
                def evacuate(u, par, k):
                    act.wait_ge(s["k_ps" if k == 1 else "v_ps"], u + 1)
                    if k == 2:
                        act.wait_ge(s["vturned"], u)
                    dst = kT[:, par, :] if k == 1 else vT[:, :]
                    act.activation(dst, ps[:, A_BANK, :], ACT.Identity, bias=b_s[:, k:k + 1]
                                   ).then_inc(s["kT" if k == 1 else "vT"], 1)

                def body(u, par, first=False, last=False):
                    for j in range(NBL):
                        act.wait_ge(s["nmax"], NBL * u + j + 1)
                        if not first or j > 3:
                            act.wait_ge(s["t_ps"], NBL * u + j - 3)
                        act.activation(Pr[:, j % 4, :], ps[:, S_BANK + j % 3, :], ACT.Exp, bias=nmax[:, j % 4:j % 4 + 1],
                                       accum_out=rsum[:, j % 4:j % 4 + 1]).then_inc(s["exp"], 1)
                    if not last:
                        evacuate(u + 1, 1 - par, 1)
                        evacuate(u + 1, 1 - par, 2)
                    act.wait_ge(s["pv"], u + 1)
                    act.wait_ge(s["y_ps"], u)
                    act.copy(oT[:, :], ps[:, O_BANK, :]).then_inc(s["oT"], 1)

                act.wait_ge(s["w"], 16 * LOADS)
                evacuate(0, 0, 1)
                evacuate(0, 0, 2)
                every_unit(act, body)

            @block.gpsimd
            def _(pool):
                def body(u, par, first=False, last=False):
                    for j in range(NBL):
                        wait_apart(pool, s["rinv"], NBL * u + j + 1)
                        pool.tensor_scalar(Pr[:, j % 4, :], Pr[:, j % 4, :], rinv[:, j % 4:j % 4 + 1], 1.0,
                                           ALU.mult, ALU.mult).then_inc(s["pn"], 1)
                every_unit(pool, body)

            @block.vector
            def _(dve):
                def queries(u, par):
                    dve.wait_ge(s["q_ps"], u + 1)
                    dve.tensor_scalar(qT[:, par, :], ps[:, A_BANK, :], b_s[:, 0:1], AD ** -0.5, ALU.add, ALU.mult
                                      ).then_inc(s["qT"], 1)

                def values(u, par):
                    dve.wait_ge(s["vturned"], u + 1)
                    dve.tensor_copy(V[:, par, :, :], ps[:, A_BANK, :].rearrange("p (t d) -> p t d", t=TPB)
                                    ).then_inc(s["V"], 1)

                def row_max(u, j):
                    dve.wait_ge(s["s_ps"], NBL * u + j + 1)
                    dve.tensor_reduce(nmax[:, j % 4:j % 4 + 1], ps[:, S_BANK + j % 3, :], AX.X, ALU.max, negate=True
                                      ).then_inc(s["nmax"], 1)

                def row_sum(u, j):
                    dve.wait_ge(s["exp"], NBL * u + j + 1)
                    dve.reciprocal(rinv[:, j % 4:j % 4 + 1], rsum[:, j % 4:j % 4 + 1]).then_inc(s["rinv"], 1)

                def keep(u, j):
                    dve.wait_ge(s["t_ps"], NBL * u + j + 1)
                    q = P * (j % TPB)
                    dve.tensor_copy(PT[:, j // TPB, :, q:q + P],
                                    ps[:, T_BANK + j % 2, :].rearrange("p (t q) -> p t q", t=TPB)).then_inc(s["pt"], 1)

                def add_out(u):
                    dve.wait_ge(s["y_ps"], u + 1)
                    for half in range(2):
                        xv = x_all[:, ds((u % B) * TPB + 2 * half, 2), :].rearrange("p t d -> p (t d)")
                        ins = dve.tensor_tensor(xv, ps[:, Y_BANK - half, :], xv, ALU.add)
                    ins.then_inc(s["x"], 1)

                def body(u, par, first=False, last=False):
                    for j in range(NBL):
                        row_max(u, j)
                        if j == 0 and not first:
                            add_out(u - 1)
                        if j >= 1:
                            row_sum(u, j - 1)
                        if j >= 3:
                            keep(u, j - 3)
                    row_sum(u, NBL - 1)
                    keep(u, NBL - 3)
                    if not last:
                        queries(u + 1, 1 - par)
                    keep(u, NBL - 2)
                    keep(u, NBL - 1)
                    if not last:
                        values(u + 1, 1 - par)

                dve.wait_ge(s["w"], 16 * LOADS)
                dve.wait_ge(s["bo"], 16)
                queries(0, 0)
                values(0, 0)
                every_unit(dve, body)
                add_out(U - 1)
                dve.wait_ge(s["x"], U)
                with dve.Fori(0, NT) as t:
                    xv = x_all[:, ds(t, 1), :].rearrange("p a d -> p (a d)")
                    dve.tensor_tensor(xv, xv, bo_s[:, :], ALU.add).then_inc(s["bo_add"], 1)


def router(nc, c, xnT_all, gate_w, rows, prob, final, idx_get, idx_put, valid):
    with ExitStack() as ctx:
        sb = allocator(ctx, nc, "ro")
        gw = sb("gw", [E, D], F32)
        gT = sb("gT", [P, DC, E], F32)
        lT = sb("lT", [E, S], F32)
        lg = sb("lg", [P, NT, E], F32)
        red = sb("red", [P, 3, NT], F32)
        pair_a = sb("pair_a", [P, NT, E, E], F32)
        pair_b = sb("pair_b", [P, NT, E, E], F32)
        before = sb("before", [P, NT, E], F32)
        rank = sb("rank", [P, NT, E], F32)
        sel = sb("sel", [P, NT, E], F32)
        key = sb("key", [P, NT, E], F32)
        t1 = sb("t1", [P, NT, E], F32)
        t2 = sb("t2", [P, NT, E], F32)
        cnt = sb("cnt", [P, E], F32)
        cnt_b = sb("cnt_b", [P, E], BF16)
        T = sb("T", [P, E], F32)
        cand = sb("cand", [P, E], F32)
        step = sb("step", [P, E], F32)
        mask_b = sb("mask_b", [P, NT, E], BF16)
        tot = sb("tot", [P, E, NT], F32)
        offs = sb("offs", [P, E, NT + 1], F32)
        pos = sb("pos", [P, NT, E], F32)
        need = sb("need", [P, E], F32)
        chunk = sb("chunk", [P, NT, E], F32)
        slot = sb("slot", [P, NT, E], F32)
        is_chunk = sb("is_chunk", [P, NT, CT], F32)
        onehot = sb("onehot", [P, 2, NT, P], BF16)
        rhs = sb("rhs", [P, 2, NT, 3, CT], BF16)
        got = sb("got", [P, 3, CT], F32)
        tok = sb("tok", [P, CT], F32)
        away = sb("away", [P, CT], F32)
        ps = ctx.enter_context(nc.psum_tensor("ro_ps", [P, 4, 512], F32))
        s = sems(ctx, nc, "ro", "gw gT_ps gT l_ps lT lt_ps lg v ones_mm pre_mm prob exp slot_ps built")
        NE = NT * E

        def flat(a):
            return a[:, :, :].rearrange("p t e -> p (t e)")

        def over_e(a):
            return a.rearrange("p (t a) -> p t a", a=1).broadcast_to([P, NT, E])

        def over_t(a):
            return a.rearrange("p (a e) -> p a e", a=1).broadcast_to([P, NT, E])

        STEPS = list(range(2, -25, -1))
        FREE_AT_START = "lT lg".split()
        with nc.Block() as block:
            @block.sync
            def _(sp):
                sp.dma_start(gw[:, :], gate_w).then_inc(s["gw"], 16)
                sp.wait_ge(s["prob"], 1)
                with nc.allow_non_contiguous_dma("8 probabilities per row"):
                    sp.dma_start(rows.rearrange("(t p) d -> p t d", p=P)[:, :, D:ROW], prob[:, :, :]).then_inc(s["gw"], 16)
                sp.wait_ge(s["gw"], 32)

            @block.scalar
            def _(act):
                act.wait_ge(s["v"], 2)
                act.activation(flat(lg), flat(lg), ACT.Exp).then_inc(s["exp"], 1)

            @block.tensor
            def _(pe):
                pe.wait_ge(s["gw"], 16)
                for k in range(DC):
                    ins = pe.transpose(ps[:, 0, E * k:E * k + E], gw[:, P * k:P * k + P], c["ident"][0:E, 0:E])
                ins.then_inc(s["gT_ps"], 1)
                pe.wait_ge(s["gT"], 1)
                with pe.Fori(0, B) as i:
                    pe.wait_ge(s["lT"], i + 1)
                    for k in range(DC):
                        ins = pe.matmul(ps[0:E, 1, :], gT[:, k, :], xnT_all[:, k, ds(i * S, S)], start=k == 0,
                                        stop=k == DC - 1)
                    ins.then_inc(s["l_ps"], 1)
                    pe.wait_ge(s["lT"], i + 2)
                    wait_apart(pe, s["lg"], i + 1)
                    for t in range(TPB):
                        ins = pe.transpose(ps[:, 2, t * E:t * E + E], lT[:, P * t:P * t + P],
                                           c["ident"][0:E, 0:E])
                    ins.then_inc(s["lt_ps"], 1)
                for n in range(len(STEPS) + 1):
                    pe.wait_ge(s["built"], n + 1)
                    pe.matmul(ps[:, 0, 0:E], c["ones_bf"][:, :], cnt_b[:, :], start=True, stop=True).then_inc(s["ones_mm"], 1)
                for n in range(2):
                    pe.wait_ge(s["built"], len(STEPS) + 2 + n)
                    pe.matmul(ps[:, 1, 0:NE], c["lower_bf"][:, :], flat(mask_b), start=True, stop=True)
                    pe.matmul(ps[:, 3, 0:NE], c["ones_bf"][:, :], flat(mask_b), start=True, stop=True
                              ).then_inc(s["pre_mm"], 1)
                for e in range(E):
                    pe.wait_ge(s["built"], len(STEPS) + 4 + e)
                    for t in range(NT):
                        ins = pe.matmul(ps[:, e % 2, 0:3 * CT], onehot[:, e % 2, t, :],
                                        rhs[:, e % 2, t, :, :].rearrange("p a c -> p (a c)"), start=t == 0,
                                        stop=t == NT - 1)
                    ins.then_inc(s["slot_ps"], 1)

            @block.vector
            def _(dve):
                for name in FREE_AT_START:
                    dve.sem_inc(s[name], 1)
                n = [0]

                def v(ins):
                    n[0] += 1
                    ins.then_inc(s["v"], 1)
                    dve.wait_ge(s["v"], n[0])

                dve.wait_ge(s["gT_ps"], 1)
                dve.tensor_copy(gT[:, :, :], ps[:, 0, 0:DC * E].rearrange("p (k e) -> p k e", k=DC)).then_inc(s["gT"], 1)
                with dve.Fori(0, B) as i:
                    dve.wait_ge(s["l_ps"], i + 1)
                    dve.tensor_copy(lT[:, :], ps[0:E, 1, :]).then_inc(s["lT"], 1)
                    dve.wait_ge(s["lt_ps"], i + 1)
                    dve.tensor_copy(lg[:, ds(i * TPB, TPB), :],
                                    ps[:, 2, 0:TPB * E].rearrange("p (t e) -> p t e", e=E)).then_inc(s["lg"], 1)
                dve.wait_ge(s["lg"], B + 1)
                v(dve.tensor_reduce(red[:, 0, :], lg[:, :, :], AX.X, ALU.max))
                v(dve.tensor_tensor(lg[:, :, :], lg[:, :, :], over_e(red[:, 0, :]), ALU.subtract))
                dve.wait_ge(s["exp"], 1)
                v(dve.tensor_reduce(red[:, 1, :], lg[:, :, :], AX.X, ALU.add))
                v(dve.reciprocal(red[:, 2, :], red[:, 1, :]))
                dve.tensor_tensor(prob[:, :, :], lg[:, :, :], over_e(red[:, 2, :]), ALU.mult).then_inc(s["prob"], 1)
                dve.wait_ge(s["prob"], 1)
                pj = prob[:, :, :].rearrange("p t (a e) -> p t a e", a=1).broadcast_to([P, NT, E, E])
                pe_ = prob[:, :, :].rearrange("p t (e a) -> p t e a", a=1).broadcast_to([P, NT, E, E])
                tie = c["earlier"][:, :, :].rearrange("p (a e) j -> p a e j", a=1).broadcast_to([P, NT, E, E])
                v(dve.tensor_tensor(pair_a[:, :, :, :], pj, pe_, ALU.is_equal))
                v(dve.tensor_tensor(pair_a[:, :, :, :], pair_a[:, :, :, :], tie, ALU.mult))
                v(dve.tensor_tensor(pair_b[:, :, :, :], pj, pe_, ALU.is_gt))
                v(dve.tensor_tensor(pair_a[:, :, :, :], pair_a[:, :, :, :], pair_b[:, :, :, :], ALU.add))
                v(dve.tensor_reduce(rank[:, :, :], pair_a[:, :, :, :], AX.X, ALU.add))
                v(dve.tensor_tensor(pair_a[:, :, :, :], pair_a[:, :, :, :], pj, ALU.mult))
                v(dve.tensor_reduce(before[:, :, :], pair_a[:, :, :, :], AX.X, ALU.add))
                v(dve.tensor_scalar(flat(sel), flat(before), 0.9, None, ALU.is_lt))
                v(dve.tensor_scalar(flat(rank), flat(rank), 1.0, None, ALU.add))
                v(dve.tensor_tensor(key[:, :, :], rank[:, :, :], prob[:, :, :], ALU.subtract))
                v(dve.tensor_tensor(key[:, :, :], key[:, :, :], sel[:, :, :], ALU.mult))
                v(dve.tensor_scalar(flat(t1), flat(sel), -FAR, FAR, ALU.mult, ALU.add))
                v(dve.tensor_tensor(key[:, :, :], key[:, :, :], t1[:, :, :], ALU.add))
                v(dve.memset(T[:, :], 0.0))

                def count(which):
                    v(dve.tensor_tensor(t2[:, :, :], key[:, :, :], over_t(which), ALU.is_lt))
                    v(dve.tensor_reduce(cnt[:, :], t2[:, :, :].rearrange("p t e -> p e t"), AX.X, ALU.add))
                    dve.tensor_copy(cnt_b[:, :], cnt[:, :]).then_inc(s["built"], 1)

                for k, bit in enumerate(STEPS):
                    v(dve.tensor_scalar(cand[:, :], T[:, :], 2.0 ** bit, None, ALU.add))
                    count(cand[:, :])
                    dve.wait_ge(s["ones_mm"], k + 1)
                    v(dve.tensor_scalar(step[:, :], ps[:, 0, 0:E], float(CAP), 2.0 ** bit, ALU.is_lt, ALU.mult))
                    v(dve.tensor_tensor(T[:, :], T[:, :], step[:, :], ALU.add))
                count(T[:, :])
                dve.wait_ge(s["ones_mm"], len(STEPS) + 1)
                v(dve.tensor_scalar(need[:, :], ps[:, 0, 0:E], -1.0, float(CAP), ALU.mult, ALU.add))

                def ranks(k):
                    dve.wait_ge(s["pre_mm"], k + 1)
                    v(dve.tensor_copy(tot[:, :, :], ps[:, 3, 0:NE].rearrange("p (t e) -> p e t", e=E)))
                    for e in range(E):
                        ins = dve.tensor_tensor_scan(offs[:, e, 1:NT + 1], c["ones_row"][:, 0:NT], tot[:, e, :], 0.0,
                                                     ALU.mult, ALU.add)
                    v(ins)
                    v(dve.tensor_tensor(pos[:, :, :], ps[:, 1, 0:NE].rearrange("p (t e) -> p t e", e=E),
                                        offs[:, :, 0:NT].rearrange("p e t -> p t e"), ALU.add))

                v(dve.memset(offs[:, :, :], 0.0))
                v(dve.tensor_tensor(t1[:, :, :], key[:, :, :], over_t(T[:, :]), ALU.is_equal))
                dve.tensor_copy(flat(mask_b), flat(t1)).then_inc(s["built"], 1)
                ranks(0)
                v(dve.tensor_tensor(pos[:, :, :], pos[:, :, :], over_t(need[:, :]), ALU.is_lt))
                v(dve.tensor_tensor(t1[:, :, :], t1[:, :, :], pos[:, :, :], ALU.mult))
                v(dve.tensor_tensor(t1[:, :, :], t1[:, :, :], t2[:, :, :], ALU.add))
                v(dve.tensor_tensor(final[:, :, :], t1[:, :, :], sel[:, :, :], ALU.mult))
                dve.tensor_copy(flat(mask_b), flat(final)).then_inc(s["built"], 1)
                ranks(1)
                v(dve.tensor_scalar(flat(chunk), flat(pos), float(P), None, ALU.is_ge))
                for k in range(2, CT):
                    v(dve.tensor_scalar(flat(t1), flat(pos), float(P * k), None, ALU.is_ge))
                    v(dve.tensor_tensor(chunk[:, :, :], chunk[:, :, :], t1[:, :, :], ALU.add))
                v(dve.scalar_tensor_tensor(out=slot[:, :, :], in0=chunk[:, :, :], scalar=-float(P), in1=pos[:, :, :],
                                           op0=ALU.mult, op1=ALU.add))
                v(dve.tensor_scalar(flat(slot), flat(slot), 1.0, None, ALU.add))
                v(dve.tensor_tensor(slot[:, :, :], slot[:, :, :], final[:, :, :], ALU.mult))
                v(dve.tensor_scalar(flat(slot), flat(slot), -1.0, None, ALU.add))
                v(dve.tensor_scalar(c["spare"][:, :], c["part"][:, :], float(N), None, ALU.add))

                def build(e):
                    oh = onehot[:, e % 2, :, :]
                    v(dve.tensor_tensor(oh, c["slot"][:, :].rearrange("p (a q) -> p a q", a=1).broadcast_to([P, NT, P]),
                                        slot[:, :, e:e + 1].broadcast_to([P, NT, P]), ALU.is_equal))
                    v(dve.tensor_tensor(is_chunk[:, :, :],
                                        c["slot"][:, 0:CT].rearrange("p (a q) -> p a q", a=1).broadcast_to([P, NT, CT]),
                                        chunk[:, :, e:e + 1].broadcast_to([P, NT, CT]), ALU.is_equal))
                    v(dve.tensor_tensor(rhs[:, e % 2, :, 0, :], is_chunk[:, :, :],
                                        c["tile_no"][:, :].rearrange("p (t a) -> p t a", a=1).broadcast_to([P, NT, CT]),
                                        ALU.mult))
                    v(dve.tensor_scalar(rhs[:, e % 2, :, 1, :], is_chunk[:, :, :], c["part"][:, 0:1], None, ALU.mult))
                    dve.tensor_copy(rhs[:, e % 2, :, 2, :], is_chunk[:, :, :]).then_inc(s["built"], 1)

                def read(e):
                    dve.wait_ge(s["slot_ps"], e + 1)
                    v(dve.tensor_copy(got[:, :, :], ps[:, e % 2, 0:3 * CT].rearrange("p (a k) -> p a k", a=3)))
                    v(dve.scalar_tensor_tensor(out=tok[:, :], in0=got[:, 0, :], scalar=float(P), in1=got[:, 1, :],
                                               op0=ALU.mult, op1=ALU.add))
                    v(dve.tensor_copy(valid[:, e, :], got[:, 2, :]))
                    v(dve.tensor_copy(idx_get[:, e, :], tok[:, :]))
                    v(dve.tensor_scalar(away[:, :], got[:, 2, :], -1.0, 1.0, ALU.mult, ALU.add))
                    v(dve.scalar_tensor_tensor(out=idx_put[:, e, :], in0=away[:, :], scalar=c["spare"][:, 0:1],
                                               in1=tok[:, :], op0=ALU.mult, op1=ALU.add))

                for e in range(E + 1):
                    if e < E:
                        build(e)
                    if e:
                        read(e - 1)


def experts(nc, c, rows, ysum, w1, w2, idx_get, idx_put, valid):
    with ExitStack() as ctx:
        sb = allocator(ctx, nc, "ex")
        w1_in = sb("w1_in", [P, EF // P, D], F32)
        w2_in = sb("w2_in", [P, DC, EF], F32)
        w1T = sb("w1T", [P, DC, EF], F32)
        w2T = sb("w2T", [P, EF // P, D], F32)
        ix = sb("ix", [P, 2, CT], I32)
        vl = sb("vl", [P, CT], F32)
        xg = sb("xg", [P, CT, ROW], F32)
        sc = sb("sc", [P, CT], F32)
        xT = sb("xT", [P, DC, CAP], F32)
        hT = sb("hT", [P, EF // P, CAP], F32)
        y = sb("y", [P, CT, D], F32)
        ps = ctx.enter_context(nc.psum_tensor("ex_ps", [P, 8, 512], F32))
        s = sems(ctx, nc, "ex", "w ix got w_ps wT x_ps xT sc sv h_ps hT y_ps y put landed")
        EC = EF // P
        FREE_AT_START = "w_ps landed y_ps".split()
        with nc.Block() as block:
            @block.sync
            def _(sp):
                with sp.Fori(0, E) as e:
                    sp.wait_ge(s["w_ps"], 2 * e + 1)
                    sp.dma_start(w1_in[:, :, :], w1[ds(e, 1)].rearrange("a (c p) d -> p (a c) d", p=P)).then_inc(s["w"], 16)
                    sp.dma_start(w2_in[:, :, :], w2[ds(e, 1)].rearrange("a (c p) f -> p (a c) f", p=P)).then_inc(s["w"], 16)

            @block.gpsimd
            def _(pool):
                with pool.Fori(0, E) as e:
                    wait_apart(pool, s["ix"], e + 1)
                    for t in range(CT):
                        pool.indirect_dma_start(
                            out=xg[:, t, :], out_offset=None, in_=rows,
                            in_offset=bass.IndirectOffsetOnAxis(ap=ix[:, 0, t:t + 1], axis=0)).then_inc(s["got"], 16)
                    wait_apart(pool, s["y"], e + 1)
                    for t in range(CT):
                        pool.indirect_dma_start(
                            out=ysum, out_offset=bass.IndirectOffsetOnAxis(ap=ix[:, 1, t:t + 1], axis=0),
                            in_=y[:, t, :], in_offset=None, compute_op=ALU.add).then_inc(s["put"], 16)
                    wait_apart(pool, s["put"], 16 * CT * (e + 1))
                    pool.sem_inc(s["landed"], 1)

            @block.tensor
            def _(pe):
                with pe.Fori(0, E) as e:
                    pe.wait_ge(s["w"], 32 * e + 32)
                    for k in range(DC):
                        for f in range(EC):
                            ins = pe.transpose(ps[:, 0, (k * EC + f) * P:(k * EC + f + 1) * P],
                                               w1_in[:, f, P * k:P * k + P], c["ident"][:, :])
                    ins.then_inc(s["w_ps"], 1)
                    for f in range(EC):
                        for k in range(DC):
                            ins = pe.transpose(ps[:, 1, (f * DC + k) * P:(f * DC + k + 1) * P],
                                               w2_in[:, k, P * f:P * f + P], c["ident"][:, :])
                    ins.then_inc(s["w_ps"], 1)
                    pe.wait_ge(s["got"], 16 * CT * (e + 1))
                    for k in range(DC):
                        for t in range(CT):
                            ins = pe.transpose(ps[:, 2 + k, P * t:P * t + P], xg[:, t, P * k:P * k + P], c["ident"][:, :])
                    ins.then_inc(s["x_ps"], 1)
                    pe.wait_ge(s["wT"], 2 * e + 2)
                    pe.wait_ge(s["xT"], e + 1)
                    for f in range(EC):
                        for k in range(DC):
                            ins = pe.matmul(ps[:, 4 + f, :], w1T[:, k, P * f:P * f + P], xT[:, k, :], start=k == 0,
                                            stop=k == DC - 1)
                        ins.then_inc(s["h_ps"], 1)
                    pe.wait_ge(s["hT"], EC * (e + 1))
                    for t in range(CT):
                        for f in range(EC):
                            ins = pe.matmul(ps[:, 6 + t // 2, D * (t % 2):D * (t % 2) + D], hT[:, f, P * t:P * t + P],
                                            w2T[:, f, :], start=f == 0, stop=f == EC - 1)
                    ins.then_inc(s["y_ps"], 1)

            @block.scalar
            def _(act):
                with act.Fori(0, E) as e:
                    act.wait_ge(s["y_ps"], e + 1)
                    act.wait_ge(s["x_ps"], e + 1)
                    for k in range(DC):
                        ins = act.copy(xT[:, k, :], ps[:, 2 + k, :])
                    ins.then_inc(s["xT"], 1)
                    for f in range(EC):
                        act.wait_ge(s["h_ps"], EC * e + f + 1)
                        act.activation(hT[:, f, :], ps[:, 4 + f, :], ACT.Gelu).then_inc(s["hT"], 1)

            @block.vector
            def _(dve):
                for name in FREE_AT_START:
                    dve.sem_inc(s[name], 1)
                with dve.Fori(0, E) as e:
                    dve.wait_ge(s["landed"], e + 1)
                    dve.tensor_copy(ix[:, 0, :], idx_get[:, ds(e, 1), :].rearrange("p a t -> p (a t)"))
                    dve.tensor_copy(ix[:, 1, :], idx_put[:, ds(e, 1), :].rearrange("p a t -> p (a t)"))
                    dve.tensor_copy(vl[:, :], valid[:, ds(e, 1), :].rearrange("p a t -> p (a t)")).then_inc(s["ix"], 1)
                    dve.wait_ge(s["w_ps"], 2 * e + 2)
                    dve.tensor_copy(w1T[:, :, :], ps[:, 0, :].rearrange("p (k f) -> p k f", k=DC)).then_inc(s["wT"], 1)
                    dve.wait_ge(s["w_ps"], 2 * e + 3)
                    dve.tensor_copy(w2T[:, :, :], ps[:, 1, :].rearrange("p (f d) -> p f d", f=EC)).then_inc(s["wT"], 1)
                    dve.wait_ge(s["got"], 16 * CT * (e + 1))
                    dve.wait_ge(s["ix"], e + 1)
                    dve.tensor_tensor(sc[:, :], xg[:, :, ds(e + D, 1)].rearrange("p t a -> p (t a)"), vl[:, :],
                                      ALU.mult).then_inc(s["sc"], 1)
                    dve.wait_ge(s["sc"], e + 1)
                    dve.wait_ge(s["y_ps"], e + 2)
                    for t in range(CT):
                        ins = dve.tensor_scalar(y[:, t, :], ps[:, 6 + t // 2, D * (t % 2):D * (t % 2) + D],
                                                sc[:, t:t + 1], None, ALU.mult)
                    ins.then_inc(s["y"], 1)


def clear_sum(nc, ysum):
    with ExitStack() as ctx:
        z = ctx.enter_context(nc.sbuf_tensor("cl_z", [P, D], F32))
        s = sems(ctx, nc, "cl", "z out")
        R = (N + SPARE) // P
        with nc.Block() as block:
            @block.vector
            def _(dve):
                dve.memset(z[:, :], 0.0).then_inc(s["z"], 1)

            @block.sync
            def _(sp):
                sp.wait_ge(s["z"], 1)
                yv = ysum.rearrange("(t p) d -> t p d", p=P)
                for t in range(R):
                    sp.dma_start(yv[t], z[:, :]).then_inc(s["out"], 16)
                sp.wait_ge(s["out"], 16 * R)


def finish(nc, x_all, ysum, out):
    with ExitStack() as ctx:
        y = ctx.enter_context(nc.sbuf_tensor("fi_y", [P, 2, TPB, D], F32))
        s = sems(ctx, nc, "fi", "y0 y1 sum out")
        yv = ysum[0:N, :].rearrange("(t p) d -> p t d", p=P)
        ov = out.rearrange("b (t p) d -> p (b t) d", p=P)
        with nc.Block() as block:
            @block.sync
            def _(sp):
                for i in range(B):
                    if i >= 2:
                        sp.wait_ge(s["sum"], i - 1)
                    sp.dma_start(y[:, i % 2, :, :], yv[:, i * TPB:(i + 1) * TPB, :]).then_inc(s[f"y{i % 2}"], 16)

            @block.vector
            def _(dve):
                for i in range(B):
                    dve.wait_ge(s[f"y{i % 2}"], 16 * (i // 2 + 1))
                    xv = x_all[:, i * TPB:(i + 1) * TPB, :]
                    dve.tensor_tensor(xv, xv, y[:, i % 2, :, :], ALU.add).then_inc(s["sum"], 1)

            @block.scalar
            def _(act):
                for i in range(B):
                    act.wait_ge(s["sum"], i + 1)
                    act.dma_start(ov[:, i * TPB:(i + 1) * TPB, :], x_all[:, i * TPB:(i + 1) * TPB, :]).then_inc(s["out"], 16)
                act.wait_ge(s["out"], 16 * B)


def build(nc, a, rows, ysum, out):
    with ExitStack() as ctx:
        sb = allocator(ctx, nc, "k")
        x_all = sb("x", [P, NT, D], F32)
        c = {"ident": sb("ident", [P, P], F32), "sel": sb("sel", [MH, MH, P], F32), "lower": sb("lower", [P, P], F32),
             "lower_bf": sb("lower_bf", [P, P], BF16), "ones_row": sb("ones_row", [P, S], F32),
             "ones_bf": sb("ones_bf", [P, P], BF16), "minus_half": sb("minus_half", [P, 16], F32),
             "earlier": sb("earlier", [P, E, E], F32), "slot": sb("slot", [P, P], F32), "part": sb("part", [P, 1], F32),
             "tile_no": sb("tile_no", [P, NT], F32), "spare": sb("spare", [P, 1], F32)}
        setup(nc, c, a["x"], x_all)
        with nc.Block() as block:
            @block.vector
            def _(dve):
                dve.tensor_copy(c["lower_bf"][:, :], c["lower"][:, :])
        with ExitStack() as mid:
            sbm = allocator(mid, nc, "m")
            ctxT_all = sbm("ctxT", [P, DC, N], F32)
            mlstm(nc, c, x_all, ctxT_all, a["ctx_1024"], a["L0_xattn_ig_kernel"], a["L0_xattn_ig_bias"],
                  a["L0_xattn_fg_kernel"], a["L0_xattn_fg_bias"], a["L0_xattn_outnorm_weight"])
            xnT_all = sbm("xnT", [P, DC, N], F32)
            norm_and_turn(nc, c, "n1", x_all, xnT_all)
            mlp(nc, c, x_all, xnT_all, a["L0_ffn_w1"], a["L0_ffn_b1"], a["L0_ffn_w2"], a["L0_ffn_b2"])
            norm_and_turn(nc, c, "n2", x_all, xnT_all)
            attention(nc, c, x_all, xnT_all, ctxT_all, a["L1_xattn_W_Query"], a["L1_xattn_W_Key"],
                      a["L1_xattn_W_Value"], a["L1_xattn_W_Output"], a["L1_xattn_B_Query"], a["L1_xattn_B_Key"],
                      a["L1_xattn_B_Value"], a["L1_xattn_B_Output"])
        clear_sum(nc, ysum)
        prob = sb("prob", [P, NT, E], F32)
        final = sb("final", [P, NT, E], F32)
        idx_get = sb("idx_get", [P, E, CT], I32)
        idx_put = sb("idx_put", [P, E, CT], I32)
        valid = sb("valid", [P, E, CT], F32)
        with ExitStack() as mid:
            xnT_all = allocator(mid, nc, "r")("xnT", [P, DC, N], F32)
            norm_and_turn(nc, c, "n3", x_all, xnT_all, rows)
            router(nc, c, xnT_all, a["L1_ffn_gate_w"], rows, prob, final, idx_get, idx_put, valid)
        experts(nc, c, rows, ysum, a["L1_ffn_w1"], a["L1_ffn_w2"], idx_get, idx_put, valid)
        finish(nc, x_all, ysum, out)


_INS = ["x", "ctx_1024", "L0_xattn_ig_kernel", "L0_xattn_ig_bias", "L0_xattn_fg_kernel", "L0_xattn_fg_bias",
        "L0_xattn_outnorm_weight", "L0_ffn_w1", "L0_ffn_b1", "L0_ffn_w2", "L0_ffn_b2", "L1_xattn_W_Query",
        "L1_xattn_W_Key", "L1_xattn_W_Value", "L1_xattn_W_Output", "L1_xattn_B_Query", "L1_xattn_B_Key",
        "L1_xattn_B_Value", "L1_xattn_B_Output", "L1_ffn_gate_w", "L1_ffn_w1", "L1_ffn_w2"]


def kernel(**inputs):
    import numpy as np
    import concourse.bacc as bacc
    from concourse.bass_utils import run_bass_kernel_spmd as run

    nc = bacc.Bacc("TRN2", target_bir_lowering=False, num_devices=1)
    arrays, aps = {}, {}
    for name in _INS:
        arr = np.ascontiguousarray(inputs[name])
        arrays[f"in_{name}"] = arr
        aps[name] = nc.dram_tensor(f"in_{name}", arr.shape, mybir.dt.from_np(arr.dtype), kind="ExternalInput").ap()
    rows = nc.dram_tensor("rows", (N, ROW), F32, kind="Internal").ap()
    ysum = nc.dram_tensor("ysum", (N + SPARE, D), F32, kind="Internal").ap()
    out = nc.dram_tensor("out_0", (B, S, D), F32, kind="ExternalOutput").ap()
    build(nc, aps, rows, ysum, out)
    r = run(nc, [arrays], core_ids=[0])
    return r.results[0]["out_0"]
```

```python
from contextlib import ExitStack

import concourse.bass as bass
from concourse import mybir

F32 = mybir.dt.float32
BF16 = mybir.dt.bfloat16
I32 = mybir.dt.int32
U32 = mybir.dt.uint32
ALU = mybir.AluOpType
ACT = mybir.ActivationFunctionType
AX = mybir.AxisListType
ds = bass.ds

P = 128
B, S, D = 8, 512, 256
N = B * S
TPB = S // P
NT = N // P
DC = D // P
MH, MD = 4, 64
F = 1024
FC = F // P
AH, AD = 16, 64
HP = AH // 2
E, EF = 8, 256
CAP = N // E
CT = CAP // P
ROW = D + E
SPARE = P
LN_EPS = 1e-5
MIX_EPS = 1e-6
FAR = 1e9


def sems(ctx, nc, phase, names):
    return {n: ctx.enter_context(nc.semaphore(f"{phase}_{n}")) for n in names.split()}


def wait_apart(eng, sem, value):
    eng.wait_ge(sem, value)
    eng.nop(nofuse=True)


def norm_batch_dve(dve, s, i, x_all, tmp, wait_free):
    for t in range(TPB):
        ins = dve.bn_stats(tmp["stats"][:, t, :], x_all[:, ds(i * TPB + t, 1), :].rearrange("p a d -> p (a d)"))
    ins.then_inc(s["stats"], 1)
    wait_apart(dve, s["stats"], i + 1)
    for t in range(TPB):
        ins = dve.bn_aggr(tmp["mv"][:, t, :], tmp["stats"][:, t, :])
    ins.then_inc(s["mv"], 1)
    dve.wait_ge(s["mv"], i + 1)
    dve.tensor_scalar(tmp["ve"][:, :], tmp["mv"][:, :, 1], LN_EPS, None, ALU.add).then_inc(s["ve"], 1)
    wait_free()
    dve.wait_ge(s["rstd"], i + 1)
    for t in range(TPB):
        ins = dve.tensor_scalar(tmp["xn"][:, t, :], x_all[:, ds(i * TPB + t, 1), :].rearrange("p a d -> p (a d)"),
                                tmp["mv"][:, t, 0:1], tmp["rstd"][:, t:t + 1], ALU.subtract, ALU.mult)
    ins.then_inc(s["xn"], 1)


def norm_batch_pool(pool, s, i, tmp, minus_half):
    wait_apart(pool, s["ve"], i + 1)
    pool.tensor_tensor(tmp["rstd"][:, :], tmp["ve"][:, :], minus_half[:, 0:TPB], ALU.pow).then_inc(s["rstd"], 1)


def norm_tmp(sb):
    return {"stats": sb("stats", [P, TPB, 6], F32), "mv": sb("mv", [P, TPB, 2], F32),
            "ve": sb("ve", [P, TPB], F32), "rstd": sb("rstd", [P, TPB], F32), "xn": sb("xn", [P, TPB, D], F32)}


def allocator(ctx, nc, phase):
    def sb(name, shape, dt):
        return ctx.enter_context(nc.sbuf_tensor(f"{phase}_{name}", shape, dt))
    return sb


def setup(nc, c, x, x_all):
    with ExitStack() as ctx:
        s = sems(ctx, nc, "st", "x zero fill")
        with nc.Block() as block:
            @block.sync
            def _(sp):
                xv = x.rearrange("b (t p) d -> p (b t) d", p=P)
                for i in range(B):
                    sp.dma_start(x_all[:, i * TPB:(i + 1) * TPB, :], xv[:, i * TPB:(i + 1) * TPB, :]).then_inc(s["x"], 16)
                sp.wait_ge(s["x"], 16 * B)

            @block.gpsimd
            def _(pool):
                pool.memset(c["ident"][:, :], 0.0)
                pool.memset(c["sel"][:, :, :], 0.0)
                pool.memset(c["lower"][:, :], 1.0)
                pool.memset(c["ones_row"][:, :], 1.0)
                pool.memset(c["ones_bf"][:, :], 1.0)
                pool.memset(c["minus_half"][:, :], -0.5)
                pool.memset(c["earlier"][:, :, :], 1.0).then_inc(s["zero"], 1)
                pool.wait_ge(s["zero"], 1)
                pool.affine_select(out=c["ident"][:, :], in_=c["ident"][:, :], compare_op=ALU.not_equal, fill=1.0,
                                   base=0, pattern=[[-1, P]], channel_multiplier=1)
                pool.affine_select(out=c["sel"][:, :, :], in_=c["sel"][:, :, :], compare_op=ALU.not_equal, fill=1.0,
                                   base=0, pattern=[[-1, MH], [0, P]], channel_multiplier=1)
                pool.affine_select(out=c["lower"][:, :], in_=c["lower"][:, :], compare_op=ALU.is_gt, fill=0.0,
                                   base=0, pattern=[[1, P]], channel_multiplier=-1)
                pool.affine_select(out=c["earlier"][:, :, :], in_=c["earlier"][:, :, :], compare_op=ALU.is_gt,
                                   fill=0.0, base=0, pattern=[[1, E], [-1, E]], channel_multiplier=0)
                pool.iota(c["slot"][:, :], pattern=[[1, P]], base=0, channel_multiplier=0,
                          allow_small_or_imprecise_dtypes=True)
                pool.iota(c["part"][:, :], pattern=[[0, 1]], base=0, channel_multiplier=1,
                          allow_small_or_imprecise_dtypes=True)
                pool.iota(c["tile_no"][:, :], pattern=[[1, NT]], base=0, channel_multiplier=0,
                          allow_small_or_imprecise_dtypes=True).then_inc(s["fill"], 1)
                pool.wait_ge(s["fill"], 1)


def mlstm(nc, c, x_all, ctxT_all, ctx_in, ig_kernel, ig_bias, fg_kernel, fg_bias, outnorm):
    OFF = [0, 512, 896, 1152]
    LEN = [S - P * t for t in range(TPB)]
    PACK = sum(LEN)
    GW = 36
    with ExitStack() as ctx:
        sb = allocator(ctx, nc, "ml")
        tmp = norm_tmp(sb)
        ctx_s = sb("ctx", [P, TPB, D], F32)
        qT = sb("qT", [P, DC, S], F32)
        kT = sb("kT", [P, DC, S], F32)
        vaug = sb("vaug", [P, TPB, MH, MD + 1], F32)
        gk_in = sb("gk_in", [P, 3 * DC, 2 * MH], F32)
        gate_w = sb("gate_w", [P, 2 * DC, GW], F32)
        gbias = sb("gbias", [GW, 1], F32)
        w_row = sb("w_row", [P, D], F32)
        ig = sb("ig", [MH, S], F32)
        fg = sb("fg", [MH, S], F32)
        absf = sb("absf", [MH, S], F32)
        efg = sb("efg", [MH, S], F32)
        lfg = sb("lfg", [MH, S], F32)
        cums = sb("cums", [MH, S], F32)
        g = sb("g", [MH, S], F32)
        gmax = sb("gmax", [MH, S], F32)
        logmax = sb("logmax", [MH, S], F32)
        floor = sb("floor", [MH, S], F32)
        cols = sb("cols", [P, 2, TPB, MH], F32)
        Dm = sb("Dm", [P, 2, PACK], F32)
        C = sb("C", [P, PACK], F32)
        hT = sb("hT", [MD + 1, S], F32)
        hs = sb("hs", [P, MH, TPB, MD + 1], F32)
        nrm = sb("nrm", [P, 8, MH * TPB], F32)
        hw = sb("hw", [P, MH * TPB, MD], F32)
        sq = sb("sq", [P, MH * TPB, MD], F32)
        ps = ctx.enter_context(nc.psum_tensor("ml_ps", [P, 8, 512], F32))
        C_BANK, M_BANK, H_BANK, ROW_BANK, TURN_BANK = 0, 3, 4, 5, 6
        s = sems(ctx, nc, "ml", "w wset gw ctx vaug stats mv ve rstd xn xn_turned ctx_turned qT kT ctxT gates rows "
                 "act_rows cols_ps cols m_ps d_in d_exp d_masked c_ps c pv hT h_turned hs fin fin_pow")
        ident = c["ident"]
        cv = ctx_in.rearrange("b (t p) d -> b p t d", p=P)
        TR = (MH + 1 - 1)

        FREE_AT_START = "pv cols d_in c hT hs c_ps ctxT cols_ps h_turned xn_turned".split()
        with nc.Block() as block:
            @block.sync
            def _(sp):
                sp.dma_start(ctx_s[:, :, :], cv[0]).then_inc(s["ctx"], 16)
                sp.dma_start(gk_in[:, :, 0:MH], ig_kernel.rearrange("(c p) h -> p c h", p=P)).then_inc(s["w"], 16)
                sp.dma_start(gk_in[:, :, MH:2 * MH], fg_kernel.rearrange("(c p) h -> p c h", p=P)).then_inc(s["w"], 16)
                sp.wait_ge(s["wset"], 1)
                sp.dma_start(gbias[0:MH, :], ig_bias.rearrange("(h a) -> h a", a=1)).then_inc(s["w"], 16)
                sp.dma_start(gbias[32:32 + MH, :], fg_bias.rearrange("(h a) -> h a", a=1)).then_inc(s["w"], 16)
                row = outnorm.rearrange("h d -> (h d)").rearrange("(a n) -> a n", a=1)
                sp.dma_start(w_row[:, :], row.broadcast_to([P, D])).then_inc(s["w"], 16)
                with sp.Fori(1, B) as i:
                    sp.wait_ge(s["ctx_turned"], i)
                    sp.wait_ge(s["vaug"], i)
                    sp.dma_start(ctx_s[:, :, :], cv[ds(i, 1)].rearrange("a p t d -> p (a t) d")).then_inc(s["ctx"], 16)

            @block.gpsimd
            def _(pool):
                pool.memset(gbias[:, :], 0.0).then_inc(s["wset"], 1)
                pool.memset(vaug[:, :, :, MD:MD + 1], 1.0)
                with pool.Fori(0, B) as i:
                    norm_batch_pool(pool, s, i, tmp, c["minus_half"])
                    wait_apart(pool, s["ctx"], 16 * i + 16)
                    wait_apart(pool, s["pv"], MH * i + 1)
                    pool.tensor_copy(vaug[:, :, :, 0:MD],
                                     ctx_s[:, :, :].rearrange("p t (h d) -> p t h d", h=MH)).then_inc(s["vaug"], 1)
                    wait_apart(pool, s["kT"], i + 1)
                    pool.tensor_copy(ctxT_all[:, :, ds(i * S, S)], kT[:, :, :]).then_inc(s["ctxT"], 1)
                    for h in range(MH):
                        wait_apart(pool, s["d_exp"], MH * i + h + 1)
                        for t in range(TPB):
                            diag = Dm[:, h % 2, OFF[t]:OFF[t] + P]
                            pool.affine_select(out=diag, in_=diag, compare_op=ALU.is_ge, fill=0.0, base=0,
                                               pattern=[[1, P]], channel_multiplier=-1).then_inc(s["d_masked"], 1)
                    wait_apart(pool, s["fin"], 14 * i + 11)
                    pool.tensor_tensor(nrm[:, 7, :], nrm[:, 6, :], c["minus_half"][:, 0:MH * TPB],
                                       ALU.pow).then_inc(s["fin_pow"], 1)

            @block.tensor
            def _(pe):
                def gate_maps(i):
                    pe.wait_ge(s["cols"], i + 1)
                    pe.wait_ge(s["qT"], i + 1)
                    pe.wait_ge(s["kT"], i + 1)
                    for k in range(2 * DC):
                        rhs = qT[:, k, :] if k < DC else kT[:, k - DC, :]
                        ins = pe.matmul(ps[0:GW, ROW_BANK, :], gate_w[:, k, :], rhs, start=k == 0, stop=k == 2 * DC - 1)
                    ins.then_inc(s["gates"], 1)

                def spread_max(i, h):
                    pe.wait_ge(s["rows"], 8 * i + 7)
                    pe.wait_ge(s["d_in"], MH * i + h + 1)
                    pe.matmul(ps[:, M_BANK, :], c["sel"][:, h, :], gmax[:, :], start=True, stop=True).then_inc(s["m_ps"], 1)

                def scores(i, h):
                    pe.wait_ge(s["c"], MH * i + h + 1)
                    lo = MD * (h % 2)
                    for t in range(TPB):
                        bank, at = (t, 0) if t < 3 else (2, LEN[2])
                        ins = pe.matmul(ps[:, C_BANK + bank, at:at + LEN[t]], kT[lo:lo + MD, h // 2, P * t:P * t + P],
                                        qT[lo:lo + MD, h // 2, P * t:S], start=True, stop=True)
                    ins.then_inc(s["c_ps"], 1)

                def values(i, h):
                    pe.wait_ge(s["c"], MH * i + h + 2)
                    pe.wait_ge(s["hT"], MH * i + h + 1)
                    for t in range(TPB):
                        ins = pe.matmul(ps[0:MD + 1, H_BANK, P * t:S], vaug[:, t, h, :], C[:, OFF[t]:OFF[t] + LEN[t]],
                                        start=t == 0, stop=t == TPB - 1, skip_group_check=True)
                    ins.then_inc(s["pv"], 1)

                def turn_head(i, h):
                    pe.wait_ge(s["hT"], MH * i + h + 2)
                    wait_apart(pe, s["hs"], MH * i + h + 1)
                    for t in range(TPB):
                        ins = pe.transpose(ps[:, TURN_BANK + 1, (MD + 1) * t:(MD + 1) * (t + 1)],
                                           hT[:, P * t:P * t + P], ident[0:MD + 1, 0:MD + 1])
                    ins.then_inc(s["h_turned"], 1)

                pe.wait_ge(s["gw"], 6)
                with pe.Fori(0, B) as i:
                    pe.wait_ge(s["xn"], i + 1)
                    pe.wait_ge(s["hs"], MH * i + 1)
                    for k in range(DC):
                        for t in range(TPB):
                            ins = pe.transpose(ps[:, TURN_BANK + k, P * t:P * t + P], tmp["xn"][:, t, P * k:P * k + P],
                                               ident[:, :])
                    ins.then_inc(s["xn_turned"], 1)
                    pe.wait_ge(s["ctx"], 16 * i + 16)
                    pe.wait_ge(s["hT"], MH * i + 1)
                    pe.wait_ge(s["cols"], i + 1)
                    for k in range(DC):
                        for t in range(TPB):
                            ins = pe.transpose(ps[:, H_BANK + k, P * t:P * t + P], ctx_s[:, t, P * k:P * k + P],
                                               ident[:, :])
                    ins.then_inc(s["ctx_turned"], 1)
                    gate_maps(i)
                    scores(i, 0)
                    wait_apart(pe, s["rows"], 8 * i + 6)
                    for t in range(TPB):
                        pe.transpose(ps[:, ROW_BANK, MH * t:MH * t + MH], g[:, P * t:P * t + P], ident[0:MH, 0:MH])
                    wait_apart(pe, s["act_rows"], 3 * i + 3)
                    for t in range(TPB):
                        ins = pe.transpose(ps[:, ROW_BANK, MH * (TPB + t):MH * (TPB + t + 1)],
                                           floor[:, P * t:P * t + P], ident[0:MH, 0:MH])
                    ins.then_inc(s["cols_ps"], 1)
                    spread_max(i, 0)
                    for h in range(MH):
                        if h:
                            scores(i, h)
                        if h + 1 < MH:
                            spread_max(i, h + 1)
                        if h:
                            turn_head(i, h - 1)
                        pe.wait_ge(s["vaug"], i + 1)
                        values(i, h)
                    turn_head(i, MH - 1)

            @block.scalar
            def _(act):
                with act.Fori(0, B) as i:
                    act.wait_ge(s["c_ps"], MH * i + 1)
                    act.wait_ge(s["xn_turned"], i + 2)
                    for k in range(DC):
                        ins = act.copy(qT[:, k, :], ps[:, TURN_BANK + k, :])
                    ins.then_inc(s["qT"], 1)
                    act.wait_ge(s["ctxT"], i + 1)
                    act.wait_ge(s["ctx_turned"], i + 1)
                    for k in range(DC):
                        ins = act.copy(kT[:, k, :], ps[:, H_BANK + k, :])
                    ins.then_inc(s["kT"], 1)
                    act.wait_ge(s["rows"], 8 * i + 3)
                    act.activation(efg[:, :], absf[:, :], ACT.Exp, scale=-1.0).then_inc(s["act_rows"], 1)
                    act.wait_ge(s["act_rows"], 3 * i + 1)
                    act.activation(lfg[:, :], efg[:, :], ACT.Ln, bias=1.0).then_inc(s["act_rows"], 1)
                    act.wait_ge(s["rows"], 8 * i + 8)
                    act.wait_ge(s["cols_ps"], i + 1)
                    act.activation(floor[:, :], logmax[:, :], ACT.Exp, scale=-1.0).then_inc(s["act_rows"], 1)
                    for h in range(MH + 1):
                        if h < MH:
                            act.wait_ge(s["d_in"], MH * i + h + 2)
                            act.activation(Dm[:, h % 2, :], Dm[:, h % 2, :], ACT.Exp, scale=-1.0).then_inc(s["d_exp"], 1)
                        if h:
                            act.wait_ge(s["pv"], MH * i + h + 1)
                            act.wait_ge(s["h_turned"], MH * i + h)
                            act.copy(hT[:, :], ps[0:MD + 1, H_BANK, :]).then_inc(s["hT"], 1)

            @block.vector
            def _(dve):
                for name in FREE_AT_START:
                    dve.sem_inc(s[name], 1)
                dve.memset(gate_w[:, :, :], 0.0).then_inc(s["gw"], 1)
                dve.wait_ge(s["gw"], 1)
                dve.wait_ge(s["w"], 16 * 5)
                for half in range(2):
                    src = gk_in[:, :, MH * half:MH * half + MH]
                    dst = gate_w[:, :, 32 * half:32 * half + MH]
                    dve.tensor_copy(dst[:, 0:DC, :], src[:, 0:DC, :]).then_inc(s["gw"], 1)
                    dve.tensor_tensor(dst[:, DC:2 * DC, :], src[:, DC:2 * DC, :], src[:, 2 * DC:3 * DC, :],
                                      ALU.add).then_inc(s["gw"], 1)
                dve.memset(nrm[:, :, :], 1.0).then_inc(s["gw"], 1)
                ones_row = c["ones_row"][0:MH, :]

                def decay_in(i, h):
                    dve.wait_ge(s["m_ps"], MH * i + h + 1)
                    for t in range(TPB):
                        ins = dve.tensor_scalar(Dm[:, h % 2, OFF[t]:OFF[t] + LEN[t]], ps[:, M_BANK, P * t:S],
                                                cols[:, 0, t, h:h + 1], 0.0, ALU.subtract, ALU.max)
                    ins.then_inc(s["d_in"], 1)

                def weigh(i, h):
                    dve.wait_ge(s["c_ps"], MH * i + h + 2)
                    dve.wait_ge(s["d_masked"], TPB * (MH * i + h + 1))
                    dve.wait_ge(s["pv"], MH * i + h + 1)
                    for bank in range(3):
                        lo, n = OFF[bank], (LEN[bank] if bank < 2 else LEN[2] + LEN[3])
                        ins = dve.scalar_tensor_tensor(out=C[:, lo:lo + n], in0=ps[:, C_BANK + bank, 0:n],
                                                       scalar=MD ** -0.5, in1=Dm[:, h % 2, lo:lo + n],
                                                       op0=ALU.mult, op1=ALU.mult)
                    ins.then_inc(s["c"], 1)

                def keep_head(i, h):
                    dve.wait_ge(s["h_turned"], MH * i + h + 2)
                    dve.tensor_copy(hs[:, h, :, :], ps[:, TURN_BANK + 1, 0:TPB * (MD + 1)].rearrange(
                        "p (t d) -> p t d", t=TPB)).then_inc(s["hs"], 1)

                with dve.Fori(0, B) as i:
                    norm_batch_dve(dve, s, i, x_all, tmp, lambda: dve.wait_ge(s["xn_turned"], i + 1))

                    def row(ins, k):
                        ins.then_inc(s["rows"], 1)
                        dve.wait_ge(s["rows"], 8 * i + k)

                    dve.wait_ge(s["gates"], i + 1)
                    row(dve.tensor_scalar(ig[:, :], ps[0:MH, ROW_BANK, :], gbias[0:MH, :], None, ALU.add), 1)
                    row(dve.tensor_scalar(fg[:, :], ps[32:32 + MH, ROW_BANK, :], gbias[32:32 + MH, :], None, ALU.add), 2)
                    row(dve.scalar_tensor_tensor(out=absf[:, :], in0=fg[:, :], scalar=-1.0, in1=fg[:, :],
                                                 op0=ALU.mult, op1=ALU.max), 3)
                    dve.wait_ge(s["act_rows"], 3 * i + 2)
                    row(dve.scalar_tensor_tensor(out=fg[:, :], in0=fg[:, :], scalar=0.0, in1=lfg[:, :],
                                                 op0=ALU.min, op1=ALU.subtract), 4)
                    row(dve.tensor_tensor_scan(cums[:, :], ones_row, fg[:, :], 0.0, ALU.mult, ALU.add), 5)
                    row(dve.tensor_tensor(g[:, :], ig[:, :], cums[:, :], ALU.subtract), 6)
                    row(dve.tensor_tensor_scan(gmax[:, :], g[:, :], g[:, :], -3.0e38, ALU.max, ALU.max), 7)
                    row(dve.tensor_tensor(logmax[:, :], cums[:, :], gmax[:, :], ALU.add), 8)
                    dve.wait_ge(s["cols_ps"], i + 2)
                    dve.tensor_copy(cols[:, :, :, :], ps[:, ROW_BANK, 0:2 * TPB * MH].rearrange(
                        "p (a t h) -> p a t h", a=2, t=TPB)).then_inc(s["cols"], 1)
                    dve.wait_ge(s["cols"], i + 2)
                    decay_in(i, 0)
                    for h in range(MH):
                        if h + 1 < MH:
                            decay_in(i, h + 1)
                        weigh(i, h)
                        if h:
                            keep_head(i, h - 1)
                    keep_head(i, MH - 1)

                    def fin(ins, k):
                        ins.then_inc(s["fin"], 1)
                        dve.wait_ge(s["fin"], 14 * i + k)

                    def wide(k):
                        return nrm[:, k, :].rearrange("p (g a) -> p g a", a=1).broadcast_to([P, MH * TPB, MD])

                    dve.wait_ge(s["hs"], MH * i + MH + 1)
                    hv = hs[:, :, :, 0:MD].rearrange("p h t d -> p (h t) d")
                    total = hs[:, :, :, MD:MD + 1].rearrange("p h t a -> p (h t a)")
                    n0 = nrm[:, 0, :].rearrange("p (h t) -> p h t", h=MH)
                    fin(dve.scalar_tensor_tensor(out=nrm[:, 0, :], in0=total, scalar=-1.0, in1=total, op0=ALU.mult,
                                                 op1=ALU.max), 1)
                    fin(dve.tensor_tensor(n0, n0, cols[:, 1, :, :].rearrange("p t h -> p h t"), ALU.max), 2)
                    fin(dve.tensor_scalar(nrm[:, 1, :], nrm[:, 0, :], MIX_EPS, None, ALU.add), 3)
                    fin(dve.reciprocal(nrm[:, 2, :], nrm[:, 1, :]), 4)
                    fin(dve.tensor_tensor(hw[:, :, :], hv, wide(2), ALU.mult), 5)
                    fin(dve.tensor_reduce(nrm[:, 3, :], hw[:, :, :], AX.X, ALU.add), 6)
                    fin(dve.tensor_scalar(nrm[:, 4, :], nrm[:, 3, :], 1.0 / MD, None, ALU.mult), 7)
                    fin(dve.tensor_tensor(hw[:, :, :], hw[:, :, :], wide(4), ALU.subtract), 8)
                    fin(dve.tensor_tensor(sq[:, :, :], hw[:, :, :], hw[:, :, :], ALU.mult), 9)
                    fin(dve.tensor_reduce(nrm[:, 5, :], sq[:, :, :], AX.X, ALU.add), 10)
                    fin(dve.tensor_scalar(nrm[:, 6, :], nrm[:, 5, :], 1.0 / MD, MIX_EPS, ALU.mult, ALU.add), 11)
                    dve.wait_ge(s["fin_pow"], i + 1)
                    fin(dve.tensor_tensor(hw[:, :, :], hw[:, :, :], wide(7), ALU.mult), 12)
                    for h in range(MH):
                        ins = dve.tensor_tensor(
                            hw[:, h * TPB:(h + 1) * TPB, :], hw[:, h * TPB:(h + 1) * TPB, :],
                            w_row[:, MD * h:MD * h + MD].rearrange("p (a d) -> p a d", a=1).broadcast_to([P, TPB, MD]),
                            ALU.mult)
                    fin(ins, 13)
                    for h in range(MH):
                        xv = x_all[:, ds(i * TPB, TPB), MD * h:MD * h + MD]
                        ins = dve.tensor_tensor(xv, xv, hw[:, h * TPB:(h + 1) * TPB, :], ALU.add)
                    fin(ins, 14)


def norm_and_turn(nc, c, phase, x_all, xnT_all, rows=None):
    with ExitStack() as ctx:
        sb = allocator(ctx, nc, phase)
        tmp = norm_tmp(sb)
        ps = ctx.enter_context(nc.psum_tensor(f"{phase}_ps", [P, DC, 512], F32))
        s = sems(ctx, nc, phase, "stats mv ve rstd xn turned out stored")
        FREE_AT_START = "turned stored out".split()
        with nc.Block() as block:
            @block.gpsimd
            def _(pool):
                with pool.Fori(0, B) as i:
                    norm_batch_pool(pool, s, i, tmp, c["minus_half"])

            @block.vector
            def _(dve):
                for name in FREE_AT_START:
                    dve.sem_inc(s[name], 1)
                with dve.Fori(0, B) as i:
                    def wait_free():
                        dve.wait_ge(s["turned"], i + 1)
                        if rows is not None:
                            dve.wait_ge(s["stored"], 16 * i + 1)
                    norm_batch_dve(dve, s, i, x_all, tmp, wait_free)

            @block.tensor
            def _(pe):
                with pe.Fori(0, B) as i:
                    pe.wait_ge(s["xn"], i + 1)
                    pe.wait_ge(s["out"], i + 1)
                    for k in range(DC):
                        for t in range(TPB):
                            ins = pe.transpose(ps[:, k, P * t:P * t + P], tmp["xn"][:, t, P * k:P * k + P],
                                               c["ident"][:, :])
                    ins.then_inc(s["turned"], 1)

            @block.scalar
            def _(act):
                with act.Fori(0, B) as i:
                    act.wait_ge(s["turned"], i + 2)
                    for k in range(DC):
                        ins = act.copy(xnT_all[:, k, ds(i * S, S)], ps[:, k, :])
                    ins.then_inc(s["out"], 1)

            if rows is not None:
                @block.sync
                def _(sp):
                    rv = rows.rearrange("(b t p) d -> b p t d", p=P, t=TPB)
                    with sp.Fori(0, B) as i:
                        sp.wait_ge(s["xn"], i + 1)
                        sp.dma_start(rv[ds(i, 1), :, :, 0:D].rearrange("a p t d -> p (a t) d"),
                                     tmp["xn"][:, :, :]).then_inc(s["stored"], 16)
                    sp.wait_ge(s["stored"], 16 * B + 1)


def mlp(nc, c, x_all, xnT_all, w1, b1, w2, b2):
    with ExitStack() as ctx:
        sb = allocator(ctx, nc, "mlp")
        w1_s = sb("w1", [P, DC, F], F32)
        w2_s = sb("w2", [P, FC, D], F32)
        b1_s = sb("b1", [P, FC], F32)
        b2_s = sb("b2", [P, D], F32)
        hT = sb("hT", [P, FC, S], F32)
        ps = ctx.enter_context(nc.psum_tensor("mlp_ps", [P, 8, 512], F32))
        s = sems(ctx, nc, "mlp", "w h_ps hT y_ps y b")
        FREE_AT_START = "y y_ps".split()
        with nc.Block() as block:
            @block.sync
            def _(sp):
                sp.dma_start(w1_s[:, :, :], w1.rearrange("(c p) f -> p c f", p=P)).then_inc(s["w"], 16)
                sp.dma_start(w2_s[:, :, :], w2.rearrange("(c p) d -> p c d", p=P)).then_inc(s["w"], 16)
                sp.dma_start(b1_s[:, :], b1.rearrange("(c p) -> p c", p=P), allow_slow_non_contiguous=True).then_inc(s["w"], 16)
                sp.dma_start(b2_s[:, :], b2.rearrange("(a d) -> a d", a=1).broadcast_to([P, D])).then_inc(s["w"], 16)

            @block.tensor
            def _(pe):
                pe.wait_ge(s["w"], 64)
                with pe.Fori(0, B) as i:
                    for f in range(FC):
                        if f >= 4:
                            pe.wait_ge(s["hT"], FC * i + f - 3)
                        for k in range(DC):
                            ins = pe.matmul(ps[:, f % 4, :], w1_s[:, k, P * f:P * f + P], xnT_all[:, k, ds(i * S, S)],
                                            start=k == 0, stop=k == DC - 1)
                        ins.then_inc(s["h_ps"], 1)
                    pe.wait_ge(s["y"], TPB * i + 1)
                    pe.wait_ge(s["hT"], FC * i + FC)
                    for t in range(TPB):
                        for f in range(FC):
                            ins = pe.matmul(ps[:, 4 + t, 0:D], hT[:, f, P * t:P * t + P], w2_s[:, f, :],
                                            start=f == 0, stop=f == FC - 1)
                        ins.then_inc(s["y_ps"], 1)

            @block.scalar
            def _(act):
                act.wait_ge(s["w"], 64)
                with act.Fori(0, B) as i:
                    act.wait_ge(s["y_ps"], TPB * i + 1)
                    for f in range(FC):
                        act.wait_ge(s["h_ps"], FC * i + f + 1)
                        act.activation(hT[:, f, :], ps[:, f % 4, :], ACT.Gelu, bias=b1_s[:, f:f + 1]).then_inc(s["hT"], 1)

            @block.vector
            def _(dve):
                for name in FREE_AT_START:
                    dve.sem_inc(s[name], 1)
                dve.wait_ge(s["w"], 64)
                with dve.Fori(0, B) as i:
                    for t in range(TPB):
                        dve.wait_ge(s["y_ps"], TPB * i + t + 2)
                        xv = x_all[:, ds(i * TPB + t, 1), :].rearrange("p a d -> p (a d)")
                        dve.tensor_tensor(xv, ps[:, 4 + t, 0:D], xv, ALU.add).then_inc(s["y"], 1)
                    dve.wait_ge(s["y"], TPB * i + TPB + 1)
                    for t in range(TPB):
                        xv = x_all[:, ds(i * TPB + t, 1), :].rearrange("p a d -> p (a d)")
                        ins = dve.tensor_tensor(xv, xv, b2_s[:, :], ALU.add)
                    ins.then_inc(s["b"], 1)


def attention(nc, c, x_all, xnT_all, ctxT_all, Wq, Wk, Wv, Wo, Bq, Bk, Bv, Bo):
    U = HP * B
    NBL = 2 * TPB
    F32R = mybir.dt.float32r
    with ExitStack() as ctx:
        sb = allocator(ctx, nc, "at")
        w_next = sb("w_next", [P, 3, DC, P], F32)
        b_next = sb("b_next", [P, 3], F32)
        w_s = sb("w", [P, 3, DC, P], F32)
        b_s = sb("b", [P, 3], F32)
        wo_s = sb("wo", [P, HP, D], F32)
        bo_s = sb("bo", [P, D], F32)
        q2 = sb("q2", [P, 2, 2, S], F32R)
        k_own = sb("k_own", [P, 2, S], F32R)
        k2 = sb("k2", [P, 2, 2, 2, S], F32R)
        vT = sb("vT", [P, S], F32)
        V = sb("V", [P, 2, TPB, P], F32)
        Pr = sb("Pr", [P, 4, S], F32)
        PT = sb("PT", [P, 2, 2, TPB, S], F32)
        oT = sb("oT", [P, S], F32)
        nmax = sb("nmax", [P, 4], F32)
        rsum = sb("rsum", [P, 4], F32)
        rinv = sb("rinv", [P, 4], F32)
        ps = ctx.enter_context(nc.psum_tensor("at_ps", [P, 8, 512], F32))
        S_BANK, T_BANK, A_BANK, O_BANK, Y_BANK = 0, 2, 4, 6, 7
        s = sems(ctx, nc, "at", "w wo bo scaled q_ps qh ql k_ps kh kl k2 v_ps vT vturned V s_ps nmax exp rinv pn t_ps "
                 "pt_v pt_a pv oT y_ps x bo_add")
        w_dram = [W.rearrange("(c p) n -> p c n", p=P) for W in (Wq, Wk, Wv)]
        b_dram = [b.rearrange("(a p) -> p a", p=P) for b in (Bq, Bk, Bv)]
        wo_dram = Wo.rearrange("(a p) d -> p a d", p=P)
        LOADS = 6
        ON_ACT = (4, 5)
        BY_ACT = [sum(j in ON_ACT for j in range(n)) for n in range(NBL + 1)]
        BY_DVE = [n - BY_ACT[n] for n in range(NBL + 1)]

        def every_unit(eng, body, begin_pair=None):
            body(0, 0, first=True)
            with eng.Fori(0, HP - 1) as hp:
                if begin_pair:
                    begin_pair(hp)
                with eng.Fori(0, B // 2 - 1) as pair:
                    body(hp * B + pair * 2 + 1, 1)
                    body(hp * B + pair * 2 + 2, 0)
                body(hp * B + (B - 1), 1, switch=hp)
                body(hp * B + B, 0)
            with eng.Fori(0, B // 2 - 1) as pair:
                body(pair * 2 + (U - B + 1), 1)
                body(pair * 2 + (U - B + 2), 0)
            body(U - 1, 1, last=True)
            body(U, 0, drain=True)

        def wait_turned_copies(eng, u, n):
            eng.wait_ge(s["pt_v"], u * BY_DVE[NBL] + BY_DVE[n])
            if BY_ACT[n]:
                eng.wait_ge(s["pt_a"], u * BY_ACT[NBL] + BY_ACT[n])

        with nc.Block() as block:
            @block.sync
            def _(sp):
                def load_qkv(hp):
                    for k in range(3):
                        sp.dma_start(w_next[:, k, :, :], w_dram[k][:, :, ds(hp * P, P)]).then_inc(s["w"], 16)
                        sp.dma_start(b_next[:, k:k + 1], b_dram[k][:, ds(hp, 1)], allow_slow_non_contiguous=True
                                     ).then_inc(s["w"], 16)

                def double_keys(u, par):
                    sp.wait_ge(s["kh"], u + 1)
                    sp.wait_ge(s["kl"], u + 1)
                    for h in range(2):
                        for half in range(2):
                            sp.dma_start(k2[AD * half:AD * half + AD, par, h, :, :].bitcast(F32),
                                         k_own[AD * h:AD * h + AD, :, :].bitcast(F32)).then_inc(s["k2"], 16)

                load_qkv(0)
                sp.dma_start(wo_s[:, :, :], wo_dram).then_inc(s["wo"], 16)
                sp.dma_start(bo_s[:, :], Bo.rearrange("(a d) -> a d", a=1).broadcast_to([P, D])).then_inc(s["bo"], 16)
                double_keys(0, 0)

                def body(u, par, first=False, last=False, switch=None, drain=False):
                    if drain or last:
                        return
                    double_keys(u + 1, 1 - par)

                def begin_pair(hp):
                    sp.wait_ge(s["scaled"], hp + 1)
                    load_qkv(hp + 1)
                every_unit(sp, body, begin_pair)

            @block.tensor
            def _(pe):
                def project(u, k):
                    src = xnT_all if k == 0 else ctxT_all
                    b = u % B
                    if k == 0:
                        pe.wait_ge(s["scaled"], u // B + 1)
                        pe.wait_ge(s["vT"], u)
                    elif k == 1:
                        pe.wait_ge(s["V"], u)
                    else:
                        pe.wait_ge(s["ql"], u + 1)
                    for d in range(DC):
                        ins = pe.matmul(ps[:, A_BANK + k % 2, :], w_s[:, k, d, :], src[:, d, ds(b * S, S)],
                                        start=d == 0, stop=d == DC - 1)
                    ins.then_inc(s[("q_ps", "k_ps", "v_ps")[k]], 1)

                def turn_values(u):
                    pe.wait_ge(s["vT"], u + 1)
                    pe.wait_ge(s["kl"], u + 1)
                    for t in range(TPB):
                        ins = pe.transpose(ps[:, A_BANK + 1, P * t:P * t + P], vT[:, P * t:P * t + P], c["ident"][:, :])
                    ins.then_inc(s["vturned"], 1)

                def score(u, par, j, first):
                    if j >= 2 or not first:
                        pe.wait_ge(s["exp"], NBL * u + j - 1)
                    if j == 0:
                        pe.wait_ge(s["ql"], u + 1)
                        pe.wait_ge(s["k2"], 64 * (u + 1))
                    h, q = j // TPB, P * (j % TPB)
                    for part in range(2):
                        ins = pe.matmul(ps[:, S_BANK + j % 2, :], q2[:, par, h, q:q + P], k2[:, par, h, part, :],
                                        start=part == 0, stop=part == 1)
                    ins.then_inc(s["s_ps"], 1)

                def turn(u, j, first=False):
                    pe.wait_ge(s["pn"], NBL * u + j + 1)
                    if j >= 2:
                        wait_turned_copies(pe, u, j - 1)
                    elif not first:
                        wait_turned_copies(pe, u - 1, NBL - 1 + j)
                    for t in range(TPB):
                        ins = pe.transpose(ps[:, T_BANK + j % 2, P * t:P * t + P], Pr[:, j % 4, P * t:P * t + P],
                                           c["ident"][:, :])
                    ins.then_inc(s["t_ps"], 1)

                def weigh_values(u, par, part):
                    if part == 0:
                        wait_turned_copies(pe, u, NBL)
                        pe.wait_ge(s["V"], u + 1)
                    for t in (2 * part, 2 * part + 1):
                        for h in range(2):
                            ins = pe.matmul(ps[AD * h:AD * h + AD, O_BANK, :], V[:, par, t, AD * h:AD * h + AD],
                                            PT[:, par, h, t, :], start=t == 0, stop=t == TPB - 1)
                    if part == 1:
                        ins.then_inc(s["pv"], 1)

                def output(u, half):
                    if half == 0:
                        pe.wait_ge(s["oT"], u + 1)
                        pe.wait_ge(s["wo"], 16)
                    for t in (2 * half, 2 * half + 1):
                        ins = pe.matmul(ps[:, Y_BANK - half, D * (t % 2):D * (t % 2) + D], oT[:, P * t:P * t + P],
                                        wo_s[:, ds(u // B, 1), :].rearrange("p a d -> p (a d)"), start=True, stop=True)
                    ins.then_inc(s["y_ps"], 1)

                def body(u, par, first=False, last=False, switch=None, drain=False):
                    for j in range(NBL):
                        if not drain:
                            score(u, par, j, first)
                        if j >= 2 and not drain:
                            turn(u, j - 2, first)
                        if j < 2 and not first:
                            turn(u - 1, NBL - 2 + j)
                        if j < 3 and not last and not drain:
                            project(u + 1, j)
                        if j in (3, 4) and not first:
                            weigh_values(u - 1, 1 - par, j - 3)
                        if j == 5 and not last and not drain:
                            turn_values(u + 1)
                        if j in (6, 7) and not first:
                            output(u - 1, j - 6)

                for k in range(3):
                    project(0, k)
                turn_values(0)
                every_unit(pe, body)

            @block.scalar
            def _(act):
                def queries(u, par):
                    act.wait_ge(s["q_ps"], u + 1)
                    for h in range(2):
                        own = slice(AD * h, AD * h + AD)
                        ins = act.activation(q2[own, par, h, :], ps[own, A_BANK, :], ACT.Identity, bias=b_s[own, 0:1])
                    ins.then_inc(s["qh"], 1)

                def keys(u):
                    act.wait_ge(s["k_ps"], u + 1)
                    if not (isinstance(u, int) and u == 0):
                        act.wait_ge(s["k2"], 64 * u)
                    act.activation(k_own[:, 0, :], ps[:, A_BANK + 1, :], ACT.Identity, bias=b_s[:, 1:2]
                                   ).then_inc(s["kh"], 1)

                def values(u):
                    act.wait_ge(s["v_ps"], u + 1)
                    act.wait_ge(s["vturned"], u)
                    act.activation(vT[:, :], ps[:, A_BANK, :], ACT.Identity, bias=b_s[:, 2:3]).then_inc(s["vT"], 1)

                def body(u, par, first=False, last=False, switch=None, drain=False):
                    ahead = not last and not drain
                    for j in range(NBL):
                        if not drain:
                            act.wait_ge(s["nmax"], NBL * u + j + 1)
                            if not first or j > 3:
                                act.wait_ge(s["t_ps"], NBL * u + j - 3)
                            act.activation(Pr[:, j % 4, :], ps[:, S_BANK + j % 2, :], ACT.Exp,
                                           bias=nmax[:, j % 4:j % 4 + 1], accum_out=rsum[:, j % 4:j % 4 + 1]
                                           ).then_inc(s["exp"], 1)
                        if j == 0 and ahead:
                            queries(u + 1, 1 - par)
                        if j == 1 and ahead:
                            keys(u + 1)
                        if j == 2 and ahead:
                            values(u + 1)
                        if j == 5 and not first:
                            act.wait_ge(s["pv"], u)
                            act.copy(oT[:, :], ps[:, O_BANK, :]).then_inc(s["oT"], 1)
                        if not drain and j - 2 in ON_ACT:
                            act.wait_ge(s["t_ps"], NBL * u + j - 1)
                            q = P * ((j - 2) % TPB)
                            act.copy(PT[:, par, (j - 2) // TPB, :, q:q + P],
                                     ps[:, T_BANK + j % 2, :].rearrange("p (t q) -> p t q", t=TPB)
                                     ).then_inc(s["pt_a"], 1)

                act.wait_ge(s["scaled"], 1)
                queries(0, 0)
                keys(0)
                values(0)
                every_unit(act, body)

            @block.gpsimd
            def _(pool):
                def body(u, par, first=False, last=False, switch=None, drain=False):
                    if drain:
                        return
                    for j in range(NBL):
                        wait_apart(pool, s["rinv"], NBL * u + j + 1)
                        pool.tensor_scalar(Pr[:, j % 4, :], Pr[:, j % 4, :], rinv[:, j % 4:j % 4 + 1], 1.0,
                                           ALU.mult, ALU.mult).then_inc(s["pn"], 1)
                every_unit(pool, body)

            @block.vector
            def _(dve):
                def queries(u, par):
                    dve.wait_ge(s["qh"], u + 1)
                    for h in range(2):
                        own, other = slice(AD * h, AD * h + AD), slice(AD - AD * h, 2 * AD - AD * h)
                        ins = dve.scalar_tensor_tensor(out=q2[other, par, h, :], in0=ps[own, A_BANK, :],
                                                       scalar=b_s[own, 0:1], in1=q2[own, par, h, :], op0=ALU.add,
                                                       op1=ALU.subtract)
                    ins.then_inc(s["ql"], 1)

                def keys(u):
                    dve.wait_ge(s["kh"], u + 1)
                    dve.scalar_tensor_tensor(out=k_own[:, 1, :], in0=ps[:, A_BANK + 1, :], scalar=b_s[:, 1:2],
                                             in1=k_own[:, 0, :], op0=ALU.add, op1=ALU.subtract).then_inc(s["kl"], 1)

                def values(u, par):
                    dve.wait_ge(s["vturned"], u + 1)
                    dve.tensor_copy(V[:, par, :, :], ps[:, A_BANK + 1, :].rearrange("p (t d) -> p t d", t=TPB)
                                    ).then_inc(s["V"], 1)

                def row_max(u, j):
                    dve.wait_ge(s["s_ps"], NBL * u + j + 1)
                    dve.tensor_reduce(nmax[:, j % 4:j % 4 + 1], ps[:, S_BANK + j % 2, :], AX.X, ALU.max, negate=True
                                      ).then_inc(s["nmax"], 1)

                def row_sum(u, j):
                    dve.wait_ge(s["exp"], NBL * u + j + 1)
                    dve.reciprocal(rinv[:, j % 4:j % 4 + 1], rsum[:, j % 4:j % 4 + 1]).then_inc(s["rinv"], 1)

                def keep(u, par, j):
                    if j in ON_ACT:
                        return
                    dve.wait_ge(s["t_ps"], NBL * u + j + 1)
                    q = P * (j % TPB)
                    dve.tensor_copy(PT[:, par, j // TPB, :, q:q + P],
                                    ps[:, T_BANK + j % 2, :].rearrange("p (t q) -> p t q", t=TPB)).then_inc(s["pt_v"], 1)

                def add_out(u, half):
                    dve.wait_ge(s["y_ps"], 2 * u + half + 1)
                    xv = x_all[:, ds((u % B) * TPB + 2 * half, 2), :].rearrange("p t d -> p (t d)")
                    dve.tensor_tensor(xv, ps[:, Y_BANK - half, :], xv, ALU.add).then_inc(s["x"], 1)

                def switch_weights(hp):
                    dve.wait_ge(s["w"], 16 * LOADS * (hp + 1))
                    dve.tensor_scalar(b_s[:, 0:1], b_next[:, 0:1], AD ** -0.5, None, ALU.mult)
                    dve.tensor_copy(b_s[:, 1:3], b_next[:, 1:3])
                    dve.tensor_scalar(w_s[:, 0, :, :], w_next[:, 0, :, :], AD ** -0.5, None, ALU.mult)
                    dve.tensor_copy(w_s[:, 1:3, :, :], w_next[:, 1:3, :, :]).then_inc(s["scaled"], 1)

                def body(u, par, first=False, last=False, switch=None, drain=False):
                    ahead = not last and not drain
                    if switch is not None:
                        dve.wait_ge(s["vT"], u + 1)
                        switch_weights(switch + 1)
                    for j in range(NBL):
                        if not drain:
                            row_max(u, j)
                            if j >= 1:
                                row_sum(u, j - 1)
                        if j >= 2 and not drain:
                            keep(u, par, j - 2)
                        if j < 2 and not first:
                            keep(u - 1, 1 - par, NBL - 2 + j)
                        if j == 1 and ahead:
                            queries(u + 1, 1 - par)
                        if j == 2 and ahead:
                            keys(u + 1)
                        if j == 6 and ahead:
                            values(u + 1, 1 - par)
                        if j == 7:
                            if not drain:
                                row_sum(u, j)
                            if not first:
                                add_out(u - 1, 0)
                                add_out(u - 1, 1)

                switch_weights(0)
                dve.wait_ge(s["bo"], 16)
                dve.wait_ge(s["scaled"], 1)
                queries(0, 0)
                keys(0)
                values(0, 0)
                every_unit(dve, body)
                dve.wait_ge(s["x"], 2 * U)
                with dve.Fori(0, NT) as t:
                    xv = x_all[:, ds(t, 1), :].rearrange("p a d -> p (a d)")
                    dve.tensor_tensor(xv, xv, bo_s[:, :], ALU.add).then_inc(s["bo_add"], 1)


def router(nc, c, xnT_all, gate_w, rows, prob, final, idx_get, idx_put, valid):
    with ExitStack() as ctx:
        sb = allocator(ctx, nc, "ro")
        gw = sb("gw", [E, D], F32)
        gT = sb("gT", [P, DC, E], F32)
        lT = sb("lT", [E, S], F32)
        lg = sb("lg", [P, NT, E], F32)
        red = sb("red", [P, 3, NT], F32)
        pair_a = sb("pair_a", [P, NT, E, E], F32)
        pair_b = sb("pair_b", [P, NT, E, E], F32)
        before = sb("before", [P, NT, E], F32)
        rank = sb("rank", [P, NT, E], F32)
        sel = sb("sel", [P, NT, E], F32)
        key = sb("key", [P, NT, E], F32)
        t1 = sb("t1", [P, NT, E], F32)
        t2 = sb("t2", [P, NT, E], F32)
        cnt = sb("cnt", [P, E], F32)
        cnt_b = sb("cnt_b", [P, E], BF16)
        T = sb("T", [P, E], F32)
        cand = sb("cand", [P, E], F32)
        step = sb("step", [P, E], F32)
        mask_b = sb("mask_b", [P, NT, E], BF16)
        tot = sb("tot", [P, E, NT], F32)
        offs = sb("offs", [P, E, NT + 1], F32)
        pos = sb("pos", [P, NT, E], F32)
        need = sb("need", [P, E], F32)
        chunk = sb("chunk", [P, NT, E], F32)
        slot = sb("slot", [P, NT, E], F32)
        is_chunk = sb("is_chunk", [P, NT, CT], F32)
        onehot = sb("onehot", [P, 2, NT, P], BF16)
        rhs = sb("rhs", [P, 2, NT, 3, CT], BF16)
        got = sb("got", [P, 3, CT], F32)
        tok = sb("tok", [P, CT], F32)
        away = sb("away", [P, CT], F32)
        ps = ctx.enter_context(nc.psum_tensor("ro_ps", [P, 4, 512], F32))
        s = sems(ctx, nc, "ro", "gw gT_ps gT l_ps lT lt_ps lg v ones_mm pre_mm prob exp slot_ps built")
        NE = NT * E

        def flat(a):
            return a[:, :, :].rearrange("p t e -> p (t e)")

        def over_e(a):
            return a.rearrange("p (t a) -> p t a", a=1).broadcast_to([P, NT, E])

        def over_t(a):
            return a.rearrange("p (a e) -> p a e", a=1).broadcast_to([P, NT, E])

        STEPS = list(range(2, -25, -1))
        FREE_AT_START = "lT lg".split()
        with nc.Block() as block:
            @block.sync
            def _(sp):
                sp.dma_start(gw[:, :], gate_w).then_inc(s["gw"], 16)
                sp.wait_ge(s["prob"], 1)
                with nc.allow_non_contiguous_dma("8 probabilities per row"):
                    sp.dma_start(rows.rearrange("(t p) d -> p t d", p=P)[:, :, D:ROW], prob[:, :, :]).then_inc(s["gw"], 16)
                sp.wait_ge(s["gw"], 32)

            @block.scalar
            def _(act):
                act.wait_ge(s["v"], 2)
                act.activation(flat(lg), flat(lg), ACT.Exp).then_inc(s["exp"], 1)

            @block.tensor
            def _(pe):
                pe.wait_ge(s["gw"], 16)
                for k in range(DC):
                    ins = pe.transpose(ps[:, 0, E * k:E * k + E], gw[:, P * k:P * k + P], c["ident"][0:E, 0:E])
                ins.then_inc(s["gT_ps"], 1)
                pe.wait_ge(s["gT"], 1)
                with pe.Fori(0, B) as i:
                    pe.wait_ge(s["lT"], i + 1)
                    for k in range(DC):
                        ins = pe.matmul(ps[0:E, 1, :], gT[:, k, :], xnT_all[:, k, ds(i * S, S)], start=k == 0,
                                        stop=k == DC - 1)
                    ins.then_inc(s["l_ps"], 1)
                    pe.wait_ge(s["lT"], i + 2)
                    wait_apart(pe, s["lg"], i + 1)
                    for t in range(TPB):
                        ins = pe.transpose(ps[:, 2, t * E:t * E + E], lT[:, P * t:P * t + P],
                                           c["ident"][0:E, 0:E])
                    ins.then_inc(s["lt_ps"], 1)
                for n in range(len(STEPS) + 1):
                    pe.wait_ge(s["built"], n + 1)
                    pe.matmul(ps[:, 0, 0:E], c["ones_bf"][:, :], cnt_b[:, :], start=True, stop=True).then_inc(s["ones_mm"], 1)
                for n in range(2):
                    pe.wait_ge(s["built"], len(STEPS) + 2 + n)
                    pe.matmul(ps[:, 1, 0:NE], c["lower_bf"][:, :], flat(mask_b), start=True, stop=True)
                    pe.matmul(ps[:, 3, 0:NE], c["ones_bf"][:, :], flat(mask_b), start=True, stop=True
                              ).then_inc(s["pre_mm"], 1)
                for e in range(E):
                    pe.wait_ge(s["built"], len(STEPS) + 4 + e)
                    for t in range(NT):
                        ins = pe.matmul(ps[:, e % 2, 0:3 * CT], onehot[:, e % 2, t, :],
                                        rhs[:, e % 2, t, :, :].rearrange("p a c -> p (a c)"), start=t == 0,
                                        stop=t == NT - 1)
                    ins.then_inc(s["slot_ps"], 1)

            @block.vector
            def _(dve):
                for name in FREE_AT_START:
                    dve.sem_inc(s[name], 1)
                n = [0]

                def v(ins):
                    n[0] += 1
                    ins.then_inc(s["v"], 1)
                    dve.wait_ge(s["v"], n[0])

                dve.wait_ge(s["gT_ps"], 1)
                dve.tensor_copy(gT[:, :, :], ps[:, 0, 0:DC * E].rearrange("p (k e) -> p k e", k=DC)).then_inc(s["gT"], 1)
                with dve.Fori(0, B) as i:
                    dve.wait_ge(s["l_ps"], i + 1)
                    dve.tensor_copy(lT[:, :], ps[0:E, 1, :]).then_inc(s["lT"], 1)
                    dve.wait_ge(s["lt_ps"], i + 1)
                    dve.tensor_copy(lg[:, ds(i * TPB, TPB), :],
                                    ps[:, 2, 0:TPB * E].rearrange("p (t e) -> p t e", e=E)).then_inc(s["lg"], 1)
                dve.wait_ge(s["lg"], B + 1)
                v(dve.tensor_reduce(red[:, 0, :], lg[:, :, :], AX.X, ALU.max))
                v(dve.tensor_tensor(lg[:, :, :], lg[:, :, :], over_e(red[:, 0, :]), ALU.subtract))
                dve.wait_ge(s["exp"], 1)
                v(dve.tensor_reduce(red[:, 1, :], lg[:, :, :], AX.X, ALU.add))
                v(dve.reciprocal(red[:, 2, :], red[:, 1, :]))
                dve.tensor_tensor(prob[:, :, :], lg[:, :, :], over_e(red[:, 2, :]), ALU.mult).then_inc(s["prob"], 1)
                dve.wait_ge(s["prob"], 1)
                pj = prob[:, :, :].rearrange("p t (a e) -> p t a e", a=1).broadcast_to([P, NT, E, E])
                pe_ = prob[:, :, :].rearrange("p t (e a) -> p t e a", a=1).broadcast_to([P, NT, E, E])
                tie = c["earlier"][:, :, :].rearrange("p (a e) j -> p a e j", a=1).broadcast_to([P, NT, E, E])
                v(dve.tensor_tensor(pair_a[:, :, :, :], pj, pe_, ALU.is_equal))
                v(dve.tensor_tensor(pair_a[:, :, :, :], pair_a[:, :, :, :], tie, ALU.mult))
                v(dve.tensor_tensor(pair_b[:, :, :, :], pj, pe_, ALU.is_gt))
                v(dve.tensor_tensor(pair_a[:, :, :, :], pair_a[:, :, :, :], pair_b[:, :, :, :], ALU.add))
                v(dve.tensor_reduce(rank[:, :, :], pair_a[:, :, :, :], AX.X, ALU.add))
                v(dve.tensor_tensor(pair_a[:, :, :, :], pair_a[:, :, :, :], pj, ALU.mult))
                v(dve.tensor_reduce(before[:, :, :], pair_a[:, :, :, :], AX.X, ALU.add))
                v(dve.tensor_scalar(flat(sel), flat(before), 0.9, None, ALU.is_lt))
                v(dve.tensor_scalar(flat(rank), flat(rank), 1.0, None, ALU.add))
                v(dve.tensor_tensor(key[:, :, :], rank[:, :, :], prob[:, :, :], ALU.subtract))
                v(dve.tensor_tensor(key[:, :, :], key[:, :, :], sel[:, :, :], ALU.mult))
                v(dve.tensor_scalar(flat(t1), flat(sel), -FAR, FAR, ALU.mult, ALU.add))
                v(dve.tensor_tensor(key[:, :, :], key[:, :, :], t1[:, :, :], ALU.add))
                v(dve.memset(T[:, :], 0.0))

                def count(which):
                    v(dve.tensor_tensor(t2[:, :, :], key[:, :, :], over_t(which), ALU.is_lt))
                    v(dve.tensor_reduce(cnt[:, :], t2[:, :, :].rearrange("p t e -> p e t"), AX.X, ALU.add))
                    dve.tensor_copy(cnt_b[:, :], cnt[:, :]).then_inc(s["built"], 1)

                for k, bit in enumerate(STEPS):
                    v(dve.tensor_scalar(cand[:, :], T[:, :], 2.0 ** bit, None, ALU.add))
                    count(cand[:, :])
                    dve.wait_ge(s["ones_mm"], k + 1)
                    v(dve.tensor_scalar(step[:, :], ps[:, 0, 0:E], float(CAP), 2.0 ** bit, ALU.is_lt, ALU.mult))
                    v(dve.tensor_tensor(T[:, :], T[:, :], step[:, :], ALU.add))
                count(T[:, :])
                dve.wait_ge(s["ones_mm"], len(STEPS) + 1)
                v(dve.tensor_scalar(need[:, :], ps[:, 0, 0:E], -1.0, float(CAP), ALU.mult, ALU.add))

                def ranks(k):
                    dve.wait_ge(s["pre_mm"], k + 1)
                    v(dve.tensor_copy(tot[:, :, :], ps[:, 3, 0:NE].rearrange("p (t e) -> p e t", e=E)))
                    for e in range(E):
                        ins = dve.tensor_tensor_scan(offs[:, e, 1:NT + 1], c["ones_row"][:, 0:NT], tot[:, e, :], 0.0,
                                                     ALU.mult, ALU.add)
                    v(ins)
                    v(dve.tensor_tensor(pos[:, :, :], ps[:, 1, 0:NE].rearrange("p (t e) -> p t e", e=E),
                                        offs[:, :, 0:NT].rearrange("p e t -> p t e"), ALU.add))

                v(dve.memset(offs[:, :, :], 0.0))
                v(dve.tensor_tensor(t1[:, :, :], key[:, :, :], over_t(T[:, :]), ALU.is_equal))
                dve.tensor_copy(flat(mask_b), flat(t1)).then_inc(s["built"], 1)
                ranks(0)
                v(dve.tensor_tensor(pos[:, :, :], pos[:, :, :], over_t(need[:, :]), ALU.is_lt))
                v(dve.tensor_tensor(t1[:, :, :], t1[:, :, :], pos[:, :, :], ALU.mult))
                v(dve.tensor_tensor(t1[:, :, :], t1[:, :, :], t2[:, :, :], ALU.add))
                v(dve.tensor_tensor(final[:, :, :], t1[:, :, :], sel[:, :, :], ALU.mult))
                dve.tensor_copy(flat(mask_b), flat(final)).then_inc(s["built"], 1)
                ranks(1)
                v(dve.tensor_scalar(flat(chunk), flat(pos), float(P), None, ALU.is_ge))
                for k in range(2, CT):
                    v(dve.tensor_scalar(flat(t1), flat(pos), float(P * k), None, ALU.is_ge))
                    v(dve.tensor_tensor(chunk[:, :, :], chunk[:, :, :], t1[:, :, :], ALU.add))
                v(dve.scalar_tensor_tensor(out=slot[:, :, :], in0=chunk[:, :, :], scalar=-float(P), in1=pos[:, :, :],
                                           op0=ALU.mult, op1=ALU.add))
                v(dve.tensor_scalar(flat(slot), flat(slot), 1.0, None, ALU.add))
                v(dve.tensor_tensor(slot[:, :, :], slot[:, :, :], final[:, :, :], ALU.mult))
                v(dve.tensor_scalar(flat(slot), flat(slot), -1.0, None, ALU.add))
                v(dve.tensor_scalar(c["spare"][:, :], c["part"][:, :], float(N), None, ALU.add))

                def build(e):
                    oh = onehot[:, e % 2, :, :]
                    v(dve.tensor_tensor(oh, c["slot"][:, :].rearrange("p (a q) -> p a q", a=1).broadcast_to([P, NT, P]),
                                        slot[:, :, e:e + 1].broadcast_to([P, NT, P]), ALU.is_equal))
                    v(dve.tensor_tensor(is_chunk[:, :, :],
                                        c["slot"][:, 0:CT].rearrange("p (a q) -> p a q", a=1).broadcast_to([P, NT, CT]),
                                        chunk[:, :, e:e + 1].broadcast_to([P, NT, CT]), ALU.is_equal))
                    v(dve.tensor_tensor(rhs[:, e % 2, :, 0, :], is_chunk[:, :, :],
                                        c["tile_no"][:, :].rearrange("p (t a) -> p t a", a=1).broadcast_to([P, NT, CT]),
                                        ALU.mult))
                    v(dve.tensor_scalar(rhs[:, e % 2, :, 1, :], is_chunk[:, :, :], c["part"][:, 0:1], None, ALU.mult))
                    dve.tensor_copy(rhs[:, e % 2, :, 2, :], is_chunk[:, :, :]).then_inc(s["built"], 1)

                def read(e):
                    dve.wait_ge(s["slot_ps"], e + 1)
                    v(dve.tensor_copy(got[:, :, :], ps[:, e % 2, 0:3 * CT].rearrange("p (a k) -> p a k", a=3)))
                    v(dve.scalar_tensor_tensor(out=tok[:, :], in0=got[:, 0, :], scalar=float(P), in1=got[:, 1, :],
                                               op0=ALU.mult, op1=ALU.add))
                    v(dve.tensor_copy(valid[:, e, :], got[:, 2, :]))
                    v(dve.tensor_copy(idx_get[:, e, :], tok[:, :]))
                    v(dve.tensor_scalar(away[:, :], got[:, 2, :], -1.0, 1.0, ALU.mult, ALU.add))
                    v(dve.scalar_tensor_tensor(out=idx_put[:, e, :], in0=away[:, :], scalar=c["spare"][:, 0:1],
                                               in1=tok[:, :], op0=ALU.mult, op1=ALU.add))

                for e in range(E + 1):
                    if e < E:
                        build(e)
                    if e:
                        read(e - 1)


def experts(nc, c, rows, ysum, w1, w2, idx_get, idx_put, valid):
    with ExitStack() as ctx:
        sb = allocator(ctx, nc, "ex")
        w1_in = sb("w1_in", [P, EF // P, D], F32)
        w2_in = sb("w2_in", [P, DC, EF], F32)
        w1T = sb("w1T", [P, DC, EF], F32)
        w2T = sb("w2T", [P, EF // P, D], F32)
        ix = sb("ix", [P, 2, CT], I32)
        vl = sb("vl", [P, CT], F32)
        xg = sb("xg", [P, CT, ROW], F32)
        sc = sb("sc", [P, CT], F32)
        xT = sb("xT", [P, DC, CAP], F32)
        hT = sb("hT", [P, EF // P, CAP], F32)
        y = sb("y", [P, CT, D], F32)
        ps = ctx.enter_context(nc.psum_tensor("ex_ps", [P, 8, 512], F32))
        s = sems(ctx, nc, "ex", "w ix got w_ps wT x_ps xT sc sv h_ps hT y_ps y put landed")
        EC = EF // P
        FREE_AT_START = "w_ps landed y_ps".split()
        with nc.Block() as block:
            @block.sync
            def _(sp):
                with sp.Fori(0, E) as e:
                    sp.wait_ge(s["w_ps"], 2 * e + 1)
                    sp.dma_start(w1_in[:, :, :], w1[ds(e, 1)].rearrange("a (c p) d -> p (a c) d", p=P)).then_inc(s["w"], 16)
                    sp.dma_start(w2_in[:, :, :], w2[ds(e, 1)].rearrange("a (c p) f -> p (a c) f", p=P)).then_inc(s["w"], 16)

            @block.gpsimd
            def _(pool):
                with pool.Fori(0, E) as e:
                    wait_apart(pool, s["ix"], e + 1)
                    for t in range(CT):
                        pool.indirect_dma_start(
                            out=xg[:, t, :], out_offset=None, in_=rows,
                            in_offset=bass.IndirectOffsetOnAxis(ap=ix[:, 0, t:t + 1], axis=0)).then_inc(s["got"], 16)
                    wait_apart(pool, s["y"], e + 1)
                    for t in range(CT):
                        pool.indirect_dma_start(
                            out=ysum, out_offset=bass.IndirectOffsetOnAxis(ap=ix[:, 1, t:t + 1], axis=0),
                            in_=y[:, t, :], in_offset=None, compute_op=ALU.add).then_inc(s["put"], 16)
                    wait_apart(pool, s["put"], 16 * CT * (e + 1))
                    pool.sem_inc(s["landed"], 1)

            @block.tensor
            def _(pe):
                with pe.Fori(0, E) as e:
                    pe.wait_ge(s["w"], 32 * e + 32)
                    for k in range(DC):
                        for f in range(EC):
                            ins = pe.transpose(ps[:, 0, (k * EC + f) * P:(k * EC + f + 1) * P],
                                               w1_in[:, f, P * k:P * k + P], c["ident"][:, :])
                    ins.then_inc(s["w_ps"], 1)
                    for f in range(EC):
                        for k in range(DC):
                            ins = pe.transpose(ps[:, 1, (f * DC + k) * P:(f * DC + k + 1) * P],
                                               w2_in[:, k, P * f:P * f + P], c["ident"][:, :])
                    ins.then_inc(s["w_ps"], 1)
                    pe.wait_ge(s["got"], 16 * CT * (e + 1))
                    for k in range(DC):
                        for t in range(CT):
                            ins = pe.transpose(ps[:, 2 + k, P * t:P * t + P], xg[:, t, P * k:P * k + P], c["ident"][:, :])
                    ins.then_inc(s["x_ps"], 1)
                    pe.wait_ge(s["wT"], 2 * e + 2)
                    pe.wait_ge(s["xT"], e + 1)
                    for f in range(EC):
                        for k in range(DC):
                            ins = pe.matmul(ps[:, 4 + f, :], w1T[:, k, P * f:P * f + P], xT[:, k, :], start=k == 0,
                                            stop=k == DC - 1)
                        ins.then_inc(s["h_ps"], 1)
                    pe.wait_ge(s["hT"], EC * (e + 1))
                    for t in range(CT):
                        for f in range(EC):
                            ins = pe.matmul(ps[:, 6 + t // 2, D * (t % 2):D * (t % 2) + D], hT[:, f, P * t:P * t + P],
                                            w2T[:, f, :], start=f == 0, stop=f == EC - 1)
                    ins.then_inc(s["y_ps"], 1)

            @block.scalar
            def _(act):
                with act.Fori(0, E) as e:
                    act.wait_ge(s["y_ps"], e + 1)
                    act.wait_ge(s["x_ps"], e + 1)
                    for k in range(DC):
                        ins = act.copy(xT[:, k, :], ps[:, 2 + k, :])
                    ins.then_inc(s["xT"], 1)
                    for f in range(EC):
                        act.wait_ge(s["h_ps"], EC * e + f + 1)
                        act.activation(hT[:, f, :], ps[:, 4 + f, :], ACT.Gelu).then_inc(s["hT"], 1)

            @block.vector
            def _(dve):
                for name in FREE_AT_START:
                    dve.sem_inc(s[name], 1)
                with dve.Fori(0, E) as e:
                    dve.wait_ge(s["landed"], e + 1)
                    dve.tensor_copy(ix[:, 0, :], idx_get[:, ds(e, 1), :].rearrange("p a t -> p (a t)"))
                    dve.tensor_copy(ix[:, 1, :], idx_put[:, ds(e, 1), :].rearrange("p a t -> p (a t)"))
                    dve.tensor_copy(vl[:, :], valid[:, ds(e, 1), :].rearrange("p a t -> p (a t)")).then_inc(s["ix"], 1)
                    dve.wait_ge(s["w_ps"], 2 * e + 2)
                    dve.tensor_copy(w1T[:, :, :], ps[:, 0, :].rearrange("p (k f) -> p k f", k=DC)).then_inc(s["wT"], 1)
                    dve.wait_ge(s["w_ps"], 2 * e + 3)
                    dve.tensor_copy(w2T[:, :, :], ps[:, 1, :].rearrange("p (f d) -> p f d", f=EC)).then_inc(s["wT"], 1)
                    dve.wait_ge(s["got"], 16 * CT * (e + 1))
                    dve.wait_ge(s["ix"], e + 1)
                    dve.tensor_tensor(sc[:, :], xg[:, :, ds(e + D, 1)].rearrange("p t a -> p (t a)"), vl[:, :],
                                      ALU.mult).then_inc(s["sc"], 1)
                    dve.wait_ge(s["sc"], e + 1)
                    dve.wait_ge(s["y_ps"], e + 2)
                    for t in range(CT):
                        ins = dve.tensor_scalar(y[:, t, :], ps[:, 6 + t // 2, D * (t % 2):D * (t % 2) + D],
                                                sc[:, t:t + 1], None, ALU.mult)
                    ins.then_inc(s["y"], 1)


def clear_sum(nc, ysum):
    with ExitStack() as ctx:
        z = ctx.enter_context(nc.sbuf_tensor("cl_z", [P, D], F32))
        s = sems(ctx, nc, "cl", "z out")
        R = (N + SPARE) // P
        with nc.Block() as block:
            @block.vector
            def _(dve):
                dve.memset(z[:, :], 0.0).then_inc(s["z"], 1)

            @block.sync
            def _(sp):
                sp.wait_ge(s["z"], 1)
                yv = ysum.rearrange("(t p) d -> t p d", p=P)
                for t in range(R):
                    sp.dma_start(yv[t], z[:, :]).then_inc(s["out"], 16)
                sp.wait_ge(s["out"], 16 * R)


def finish(nc, x_all, ysum, out):
    with ExitStack() as ctx:
        y = ctx.enter_context(nc.sbuf_tensor("fi_y", [P, 2, TPB, D], F32))
        s = sems(ctx, nc, "fi", "y0 y1 sum out")
        yv = ysum[0:N, :].rearrange("(t p) d -> p t d", p=P)
        ov = out.rearrange("b (t p) d -> p (b t) d", p=P)
        with nc.Block() as block:
            @block.sync
            def _(sp):
                for i in range(B):
                    if i >= 2:
                        sp.wait_ge(s["sum"], i - 1)
                    sp.dma_start(y[:, i % 2, :, :], yv[:, i * TPB:(i + 1) * TPB, :]).then_inc(s[f"y{i % 2}"], 16)

            @block.vector
            def _(dve):
                for i in range(B):
                    dve.wait_ge(s[f"y{i % 2}"], 16 * (i // 2 + 1))
                    xv = x_all[:, i * TPB:(i + 1) * TPB, :]
                    dve.tensor_tensor(xv, xv, y[:, i % 2, :, :], ALU.add).then_inc(s["sum"], 1)

            @block.scalar
            def _(act):
                for i in range(B):
                    act.wait_ge(s["sum"], i + 1)
                    act.dma_start(ov[:, i * TPB:(i + 1) * TPB, :], x_all[:, i * TPB:(i + 1) * TPB, :]).then_inc(s["out"], 16)
                act.wait_ge(s["out"], 16 * B)


def build(nc, a, rows, ysum, out):
    with ExitStack() as ctx:
        sb = allocator(ctx, nc, "k")
        x_all = sb("x", [P, NT, D], F32)
        c = {"ident": sb("ident", [P, P], F32), "sel": sb("sel", [MH, MH, P], F32), "lower": sb("lower", [P, P], F32),
             "lower_bf": sb("lower_bf", [P, P], BF16), "ones_row": sb("ones_row", [P, S], F32),
             "ones_bf": sb("ones_bf", [P, P], BF16), "minus_half": sb("minus_half", [P, 16], F32),
             "earlier": sb("earlier", [P, E, E], F32), "slot": sb("slot", [P, P], F32), "part": sb("part", [P, 1], F32),
             "tile_no": sb("tile_no", [P, NT], F32), "spare": sb("spare", [P, 1], F32)}
        setup(nc, c, a["x"], x_all)
        with nc.Block() as block:
            @block.vector
            def _(dve):
                dve.tensor_copy(c["lower_bf"][:, :], c["lower"][:, :])
        with ExitStack() as mid:
            sbm = allocator(mid, nc, "m")
            ctxT_all = sbm("ctxT", [P, DC, N], F32)
            mlstm(nc, c, x_all, ctxT_all, a["ctx_1024"], a["L0_xattn_ig_kernel"], a["L0_xattn_ig_bias"],
                  a["L0_xattn_fg_kernel"], a["L0_xattn_fg_bias"], a["L0_xattn_outnorm_weight"])
            xnT_all = sbm("xnT", [P, DC, N], F32)
            norm_and_turn(nc, c, "n1", x_all, xnT_all)
            mlp(nc, c, x_all, xnT_all, a["L0_ffn_w1"], a["L0_ffn_b1"], a["L0_ffn_w2"], a["L0_ffn_b2"])
            norm_and_turn(nc, c, "n2", x_all, xnT_all)
            attention(nc, c, x_all, xnT_all, ctxT_all, a["L1_xattn_W_Query"], a["L1_xattn_W_Key"],
                      a["L1_xattn_W_Value"], a["L1_xattn_W_Output"], a["L1_xattn_B_Query"], a["L1_xattn_B_Key"],
                      a["L1_xattn_B_Value"], a["L1_xattn_B_Output"])
        clear_sum(nc, ysum)
        prob = sb("prob", [P, NT, E], F32)
        final = sb("final", [P, NT, E], F32)
        idx_get = sb("idx_get", [P, E, CT], I32)
        idx_put = sb("idx_put", [P, E, CT], I32)
        valid = sb("valid", [P, E, CT], F32)
        with ExitStack() as mid:
            xnT_all = allocator(mid, nc, "r")("xnT", [P, DC, N], F32)
            norm_and_turn(nc, c, "n3", x_all, xnT_all, rows)
            router(nc, c, xnT_all, a["L1_ffn_gate_w"], rows, prob, final, idx_get, idx_put, valid)
        experts(nc, c, rows, ysum, a["L1_ffn_w1"], a["L1_ffn_w2"], idx_get, idx_put, valid)
        finish(nc, x_all, ysum, out)


_INS = ["x", "ctx_1024", "L0_xattn_ig_kernel", "L0_xattn_ig_bias", "L0_xattn_fg_kernel", "L0_xattn_fg_bias",
        "L0_xattn_outnorm_weight", "L0_ffn_w1", "L0_ffn_b1", "L0_ffn_w2", "L0_ffn_b2", "L1_xattn_W_Query",
        "L1_xattn_W_Key", "L1_xattn_W_Value", "L1_xattn_W_Output", "L1_xattn_B_Query", "L1_xattn_B_Key",
        "L1_xattn_B_Value", "L1_xattn_B_Output", "L1_ffn_gate_w", "L1_ffn_w1", "L1_ffn_w2"]


def kernel(**inputs):
    import numpy as np
    import concourse.bacc as bacc
    from concourse.bass_utils import run_bass_kernel_spmd as run

    nc = bacc.Bacc("TRN2", target_bir_lowering=False, num_devices=1)
    arrays, aps = {}, {}
    for name in _INS:
        arr = np.ascontiguousarray(inputs[name])
        arrays[f"in_{name}"] = arr
        aps[name] = nc.dram_tensor(f"in_{name}", arr.shape, mybir.dt.from_np(arr.dtype), kind="ExternalInput").ap()
    rows = nc.dram_tensor("rows", (N, ROW), F32, kind="Internal").ap()
    ysum = nc.dram_tensor("ysum", (N + SPARE, D), F32, kind="Internal").ap()
    out = nc.dram_tensor("out_0", (B, S, D), F32, kind="ExternalOutput").ap()
    build(nc, aps, rows, ysum, out)
    r = run(nc, [arrays], core_ids=[0])
    return r.results[0]["out_0"]
```

```python
from contextlib import ExitStack

import concourse.bass as bass
from concourse import mybir

F32 = mybir.dt.float32
BF16 = mybir.dt.bfloat16
I32 = mybir.dt.int32
U32 = mybir.dt.uint32
ALU = mybir.AluOpType
ACT = mybir.ActivationFunctionType
AX = mybir.AxisListType
ds = bass.ds

P = 128
B, S, D = 8, 512, 256
N = B * S
TPB = S // P
NT = N // P
DC = D // P
MH, MD = 4, 64
F = 1024
FC = F // P
AH, AD = 16, 64
HP = AH // 2
E, EF = 8, 256
CAP = N // E
CT = CAP // P
ROW = D + E
SPARE = P
LN_EPS = 1e-5
MIX_EPS = 1e-6
FAR = 1e9


def sems(ctx, nc, phase, names):
    return {n: ctx.enter_context(nc.semaphore(f"{phase}_{n}")) for n in names.split()}


def wait_apart(eng, sem, value):
    eng.wait_ge(sem, value)
    eng.nop(nofuse=True)


def norm_stats_dve(dve, s, i, x_all, tmp):
    for t in range(TPB):
        ins = dve.bn_stats(tmp["stats"][:, t, :], x_all[:, ds(i * TPB + t, 1), :].rearrange("p a d -> p (a d)"))
    ins.then_inc(s["stats"], 1)
    wait_apart(dve, s["stats"], i + 1)
    for t in range(TPB):
        ins = dve.bn_aggr(tmp["mv"][:, t, :], tmp["stats"][:, t, :])
    ins.then_inc(s["mv"], 1)
    dve.wait_ge(s["mv"], i + 1)
    dve.tensor_scalar(tmp["ve"][:, :], tmp["mv"][:, :, 1], LN_EPS, None, ALU.add).then_inc(s["ve"], 1)


def norm_apply_dve(dve, s, i, x_all, tmp, wait_free):
    wait_free()
    dve.wait_ge(s["rstd"], i + 1)
    for t in range(TPB):
        ins = dve.tensor_scalar(tmp["xn"][:, t, :], x_all[:, ds(i * TPB + t, 1), :].rearrange("p a d -> p (a d)"),
                                tmp["mv"][:, t, 0:1], tmp["rstd"][:, t:t + 1], ALU.subtract, ALU.mult)
    ins.then_inc(s["xn"], 1)


def norm_batch_dve(dve, s, i, x_all, tmp, wait_free):
    norm_stats_dve(dve, s, i, x_all, tmp)
    norm_apply_dve(dve, s, i, x_all, tmp, wait_free)


def norm_batch_pool(pool, s, i, tmp, minus_half):
    wait_apart(pool, s["ve"], i + 1)
    pool.tensor_tensor(tmp["rstd"][:, :], tmp["ve"][:, :], minus_half[:, 0:TPB], ALU.pow).then_inc(s["rstd"], 1)


def norm_tmp(sb, count):
    return [{"stats": sb(f"stats{n}", [P, TPB, 6], F32), "mv": sb(f"mv{n}", [P, TPB, 2], F32),
             "ve": sb(f"ve{n}", [P, TPB], F32), "rstd": sb(f"rstd{n}", [P, TPB], F32),
             "xn": sb(f"xn{n}", [P, TPB, D], F32)} for n in range(count)]


def allocator(ctx, nc, phase):
    def sb(name, shape, dt):
        return ctx.enter_context(nc.sbuf_tensor(f"{phase}_{name}", shape, dt))
    return sb


def setup(nc, c):
    with ExitStack() as ctx:
        s = sems(ctx, nc, "st", "zero cleared fill lower")
        with nc.Block() as block:
            @block.vector
            def _(dve):
                dve.memset(c["zeros"][:, :], 0.0)
                dve.memset(c["group"][:, :], 0.0).then_inc(s["cleared"], 1)
                dve.wait_ge(s["cleared"], 1)
                for g in range(P // NT):
                    dve.memset(c["group"][NT * g:NT * g + NT, NT * g:NT * g + NT], 1.0)
                dve.wait_ge(s["fill"], 1)
                dve.tensor_copy(c["lower_bf"][:, :], c["lower"][:, :]).then_inc(s["lower"], 1)

            @block.gpsimd
            def _(pool):
                pool.memset(c["ident"][:, :], 0.0)
                pool.memset(c["sel"][:, :, :], 0.0)
                pool.memset(c["lower"][:, :], 1.0)
                pool.memset(c["ones_row"][:, :], 1.0)
                pool.memset(c["ones_bf"][:, :], 1.0)
                pool.memset(c["minus_half"][:, :], -0.5)
                pool.memset(c["earlier"][:, :, :], 1.0).then_inc(s["zero"], 1)
                pool.wait_ge(s["zero"], 1)
                pool.affine_select(out=c["ident"][:, :], in_=c["ident"][:, :], compare_op=ALU.not_equal, fill=1.0,
                                   base=0, pattern=[[-1, P]], channel_multiplier=1)
                pool.affine_select(out=c["sel"][:, :, :], in_=c["sel"][:, :, :], compare_op=ALU.not_equal, fill=1.0,
                                   base=0, pattern=[[-1, MH], [0, P]], channel_multiplier=1)
                pool.affine_select(out=c["lower"][:, :], in_=c["lower"][:, :], compare_op=ALU.is_gt, fill=0.0,
                                   base=0, pattern=[[1, P]], channel_multiplier=-1)
                pool.affine_select(out=c["earlier"][:, :, :], in_=c["earlier"][:, :, :], compare_op=ALU.is_gt,
                                   fill=0.0, base=0, pattern=[[1, E], [-1, E]], channel_multiplier=0)
                pool.iota(c["slot"][:, :], pattern=[[1, P]], base=0, channel_multiplier=0,
                          allow_small_or_imprecise_dtypes=True)
                pool.iota(c["part"][:, :], pattern=[[0, 1]], base=0, channel_multiplier=1,
                          allow_small_or_imprecise_dtypes=True)
                pool.iota(c["tile_no"][:, :], pattern=[[1, NT]], base=0, channel_multiplier=0,
                          allow_small_or_imprecise_dtypes=True).then_inc(s["fill"], 1)
                pool.wait_ge(s["fill"], 1)


def mlstm_gates(nc, c, x, x_all, xnT_all, ctxT_all, cols, gate_rows, max_rows, ctx_in, ig_kernel, ig_bias, fg_kernel,
                fg_bias):
    R = MH * B
    GW = 36
    with ExitStack() as ctx:
        sb = allocator(ctx, nc, "mg")
        tmp = norm_tmp(sb, 2)
        ctx_s = sb("ctx", [P, 2, TPB, D], F32)
        gk_in = sb("gk_in", [P, 3 * DC, 2 * MH], F32)
        gate_w = sb("gate_w", [P, 2 * DC, GW], F32)
        gbias = sb("gbias", [GW, 1], F32)
        own = sb("own", [GW, B, S], F32)
        ig, fg, absf, efg, lfg, cums, g, gmax, logmax, floor = (
            sb(n, [R, S], F32) for n in "ig fg absf efg lfg cums g gmax logmax floor".split())
        ps = ctx.enter_context(nc.psum_tensor("mg_ps", [P, 8, 512], F32))
        XN_BANK, CTX_BANK, GATE_BANK, COL_BANK = 0, 2, 4, 6
        s = sems(ctx, nc, "mg", "x0 x1 x2 x_rest w bias wset gw ctx0 ctx1 stats mv ve rstd xn xn_turned ctx_turned "
                 "xnT ctxT gates own own_stored "
                 "ig_in fg_in rows act_rows cols_ps cols max_stored")
        xv = x.rearrange("b (t p) d -> b p t d", p=P)
        cv = ctx_in.rearrange("b (t p) d -> b p t d", p=P)
        ident = c["ident"]
        BANKS_FREE = 2

        with nc.Block() as block:
            @block.sync
            def _(sp):
                def store_gates(i):
                    sp.wait_ge(s["own"], BANKS_FREE + i + 1)
                    for half in range(2):
                        sp.dma_start(gate_rows[half, ds(i, 1), :, :].rearrange("a h n -> (a h) n"),
                                     own[32 * half:32 * half + MH, ds(i, 1), :].rearrange("h a n -> h (a n)")
                                     ).then_inc(s["own_stored"], 16)

                for i in range(2):
                    sp.dma_start(x_all[:, i * TPB:(i + 1) * TPB, :], xv[i]).then_inc(s[f"x{i}"], 16)
                sp.dma_start(gk_in[:, :, 0:MH], ig_kernel.rearrange("(c p) h -> p c h", p=P)).then_inc(s["w"], 16)
                sp.dma_start(gk_in[:, :, MH:2 * MH], fg_kernel.rearrange("(c p) h -> p c h", p=P)).then_inc(s["w"], 16)
                sp.wait_ge(s["wset"], 1)
                sp.dma_start(gbias[0:MH, :], ig_bias.rearrange("(h a) -> h a", a=1)).then_inc(s["bias"], 16)
                sp.dma_start(gbias[32:32 + MH, :], fg_bias.rearrange("(h a) -> h a", a=1)).then_inc(s["bias"], 16)
                sp.dma_start(x_all[:, 2 * TPB:3 * TPB, :], xv[2]).then_inc(s["x2"], 16)
                with sp.Fori(3, B) as i:
                    sp.dma_start(x_all[:, ds(i * TPB, TPB), :], xv[ds(i, 1)].rearrange("a p t d -> p (a t) d")
                                 ).then_inc(s["x_rest"], 16)
                with sp.Fori(0, B // 2 - 1) as pair:
                    for par in range(2):
                        i = pair * 2 + par
                        store_gates(i)
                store_gates(B - 2)
                store_gates(B - 1)
                sp.wait_ge(s["own_stored"], 32 * B)
                for half, row, name in ((0, ig, "ig_in"), (1, fg, "fg_in")):
                    sp.dma_start(row[:, :], gate_rows[half].rearrange("b h n -> (b h) n")).then_inc(s[name], 16)
                sp.wait_ge(s["rows"], 5)
                sp.dma_start(max_rows.rearrange("b h n -> (b h) n"), gmax[:, :]).then_inc(s["max_stored"], 16)
                sp.wait_ge(s["max_stored"], 16)

            @block.gpsimd
            def _(pool):
                pool.memset(gbias[:, :], 0.0).then_inc(s["wset"], 1)
                with pool.Fori(0, B // 2) as pair:
                    for par in range(2):
                        norm_batch_pool(pool, s, pair * 2 + par, tmp[par], c["minus_half"])

            @block.tensor
            def _(pe):
                def turn(i, par):
                    pe.wait_ge(s["xn"], i + 1)
                    pe.wait_ge(s["xnT"], i)
                    for k in range(DC):
                        for t in range(TPB):
                            ins = pe.transpose(ps[:, XN_BANK + k, P * t:P * t + P],
                                               tmp[par]["xn"][:, t, P * k:P * k + P], ident[:, :])
                    ins.then_inc(s["xn_turned"], 1)
                    pe.wait_ge(s[f"ctx{par}"], 16 * (i // 2 + 1))
                    pe.wait_ge(s["ctxT"], i)
                    for k in range(DC):
                        for t in range(TPB):
                            ins = pe.transpose(ps[:, CTX_BANK + k, P * t:P * t + P], ctx_s[:, par, t, P * k:P * k + P],
                                               ident[:, :])
                    ins.then_inc(s["ctx_turned"], 1)

                def gate_maps(i, par):
                    pe.wait_ge(s["xnT"], i + 1)
                    pe.wait_ge(s["ctxT"], i + 1)
                    pe.wait_ge(s["own"], i + 1)
                    for k in range(2 * DC):
                        rhs = (xnT_all if k < DC else ctxT_all)[:, k % DC, ds(i * S, S)]
                        ins = pe.matmul(ps[0:GW, GATE_BANK + par, :], gate_w[:, k, :], rhs, start=k == 0,
                                        stop=k == 2 * DC - 1)
                    ins.then_inc(s["gates"], 1)

                turn(0, 0)
                pe.wait_ge(s["gw"], 5)
                with pe.Fori(0, B // 2 - 1) as pair:
                    for par in range(2):
                        turn(pair * 2 + par + 1, 1 - par)
                        gate_maps(pair * 2 + par, par)
                turn(B - 1, 1)
                gate_maps(B - 2, 0)
                gate_maps(B - 1, 1)
                pe.wait_ge(s["rows"], 4)
                for t in range(TPB):
                    pe.transpose(ps[:, COL_BANK, R * t:R * t + R], g[:, P * t:P * t + P], ident[0:R, 0:R])
                pe.wait_ge(s["act_rows"], 3)
                for t in range(TPB):
                    ins = pe.transpose(ps[:, COL_BANK, R * (TPB + t):R * (TPB + t + 1)], floor[:, P * t:P * t + P],
                                       ident[0:R, 0:R])
                ins.then_inc(s["cols_ps"], 1)

            @block.scalar
            def _(act):
                def load_ctx(i, par):
                    act.dma_start(ctx_s[:, par, :, :], cv[ds(i, 1)].rearrange("a p t d -> p (a t) d")
                                  ).then_inc(s[f"ctx{par}"], 16)

                def keep_turned(i):
                    act.wait_ge(s["xn_turned"], i + 1)
                    for k in range(DC):
                        ins = act.copy(xnT_all[:, k, ds(i * S, S)], ps[:, XN_BANK + k, :])
                    ins.then_inc(s["xnT"], 1)
                    act.wait_ge(s["ctx_turned"], i + 1)
                    for k in range(DC):
                        ins = act.copy(ctxT_all[:, k, ds(i * S, S)], ps[:, CTX_BANK + k, :])
                    ins.then_inc(s["ctxT"], 1)

                def keep_gates(i, par):
                    act.wait_ge(s["gates"], i + 1)
                    act.activation(own[:, ds(i, 1), :].rearrange("h a n -> h (a n)"), ps[0:GW, GATE_BANK + par, :],
                                   ACT.Identity, bias=gbias[:, :]).then_inc(s["own"], 1)

                load_ctx(0, 0)
                load_ctx(1, 1)
                act.wait_ge(s["bias"], 32)
                keep_turned(0)
                with act.Fori(0, B // 2 - 1) as pair:
                    for par in range(2):
                        load_ctx(pair * 2 + par + 2, par)
                        keep_turned(pair * 2 + par + 1)
                        keep_gates(pair * 2 + par, par)
                keep_turned(B - 1)
                keep_gates(B - 2, 0)
                keep_gates(B - 1, 1)
                act.wait_ge(s["rows"], 1)
                act.activation(efg[:, :], absf[:, :], ACT.Exp, scale=-1.0).then_inc(s["act_rows"], 1)
                act.wait_ge(s["act_rows"], 1)
                act.activation(lfg[:, :], efg[:, :], ACT.Ln, bias=1.0).then_inc(s["act_rows"], 1)
                act.wait_ge(s["rows"], 6)
                act.activation(floor[:, :], logmax[:, :], ACT.Exp, scale=-1.0).then_inc(s["act_rows"], 1)

            @block.vector
            def _(dve):
                dve.sem_inc(s["own"], BANKS_FREE)
                dve.memset(gate_w[:, :, :], 0.0).then_inc(s["gw"], 1)
                for i in range(2):
                    dve.wait_ge(s[f"x{i}"], 16)
                    norm_stats_dve(dve, s, i, x_all, tmp[i])
                norm_apply_dve(dve, s, 0, x_all, tmp[0], lambda: None)
                dve.wait_ge(s["gw"], 1)
                dve.wait_ge(s["w"], 16 * 2)
                for half in range(2):
                    src = gk_in[:, :, MH * half:MH * half + MH]
                    dst = gate_w[:, :, 32 * half:32 * half + MH]
                    dve.tensor_copy(dst[:, 0:DC, :], src[:, 0:DC, :]).then_inc(s["gw"], 1)
                    dve.tensor_tensor(dst[:, DC:2 * DC, :], src[:, DC:2 * DC, :], src[:, 2 * DC:3 * DC, :],
                                      ALU.add).then_inc(s["gw"], 1)
                dve.wait_ge(s["x2"], 16)
                dve.wait_ge(s["xn"], 1)
                norm_stats_dve(dve, s, 2, x_all, tmp[0])
                norm_apply_dve(dve, s, 1, x_all, tmp[1], lambda: None)
                dve.wait_ge(s["x_rest"], 16 * (B - 3))

                def stats_ahead(i, par):
                    wait_apart(dve, s["xn"], i)
                    norm_stats_dve(dve, s, i + 1, x_all, tmp[1 - par])
                    norm_apply_dve(dve, s, i, x_all, tmp[par], lambda: dve.wait_ge(s["xn_turned"], i - 1))

                with dve.Fori(1, B // 2 - 1) as pair:
                    stats_ahead(pair * 2, 0)
                    stats_ahead(pair * 2 + 1, 1)
                stats_ahead(B - 2, 0)
                norm_apply_dve(dve, s, B - 1, x_all, tmp[1], lambda: dve.wait_ge(s["xn_turned"], B - 2))

                def row(ins, k):
                    ins.then_inc(s["rows"], 1)
                    dve.wait_ge(s["rows"], k)

                dve.wait_ge(s["ig_in"], 16)
                dve.wait_ge(s["fg_in"], 16)
                row(dve.scalar_tensor_tensor(out=absf[:, :], in0=fg[:, :], scalar=-1.0, in1=fg[:, :],
                                             op0=ALU.mult, op1=ALU.max), 1)
                dve.wait_ge(s["act_rows"], 2)
                row(dve.scalar_tensor_tensor(out=fg[:, :], in0=fg[:, :], scalar=0.0, in1=lfg[:, :],
                                             op0=ALU.min, op1=ALU.subtract), 2)
                row(dve.tensor_tensor_scan(cums[:, :], c["ones_row"][0:R, :], fg[:, :], 0.0, ALU.mult, ALU.add), 3)
                row(dve.tensor_tensor(g[:, :], ig[:, :], cums[:, :], ALU.subtract), 4)
                row(dve.tensor_tensor_scan(gmax[:, :], g[:, :], g[:, :], -3.0e38, ALU.max, ALU.max), 5)
                row(dve.tensor_tensor(logmax[:, :], cums[:, :], gmax[:, :], ALU.add), 6)
                dve.wait_ge(s["cols_ps"], 1)
                dve.tensor_copy(cols[:, :, :, :], ps[:, COL_BANK, 0:2 * TPB * R].rearrange(
                    "p (a t r) -> p a t r", a=2, t=TPB)).then_inc(s["cols"], 1)


def wait_count(eng, sem, value):
    if not isinstance(value, int) or value > 0:
        eng.wait_ge(sem, value)


def wide(m, k):
    return m["nrm"][:, k, :].rearrange("p (g a) -> p g a", a=1).broadcast_to([P, MH * TPB, MD])


def finish_heads(dve, s, m, i, par, part):
    def fin(ins, k):
        ins.then_inc(s["fin"], 1)
        dve.wait_ge(s["fin"], 11 * i + k)

    if part == 0:
        total = m["hs"][:, par, :, :, MD:MD + 1].rearrange("p h t a -> p (h t a)")
        n0 = m["nrm"][:, 0, :].rearrange("p (h t) -> p h t", h=MH)
        dve.wait_ge(s["hs"], MH * (i + 1))
        wait_count(dve, s["out"], i - 1)
        fin(dve.scalar_tensor_tensor(out=m["nrm"][:, 0, :], in0=total, scalar=-1.0, in1=total,
                                     op0=ALU.mult, op1=ALU.max), 1)
        fin(dve.tensor_tensor(n0, n0, m["cols"][:, 1, :, ds(i * MH, MH)].rearrange("p t h -> p h t"),
                              ALU.max), 2)
        fin(dve.tensor_scalar(m["nrm"][:, 1, :], m["nrm"][:, 0, :], MIX_EPS, None, ALU.add), 3)
        fin(dve.reciprocal(m["nrm"][:, 2, :], m["nrm"][:, 1, :]), 4)
        fin(dve.tensor_tensor(m["hw"][:, par, :, :], m["hs"][:, par, :, :, 0:MD].rearrange("p h t d -> p (h t) d"),
                              wide(m, 2), ALU.mult), 5)
    elif part == 1:
        fin(dve.tensor_reduce(m["nrm"][:, 3, :], m["hw"][:, par, :, :], AX.X, ALU.add), 6)
        fin(dve.tensor_scalar(m["nrm"][:, 4, :], m["nrm"][:, 3, :], 1.0 / MD, None, ALU.mult), 7)
        fin(dve.tensor_tensor(m["hw"][:, par, :, :], m["hw"][:, par, :, :], wide(m, 4), ALU.subtract), 8)
    else:
        fin(dve.tensor_tensor(m["sq"][:, :, :], m["hw"][:, par, :, :], m["hw"][:, par, :, :], ALU.mult), 9)
        fin(dve.tensor_reduce(m["nrm"][:, 5, :], m["sq"][:, :, :], AX.X, ALU.add), 10)
        wait_count(dve, s["fin_pow"], 3 * i - 2)
        fin(dve.tensor_scalar(m["nrm"][:, 6, :], m["nrm"][:, 5, :], 1.0 / MD, MIX_EPS, ALU.mult, ALU.add), 11)


def add_heads(pool, c, s, m, x_all, i, par, part):
    hw = m["hw"][:, par, :, :]
    hv = hw.rearrange("p (h t) d -> p h t d", h=MH)
    if part == 0:
        wait_apart(pool, s["fin"], 11 * i + 11)
        pool.tensor_tensor(m["nrm"][:, 7, :], m["nrm"][:, 6, :], c["minus_half"][:, 0:MH * TPB],
                           ALU.pow).then_inc(s["fin_pow"], 1)
        wait_apart(pool, s["fin_pow"], 3 * i + 1)
    elif part == 1:
        pool.tensor_tensor(hw, hw, wide(m, 7), ALU.mult).then_inc(s["fin_pow"], 1)
        wait_apart(pool, s["fin_pow"], 3 * i + 2)
    elif part == 2:
        wv = m["w_row"][:, :].rearrange("p (h a d) -> p h a d", h=MH, a=1).broadcast_to([P, MH, TPB, MD])
        pool.tensor_tensor(hv, hv, wv, ALU.mult).then_inc(s["fin_pow"], 1)
        wait_apart(pool, s["fin_pow"], 3 * i + 3)
    else:
        xv = x_all[:, ds(i * TPB, TPB), :].rearrange("p t (h d) -> p h t d", h=MH)
        pool.tensor_tensor(xv, xv, hv, ALU.add).then_inc(s["out"], 1)


def mlstm_mix(nc, c, s_fin, m, x_all, xnT_all, ctxT_all, max_rows, ctx_in, outnorm):
    OFF = [0, 512, 896, 1152]
    LEN = [S - P * t for t in range(TPB)]
    PACK = sum(LEN)
    U = MH * B
    F32R = mybir.dt.float32r
    DOUBLES = 16 * 2 * MH
    with ExitStack() as ctx:
        sb = allocator(ctx, nc, "mm")
        q2 = sb("q2", [P, 2, S], F32R)
        k_own = sb("k_own", [P, 2, DC, S], F32R)
        k2 = sb("k2", [P, 2, MH, 2, S], F32R)
        vaug = sb("vaug", [P, 2, TPB, MH, MD + 1], F32)
        mrow = sb("mrow", [MH, 2, S], F32)
        Dm = sb("Dm", [P, 2, PACK], F32)
        C = sb("C", [P, 2, PACK], F32)
        hT = sb("hT", [MD + 1, 2, S], F32)
        ps = ctx.enter_context(nc.psum_tensor("mm_ps", [P, 8, 512], F32))
        M_BANK, C_BANK, H_BANK, TURN_BANK = 0, 2, 5, 7
        s = sems(ctx, nc, "mm", "ones kh kl k2 qh ql mrow vaug m_ps d_exp d_masked c_ps c pv hT h_turned")
        cv = ctx_in.rearrange("b (t p) d -> b p t d", p=P)

        def unit_at(i, par, h, k):
            shift, head = (h + k) // MH, (h + k) % MH
            row, row_par = i + shift, (par + shift) % 2
            u = row * MH + head
            return None if isinstance(u, int) and not 0 <= u < U else (u, row, row_par, head)

        def every_slot(eng, slot):
            for i in range(2):
                for h in range(MH):
                    slot(i, i, h)
            with eng.Fori(1, B // 2 - 1) as pair:
                for par in range(2):
                    for h in range(MH):
                        slot(pair * 2 + par, par, h)
            for i in range(B - 2, B + 1):
                for h in range(MH):
                    slot(i, i % 2, h)

        def has_next(i):
            return not (isinstance(i, int) and i >= B - 1)

        with nc.Block() as block:
            @block.sync
            def _(sp):
                def load(i, par):
                    sp.dma_start(mrow[:, par, :], max_rows[ds(i, 1), :, :].rearrange("a h n -> (a h) n")
                                 ).then_inc(s["mrow"], 16)
                    for t in range(TPB):
                        sp.dma_start(vaug[:, par, t, :, 0:MD], cv[ds(i, 1), :, t, :].rearrange(
                            "a p (h d) -> p (a h) d", h=MH)).then_inc(s["vaug"], 16)
                    sp.wait_ge(s["kh"], i + 1)
                    sp.wait_ge(s["kl"], i + 1)
                    for h in range(MH):
                        own = slice(MD * (h % 2), MD * (h % 2) + MD)
                        for half in range(2):
                            sp.dma_start(k2[MD * half:MD * half + MD, par, h, :, :].bitcast(F32),
                                         k_own[own, :, h // 2, :].bitcast(F32)).then_inc(s["k2"], 16)

                load(0, 0)
                row = outnorm.rearrange("h d -> (h d)").rearrange("(a n) -> a n", a=1)
                sp.dma_start(m["w_row"][:, :], row.broadcast_to([P, D])).then_inc(s_fin["w"], 16)
                sp.wait_ge(s["pv"], 1)
                load(1, 1)
                with sp.Fori(0, B // 2 - 1) as pair:
                    for par in range(2):
                        i = pair * 2 + par + 2
                        sp.wait_ge(s["pv"], MH * (i - 1) + 1)
                        load(i, par)

            @block.tensor
            def _(pe):
                def spread_max(u, i, par, h):
                    pe.wait_ge(s["mrow"], 16 * (i + 1))
                    wait_count(pe, s["d_exp"], u - 1)
                    pe.matmul(ps[:, M_BANK + h % 2, :], c["sel"][:, h, :], mrow[:, par, :], start=True, stop=True
                              ).then_inc(s["m_ps"], 1)

                def turn_head(u, i, par, h):
                    wait_count(pe, s_fin["hs"], u)
                    wait_apart(pe, s["hT"], u + 1)
                    for t in range(TPB):
                        ins = pe.transpose(ps[:, TURN_BANK, (MD + 1) * t:(MD + 1) * (t + 1)],
                                           hT[:, h % 2, P * t:P * t + P], c["ident"][0:MD + 1, 0:MD + 1])
                    ins.then_inc(s["h_turned"], 1)

                def scores(u, i, par, h):
                    pe.wait_ge(s["k2"], DOUBLES * (i + 1))
                    pe.wait_ge(s["ql"], u + 1)
                    for t in range(TPB):
                        bank, at = (t, 0) if t < 3 else (2, LEN[2])
                        if t < 3:
                            wait_count(pe, s["c"], u * 3 - 2 + t)
                        for part in range(2):
                            ins = pe.matmul(ps[:, C_BANK + bank, at:at + LEN[t]],
                                            k2[:, par, h, part, P * t:P * t + P], q2[:, h % 2, P * t:S],
                                            start=part == 0, stop=part == 1)
                        if t != 2:
                            ins.then_inc(s["c_ps"], 1)

                def values(u, i, par, h):
                    pe.wait_ge(s["vaug"], 16 * TPB * (i + 1))
                    wait_count(pe, s["hT"], u - 1)
                    pe.wait_ge(s["c"], u * 3 + 3)
                    for t in range(TPB):
                        ins = pe.matmul(ps[0:MD + 1, H_BANK + h % 2, P * t:S], vaug[:, par, t, h, :],
                                        C[:, h % 2, OFF[t]:OFF[t] + LEN[t]],
                                        start=t == 0, stop=t == TPB - 1, skip_group_check=True)
                    ins.then_inc(s["pv"], 1)

                def slot(i, par, h):
                    for k, stage in ((1, spread_max), (-2, turn_head), (0, scores), (-1, values)):
                        at = unit_at(i, par, h, k)
                        if at:
                            stage(*at)

                pe.wait_ge(s["ones"], 1)
                spread_max(0, 0, 0, 0)
                every_slot(pe, slot)

            @block.scalar
            def _(act):
                def split_keys(i):
                    if not (isinstance(i, int) and i == 0):
                        act.wait_ge(s["k2"], DOUBLES * i)
                    act.copy(k_own[:, 0, :, :], ctxT_all[:, :, ds(i * S, S)]).then_inc(s["kh"], 1)

                def split_queries(u, i, par, h):
                    wait_count(act, s["c_ps"], u * 3 - 3)
                    own = slice(MD * (h % 2), MD * (h % 2) + MD)
                    act.copy(q2[own, h % 2, :], xnT_all[own, h // 2, ds(i * S, S)]).then_inc(s["qh"], 1)

                def decay(u, i, par, h):
                    act.wait_ge(s["m_ps"], u + 1)
                    wait_count(act, s["c"], u * 3 - 3)
                    for t in range(TPB):
                        ins = act.activation(Dm[:, h % 2, OFF[t]:OFF[t] + LEN[t]], ps[:, M_BANK + h % 2, P * t:S],
                                             ACT.Exp, scale=-1.0, bias=m["cols"][:, 0, t, ds(u, 1)])
                    ins.then_inc(s["d_exp"], 1)

                def keep_outputs(u, i, par, h):
                    act.wait_ge(s["pv"], u + 1)
                    wait_count(act, s["h_turned"], u - 1)
                    act.copy(hT[:, h % 2, :], ps[0:MD + 1, H_BANK + h % 2, :]).then_inc(s["hT"], 1)

                def slot(i, par, h):
                    for k, stage in ((1, split_queries), (1, decay), (-1, keep_outputs)):
                        at = unit_at(i, par, h, k)
                        if at:
                            stage(*at)
                    if h == 1 and has_next(i):
                        split_keys(i + 1)

                split_keys(0)
                split_queries(0, 0, 0, 0)
                decay(0, 0, 0, 0)
                every_slot(act, slot)

            @block.gpsimd
            def _(pool):
                def mask(u, i, par, h):
                    wait_apart(pool, s["d_exp"], u + 1)
                    for t in range(TPB):
                        diag = Dm[:, h % 2, OFF[t]:OFF[t] + P]
                        pool.affine_select(out=diag, in_=diag, compare_op=ALU.is_ge, fill=0.0, base=0,
                                           pattern=[[1, P]], channel_multiplier=-1).then_inc(s["d_masked"], 1)

                def slot(i, par, h):
                    at = unit_at(i, par, h, 1)
                    if at:
                        mask(*at)
                    if h == MH - 1 and not (isinstance(i, int) and i in (0, B - 1, B)):
                        add_heads(pool, c, s_fin, m, x_all, i - 1, 1 - par, 0)
                    if h < MH - 1 and not (isinstance(i, int) and i in (0, 1, B)):
                        add_heads(pool, c, s_fin, m, x_all, i - 2, par, h + 1)

                pool.memset(vaug[:, :, :, :, MD:MD + 1], 1.0).then_inc(s["ones"], 1)
                pool.wait_ge(s_fin["w"], 16)
                mask(0, 0, 0, 0)
                every_slot(pool, slot)

            @block.vector
            def _(dve):
                def weigh(u, i, par, h):
                    dve.wait_ge(s["d_masked"], TPB * (u + 1))
                    wait_count(dve, s["pv"], u - 1)
                    for bank in range(3):
                        dve.wait_ge(s["c_ps"], u * 3 + bank + 1)
                        lo, n = OFF[bank], (LEN[bank] if bank < 2 else LEN[2] + LEN[3])
                        dve.scalar_tensor_tensor(out=C[:, h % 2, lo:lo + n], in0=ps[:, C_BANK + bank, 0:n],
                                                 scalar=MD ** -0.5, in1=Dm[:, h % 2, lo:lo + n],
                                                 op0=ALU.mult, op1=ALU.mult).then_inc(s["c"], 1)

                def split_keys(i):
                    dve.wait_ge(s["kh"], i + 1)
                    dve.tensor_tensor(k_own[:, 1, :, :], ctxT_all[:, :, ds(i * S, S)], k_own[:, 0, :, :],
                                      ALU.subtract).then_inc(s["kl"], 1)

                def split_queries(u, i, par, h):
                    dve.wait_ge(s["qh"], u + 1)
                    own, other = slice(MD * (h % 2), MD * (h % 2) + MD), slice(MD - MD * (h % 2), 2 * MD - MD * (h % 2))
                    dve.tensor_tensor(q2[other, h % 2, :], xnT_all[own, h // 2, ds(i * S, S)], q2[own, h % 2, :],
                                      ALU.subtract).then_inc(s["ql"], 1)

                def keep_head(u, i, par, h):
                    dve.wait_ge(s["h_turned"], u + 1)
                    dve.tensor_copy(m["hs"][:, par, h, :, :], ps[:, TURN_BANK, 0:TPB * (MD + 1)].rearrange(
                        "p (t d) -> p t d", t=TPB)).then_inc(s_fin["hs"], 1)

                def slot(i, par, h):
                    for k, stage in ((-2, keep_head), (0, weigh), (1, split_queries)):
                        at = unit_at(i, par, h, k)
                        if at:
                            stage(*at)
                    if h == 1 and has_next(i):
                        split_keys(i + 1)
                    if h and not (isinstance(i, int) and i in (0, B)):
                        finish_heads(dve, s_fin, m, i - 1, 1 - par, h - 1)

                split_keys(0)
                split_queries(0, 0, 0, 0)
                every_slot(dve, slot)


def mlp(nc, c, s_fin, m, x_all, xnT_all, w1, b1, w2, b2, bias_after):
    with ExitStack() as ctx:
        sb = allocator(ctx, nc, "mlp")
        tmp_in, tmp_out = norm_tmp(sb, 2)
        w1_s = sb("w1", [P, DC, F], F32)
        w2_s = sb("w2", [P, FC, D], F32)
        b1_s = sb("b1", [P, FC], F32)
        b2_s = sb("b2", [P, D], F32)
        after_s = sb("after", [P, D], F32)
        hT = sb("hT", [P, FC, S], F32)
        ps = ctx.enter_context(nc.psum_tensor("mlp_ps", [P, 8, 512], F32))
        H_BANK, Y_BANK, TURN_BANK = 0, 4, 6
        YB = TPB // 2
        s = sems(ctx, nc, "mlp", "w h_ps hT y_ps y b after")
        s_in = sems(ctx, nc, "mli", "stats mv ve rstd xn turned out")
        s_out = sems(ctx, nc, "mlo", "stats mv ve rstd xn turned out")
        FREE_AT_START = [s["y"], s["y_ps"], s_in["turned"], s_out["turned"], s_out["out"]]

        def every_row(eng, step):
            step(0, first=True)
            with eng.Fori(1, B - 1) as i:
                step(i)
            step(B - 1, last=True)

        with nc.Block() as block:
            @block.sync
            def _(sp):
                sp.dma_start(w1_s[:, :, :], w1.rearrange("(c p) f -> p c f", p=P)).then_inc(s["w"], 16)
                sp.dma_start(w2_s[:, :, :], w2.rearrange("(c p) d -> p c d", p=P)).then_inc(s["w"], 16)
                sp.dma_start(b1_s[:, :], b1.rearrange("(c p) -> p c", p=P), allow_slow_non_contiguous=True).then_inc(s["w"], 16)
                sp.dma_start(b2_s[:, :], b2.rearrange("(a d) -> a d", a=1).broadcast_to([P, D])).then_inc(s["w"], 16)
                sp.dma_start(after_s[:, :], bias_after.rearrange("(a d) -> a d", a=1).broadcast_to([P, D])
                             ).then_inc(s["w"], 16)

            @block.gpsimd
            def _(pool):
                def step(i, first=False, last=False):
                    if not last:
                        norm_batch_pool(pool, s_in, i + 1, tmp_in, c["minus_half"])
                    if first:
                        for row in (B - 2, B - 1):
                            for part in range(4):
                                add_heads(pool, c, s_fin, m, x_all, row, row % 2, part)
                    norm_batch_pool(pool, s_out, i, tmp_out, c["minus_half"])

                norm_batch_pool(pool, s_in, 0, tmp_in, c["minus_half"])
                every_row(pool, step)

            @block.tensor
            def _(pe):
                def turn(sn, i, tmp):
                    pe.wait_ge(sn["xn"], i + 1)
                    for k in range(DC):
                        for t in range(TPB):
                            ins = pe.transpose(ps[:, TURN_BANK + k, P * t:P * t + P], tmp["xn"][:, t, P * k:P * k + P],
                                               c["ident"][:, :])
                    ins.then_inc(sn["turned"], 1)

                def step(i, first=False, last=False):
                    pe.wait_ge(s_in["out"], i + 1)
                    for f in range(FC):
                        if f >= 4:
                            pe.wait_ge(s["hT"], FC * i + f - 3)
                        for k in range(DC):
                            ins = pe.matmul(ps[:, H_BANK + f % 4, :], w1_s[:, k, P * f:P * f + P],
                                            xnT_all[:, k, ds(i * S, S)], start=k == 0, stop=k == DC - 1)
                        ins.then_inc(s["h_ps"], 1)
                    if not last:
                        pe.wait_ge(s_out["out"], i + (1 if first else 0))
                        turn(s_in, i + 1, tmp_in)
                    pe.wait_ge(s["y"], YB * i + 1)
                    pe.wait_ge(s["hT"], FC * i + FC)
                    for t in range(TPB):
                        for f in range(FC):
                            ins = pe.matmul(ps[:, Y_BANK + t // 2, D * (t % 2):D * (t % 2) + D],
                                            hT[:, f, P * t:P * t + P], w2_s[:, f, :], start=f == 0, stop=f == FC - 1)
                        if t % 2:
                            ins.then_inc(s["y_ps"], 1)
                    if not first:
                        if not last:
                            pe.wait_ge(s_in["out"], i + 2)
                        turn(s_out, i - 1, tmp_out)

                turn(s_in, 0, tmp_in)
                pe.wait_ge(s["w"], 80)
                every_row(pe, step)
                pe.wait_ge(s_out["out"], B)
                turn(s_out, B - 1, tmp_out)

            @block.scalar
            def _(act):
                def keep_turned(sn, i):
                    act.wait_ge(sn["turned"], i + 2)
                    for k in range(DC):
                        ins = act.copy(xnT_all[:, k, ds(i * S, S)], ps[:, TURN_BANK + k, :])
                    ins.then_inc(sn["out"], 1)

                def step(i, first=False, last=False):
                    act.wait_ge(s["y_ps"], YB * i + 1)
                    for f in range(FC):
                        act.wait_ge(s["h_ps"], FC * i + f + 1)
                        act.activation(hT[:, f, :], ps[:, H_BANK + f % 4, :], ACT.Gelu, bias=b1_s[:, f:f + 1]
                                       ).then_inc(s["hT"], 1)
                    if not last:
                        keep_turned(s_in, i + 1)
                    if not first:
                        keep_turned(s_out, i - 1)

                keep_turned(s_in, 0)
                act.wait_ge(s["w"], 80)
                every_row(act, step)
                keep_turned(s_out, B - 1)

            @block.vector
            def _(dve):
                for sem in FREE_AT_START:
                    dve.sem_inc(sem, 1)

                def norm(sn, i, tmp):
                    norm_batch_dve(dve, sn, i, x_all, tmp, lambda: dve.wait_ge(sn["turned"], i + 1))

                def step(i, first=False, last=False):
                    if not last:
                        norm(s_in, i + 1, tmp_in)
                    if first:
                        for part in range(3):
                            finish_heads(dve, s_fin, m, B - 1, 1, part)
                    for bank in range(YB):
                        dve.wait_ge(s["y_ps"], YB * i + bank + 2)
                        xv = x_all[:, ds(i * TPB + 2 * bank, 2), :].rearrange("p t d -> p (t d)")
                        dve.tensor_tensor(xv, ps[:, Y_BANK + bank, :], xv, ALU.add).then_inc(s["y"], 1)
                    dve.wait_ge(s["y"], YB * i + YB + 1)
                    for t in range(TPB):
                        xv = x_all[:, ds(i * TPB + t, 1), :].rearrange("p a d -> p (a d)")
                        ins = dve.tensor_tensor(xv, xv, b2_s[:, :], ALU.add)
                    ins.then_inc(s["b"], 1)
                    wait_apart(dve, s["b"], i + 1)
                    norm(s_out, i, tmp_out)
                    dve.wait_ge(s_out["xn"], i + 1)
                    for t in range(TPB):
                        xv = x_all[:, ds(i * TPB + t, 1), :].rearrange("p a d -> p (a d)")
                        ins = dve.tensor_tensor(xv, xv, after_s[:, :], ALU.add)
                    ins.then_inc(s["after"], 1)
                    if first:
                        dve.wait_ge(s_fin["out"], B)

                norm(s_in, 0, tmp_in)
                dve.wait_ge(s["w"], 80)
                every_row(dve, step)


def attention(nc, c, x_all, xnT_all, ctxT_all, Wq, Wk, Wv, Wo, Bq, Bk, Bv):
    U = HP * B
    NBL = 2 * TPB
    F32R = mybir.dt.float32r
    with ExitStack() as ctx:
        sb = allocator(ctx, nc, "at")
        w_next = sb("w_next", [P, 3, DC, P], F32)
        b_next = sb("b_next", [P, 3], F32)
        w_s = sb("w", [P, 3, DC, P], F32)
        b_s = sb("b", [P, 3], F32)
        wo_s = sb("wo", [P, HP, D], F32)
        q2 = sb("q2", [P, 2, 2, S], F32R)
        k_own = sb("k_own", [P, 2, S], F32R)
        k2 = sb("k2", [P, 2, 2, 2, S], F32R)
        vT = sb("vT", [P, S], F32)
        V = sb("V", [P, 2, TPB, P], F32)
        Pr = sb("Pr", [P, 4, S], F32)
        PT = sb("PT", [P, 2, 2, TPB, S], F32)
        oT = sb("oT", [P, S], F32)
        nmax = sb("nmax", [P, 4], F32)
        rsum = sb("rsum", [P, 4], F32)
        rinv = sb("rinv", [P, 4], F32)
        ps = ctx.enter_context(nc.psum_tensor("at_ps", [P, 8, 512], F32))
        S_BANK, T_BANK, A_BANK, O_BANK, Y_BANK = 0, 2, 4, 6, 7
        s = sems(ctx, nc, "at", "w wo scaled q_ps qh ql k_ps kh kl k2 v_ps vT vturned V s_ps nmax exp rinv pn t_ps "
                 "pt_v pt_a pv oT y_ps x")
        w_dram = [W.rearrange("(c p) n -> p c n", p=P) for W in (Wq, Wk, Wv)]
        b_dram = [b.rearrange("(a p) -> p a", p=P) for b in (Bq, Bk, Bv)]
        wo_dram = Wo.rearrange("(a p) d -> p a d", p=P)
        LOADS = 6
        ON_ACT = (4, 5)
        BY_ACT = [sum(j in ON_ACT for j in range(n)) for n in range(NBL + 1)]
        BY_DVE = [n - BY_ACT[n] for n in range(NBL + 1)]

        def every_unit(eng, body, begin_pair=None):
            body(0, 0, first=True)
            with eng.Fori(0, HP - 1) as hp:
                if begin_pair:
                    begin_pair(hp)
                with eng.Fori(0, B // 2 - 2) as pair:
                    body(hp * B + pair * 2 + 1, 1)
                    body(hp * B + pair * 2 + 2, 0)
                body(hp * B + (B - 3), 1)
                body(hp * B + (B - 2), 0, switch=hp)
                body(hp * B + (B - 1), 1)
                body(hp * B + B, 0)
            with eng.Fori(0, B // 2 - 1) as pair:
                body(pair * 2 + (U - B + 1), 1)
                body(pair * 2 + (U - B + 2), 0)
            body(U - 1, 1, last=True)
            body(U, 0, drain=True)

        def wait_turned_copies(eng, u, n):
            eng.wait_ge(s["pt_v"], u * BY_DVE[NBL] + BY_DVE[n])
            if BY_ACT[n]:
                eng.wait_ge(s["pt_a"], u * BY_ACT[NBL] + BY_ACT[n])

        with nc.Block() as block:
            @block.sync
            def _(sp):
                def load_qkv(hp):
                    for k in range(3):
                        sp.dma_start(w_next[:, k, :, :], w_dram[k][:, :, ds(hp * P, P)]).then_inc(s["w"], 16)
                        sp.dma_start(b_next[:, k:k + 1], b_dram[k][:, ds(hp, 1)], allow_slow_non_contiguous=True
                                     ).then_inc(s["w"], 16)

                def double_keys(u, par):
                    sp.wait_ge(s["kh"], u + 1)
                    sp.wait_ge(s["kl"], u + 1)
                    for h in range(2):
                        for half in range(2):
                            sp.dma_start(k2[AD * half:AD * half + AD, par, h, :, :].bitcast(F32),
                                         k_own[AD * h:AD * h + AD, :, :].bitcast(F32)).then_inc(s["k2"], 16)

                load_qkv(0)
                sp.dma_start(wo_s[:, :, :], wo_dram).then_inc(s["wo"], 16)
                double_keys(0, 0)

                def body(u, par, first=False, last=False, switch=None, drain=False):
                    if drain or last:
                        return
                    double_keys(u + 1, 1 - par)

                def begin_pair(hp):
                    sp.wait_ge(s["scaled"], hp + 1)
                    load_qkv(hp + 1)
                every_unit(sp, body, begin_pair)

            @block.tensor
            def _(pe):
                def project(u, k):
                    src = xnT_all if k == 0 else ctxT_all
                    b = u % B
                    if k == 0:
                        pe.wait_ge(s["scaled"], u // B + 1)
                        pe.wait_ge(s["vT"], u)
                    elif k == 1:
                        pe.wait_ge(s["V"], u)
                    else:
                        pe.wait_ge(s["ql"], u + 1)
                    for d in range(DC):
                        ins = pe.matmul(ps[:, A_BANK + k % 2, :], w_s[:, k, d, :], src[:, d, ds(b * S, S)],
                                        start=d == 0, stop=d == DC - 1)
                    ins.then_inc(s[("q_ps", "k_ps", "v_ps")[k]], 1)

                def turn_values(u):
                    pe.wait_ge(s["vT"], u + 1)
                    pe.wait_ge(s["kl"], u + 1)
                    for t in range(TPB):
                        ins = pe.transpose(ps[:, A_BANK + 1, P * t:P * t + P], vT[:, P * t:P * t + P], c["ident"][:, :])
                    ins.then_inc(s["vturned"], 1)

                def score(u, par, j, first):
                    if j >= 2 or not first:
                        pe.wait_ge(s["exp"], NBL * u + j - 1)
                    if j == 0:
                        pe.wait_ge(s["ql"], u + 1)
                        pe.wait_ge(s["k2"], 64 * (u + 1))
                    h, q = j // TPB, P * (j % TPB)
                    for part in range(2):
                        ins = pe.matmul(ps[:, S_BANK + j % 2, :], q2[:, par, h, q:q + P], k2[:, par, h, part, :],
                                        start=part == 0, stop=part == 1)
                    ins.then_inc(s["s_ps"], 1)

                def turn(u, j, first=False):
                    pe.wait_ge(s["pn"], NBL * u + j + 1)
                    if j >= 2:
                        wait_turned_copies(pe, u, j - 1)
                    elif not first:
                        wait_turned_copies(pe, u - 1, NBL - 1 + j)
                    for t in range(TPB):
                        ins = pe.transpose(ps[:, T_BANK + j % 2, P * t:P * t + P], Pr[:, j % 4, P * t:P * t + P],
                                           c["ident"][:, :])
                    ins.then_inc(s["t_ps"], 1)

                def weigh_values(u, par, part):
                    if part == 0:
                        wait_turned_copies(pe, u, NBL)
                        pe.wait_ge(s["V"], u + 1)
                    for t in (2 * part, 2 * part + 1):
                        for h in range(2):
                            ins = pe.matmul(ps[AD * h:AD * h + AD, O_BANK, :], V[:, par, t, AD * h:AD * h + AD],
                                            PT[:, par, h, t, :], start=t == 0, stop=t == TPB - 1)
                    if part == 1:
                        ins.then_inc(s["pv"], 1)

                def output(u, half):
                    if half == 0:
                        pe.wait_ge(s["oT"], u + 1)
                        pe.wait_ge(s["wo"], 16)
                    for t in (2 * half, 2 * half + 1):
                        ins = pe.matmul(ps[:, Y_BANK - half, D * (t % 2):D * (t % 2) + D], oT[:, P * t:P * t + P],
                                        wo_s[:, ds(u // B, 1), :].rearrange("p a d -> p (a d)"), start=True, stop=True)
                    ins.then_inc(s["y_ps"], 1)

                def body(u, par, first=False, last=False, switch=None, drain=False):
                    for j in range(NBL):
                        if not drain:
                            score(u, par, j, first)
                        if j >= 2 and not drain:
                            turn(u, j - 2, first)
                        if j < 2 and not first:
                            turn(u - 1, NBL - 2 + j)
                        if j < 3 and not last and not drain:
                            project(u + 1, j)
                        if j in (3, 4) and not first:
                            weigh_values(u - 1, 1 - par, j - 3)
                        if j == 5 and not last and not drain:
                            turn_values(u + 1)
                        if j in (6, 7) and not first:
                            output(u - 1, j - 6)

                for k in range(3):
                    project(0, k)
                turn_values(0)
                every_unit(pe, body)

            @block.scalar
            def _(act):
                def queries(u, par):
                    act.wait_ge(s["q_ps"], u + 1)
                    for h in range(2):
                        own = slice(AD * h, AD * h + AD)
                        ins = act.activation(q2[own, par, h, :], ps[own, A_BANK, :], ACT.Identity, bias=b_s[own, 0:1])
                    ins.then_inc(s["qh"], 1)

                def keys(u):
                    act.wait_ge(s["k_ps"], u + 1)
                    if not (isinstance(u, int) and u == 0):
                        act.wait_ge(s["k2"], 64 * u)
                    act.activation(k_own[:, 0, :], ps[:, A_BANK + 1, :], ACT.Identity, bias=b_s[:, 1:2]
                                   ).then_inc(s["kh"], 1)

                def values(u):
                    act.wait_ge(s["v_ps"], u + 1)
                    act.wait_ge(s["vturned"], u)
                    act.activation(vT[:, :], ps[:, A_BANK, :], ACT.Identity, bias=b_s[:, 2:3]).then_inc(s["vT"], 1)

                def body(u, par, first=False, last=False, switch=None, drain=False):
                    ahead = not last and not drain
                    for j in range(NBL):
                        if j == 5 and not first:
                            act.wait_ge(s["pv"], u)
                            act.copy(oT[:, :], ps[:, O_BANK, :]).then_inc(s["oT"], 1)
                        if not drain:
                            act.wait_ge(s["nmax"], NBL * u + j + 1)
                            if not first or j > 3:
                                act.wait_ge(s["t_ps"], NBL * u + j - 3)
                            act.activation(Pr[:, j % 4, :], ps[:, S_BANK + j % 2, :], ACT.Exp,
                                           bias=nmax[:, j % 4:j % 4 + 1], accum_out=rsum[:, j % 4:j % 4 + 1]
                                           ).then_inc(s["exp"], 1)
                        if j == 0 and ahead:
                            queries(u + 1, 1 - par)
                        if j == 1 and ahead:
                            keys(u + 1)
                        if j == 2 and ahead:
                            values(u + 1)
                        if not drain and j - 2 in ON_ACT:
                            act.wait_ge(s["t_ps"], NBL * u + j - 1)
                            q = P * ((j - 2) % TPB)
                            act.copy(PT[:, par, (j - 2) // TPB, :, q:q + P],
                                     ps[:, T_BANK + j % 2, :].rearrange("p (t q) -> p t q", t=TPB)
                                     ).then_inc(s["pt_a"], 1)

                act.wait_ge(s["scaled"], 1)
                queries(0, 0)
                keys(0)
                values(0)
                every_unit(act, body)

            @block.gpsimd
            def _(pool):
                def body(u, par, first=False, last=False, switch=None, drain=False):
                    if drain:
                        return
                    for j in range(NBL):
                        wait_apart(pool, s["rinv"], NBL * u + j + 1)
                        pool.tensor_scalar(Pr[:, j % 4, :], Pr[:, j % 4, :], rinv[:, j % 4:j % 4 + 1], 1.0,
                                           ALU.mult, ALU.mult).then_inc(s["pn"], 1)
                every_unit(pool, body)

            @block.vector
            def _(dve):
                def queries(u, par):
                    dve.wait_ge(s["qh"], u + 1)
                    for h in range(2):
                        own, other = slice(AD * h, AD * h + AD), slice(AD - AD * h, 2 * AD - AD * h)
                        ins = dve.scalar_tensor_tensor(out=q2[other, par, h, :], in0=ps[own, A_BANK, :],
                                                       scalar=b_s[own, 0:1], in1=q2[own, par, h, :], op0=ALU.add,
                                                       op1=ALU.subtract)
                    ins.then_inc(s["ql"], 1)

                def keys(u):
                    dve.wait_ge(s["kh"], u + 1)
                    dve.scalar_tensor_tensor(out=k_own[:, 1, :], in0=ps[:, A_BANK + 1, :], scalar=b_s[:, 1:2],
                                             in1=k_own[:, 0, :], op0=ALU.add, op1=ALU.subtract).then_inc(s["kl"], 1)

                def values(u, par):
                    dve.wait_ge(s["vturned"], u + 1)
                    dve.tensor_copy(V[:, par, :, :], ps[:, A_BANK + 1, :].rearrange("p (t d) -> p t d", t=TPB)
                                    ).then_inc(s["V"], 1)

                def row_max(u, j):
                    dve.wait_ge(s["s_ps"], NBL * u + j + 1)
                    dve.tensor_reduce(nmax[:, j % 4:j % 4 + 1], ps[:, S_BANK + j % 2, :], AX.X, ALU.max, negate=True
                                      ).then_inc(s["nmax"], 1)

                def row_sum(u, j):
                    dve.wait_ge(s["exp"], NBL * u + j + 1)
                    dve.reciprocal(rinv[:, j % 4:j % 4 + 1], rsum[:, j % 4:j % 4 + 1]).then_inc(s["rinv"], 1)

                def keep(u, par, j):
                    if j in ON_ACT:
                        return
                    dve.wait_ge(s["t_ps"], NBL * u + j + 1)
                    q = P * (j % TPB)
                    dve.tensor_copy(PT[:, par, j // TPB, :, q:q + P],
                                    ps[:, T_BANK + j % 2, :].rearrange("p (t q) -> p t q", t=TPB)).then_inc(s["pt_v"], 1)

                def add_out(u, half):
                    dve.wait_ge(s["y_ps"], 2 * u + half + 1)
                    xv = x_all[:, ds((u % B) * TPB + 2 * half, 2), :].rearrange("p t d -> p (t d)")
                    dve.tensor_tensor(xv, ps[:, Y_BANK - half, :], xv, ALU.add).then_inc(s["x"], 1)

                def switch_weights(hp):
                    dve.wait_ge(s["w"], 16 * LOADS * (hp + 1))
                    dve.tensor_scalar(b_s[:, 0:1], b_next[:, 0:1], AD ** -0.5, None, ALU.mult)
                    dve.tensor_copy(b_s[:, 1:3], b_next[:, 1:3])
                    dve.tensor_scalar(w_s[:, 0, :, :], w_next[:, 0, :, :], AD ** -0.5, None, ALU.mult)
                    dve.tensor_copy(w_s[:, 1:3, :, :], w_next[:, 1:3, :, :]).then_inc(s["scaled"], 1)

                def body(u, par, first=False, last=False, switch=None, drain=False):
                    ahead = not last and not drain
                    for j in range(NBL):
                        if not drain:
                            if j >= 1:
                                row_sum(u, j - 1)
                            row_max(u, j)
                        if j >= 2 and not drain:
                            keep(u, par, j - 2)
                        if j < 2 and not first:
                            keep(u - 1, 1 - par, NBL - 2 + j)
                        if j == 1 and ahead:
                            queries(u + 1, 1 - par)
                        if j == 2 and ahead:
                            keys(u + 1)
                        if j == 6 and ahead:
                            values(u + 1, 1 - par)
                        if j == 7:
                            if not drain:
                                row_sum(u, j)
                            if not first:
                                add_out(u - 1, 0)
                                add_out(u - 1, 1)
                    if switch is not None:
                        dve.wait_ge(s["vT"], u + 2)
                        switch_weights(switch + 1)

                switch_weights(0)
                dve.wait_ge(s["scaled"], 1)
                queries(0, 0)
                keys(0)
                values(0, 0)
                every_unit(dve, body)


def logits(nc, c, landed, x_all, gate_w, rows, lg, out):
    with ExitStack() as ctx:
        sb = allocator(ctx, nc, "lo")
        tmp = norm_tmp(sb, 2)
        gw = sb("gw", [E, D], F32)
        gT = sb("gT", [P, DC, E], F32)
        xT = sb("xT", [P, 2, DC, S], F32)
        ps = ctx.enter_context(nc.psum_tensor("lo_ps", [P, 8, 512], F32))
        TURN_BANK, L_BANK, G_BANK = 0, 4, 6
        s = sems(ctx, nc, "lo", "gw gT_ps gT stats mv ve rstd xn turned xT l_ps lg stored0 stored1")

        def every_row(step):
            def looped(eng):
                step(0, 0)
                with eng.Fori(0, B // 2 - 1) as pair:
                    step(pair * 2 + 1, 1)
                    step(pair * 2 + 2, 0)
                step(B - 1, 1)
            return looped

        with nc.Block() as block:
            @block.sync
            def _(sp):
                rv = rows.rearrange("(b t p) d -> b p t d", p=P, t=TPB)

                def step(i, par):
                    sp.wait_ge(s["xn"], i + 1)
                    sp.dma_start(rv[ds(i, 1), :, :, 0:D].rearrange("a p t d -> p (a t) d"),
                                 tmp[par]["xn"][:, :, :]).then_inc(s[f"stored{par}"], 16)

                sp.dma_start(gw[:, :], gate_w).then_inc(s["gw"], 16)
                every_row(step)(sp)
                sp.dma_start(out[0:N, :].rearrange("(t p) d -> p t d", p=P), x_all[:, :, :]).then_inc(landed, 16)
                sp.dma_start(out[N:N + SPARE, :], c["zeros"][:, :]).then_inc(landed, 16)
                sp.wait_ge(s["stored0"], 16 * B // 2)
                sp.wait_ge(s["stored1"], 16 * B // 2)

            @block.gpsimd
            def _(pool):
                every_row(lambda i, par: norm_batch_pool(pool, s, i, tmp[par], c["minus_half"]))(pool)

            @block.vector
            def _(dve):
                def step(i, par):
                    def wait_free():
                        if not (isinstance(i, int) and i < 2):
                            dve.wait_ge(s["turned"], i - 1)
                            dve.wait_ge(s[f"stored{par}"], 16 * (i // 2))
                    if not (isinstance(i, int) and i == B - 1):
                        if not (isinstance(i, int) and i == 0):
                            wait_apart(dve, s["xn"], i)
                        norm_stats_dve(dve, s, i + 1, x_all, tmp[1 - par])
                    norm_apply_dve(dve, s, i, x_all, tmp[par], wait_free)

                dve.wait_ge(s["gT_ps"], 1)
                dve.tensor_copy(gT[:, :, :], ps[:, G_BANK, 0:DC * E].rearrange("p (k e) -> p k e", k=DC)
                                ).then_inc(s["gT"], 1)
                norm_stats_dve(dve, s, 0, x_all, tmp[0])
                step(0, 0)
                step(1, 1)
                with dve.Fori(1, B // 2 - 1) as pair:
                    step(pair * 2, 0)
                    step(pair * 2 + 1, 1)
                step(B - 2, 0)
                step(B - 1, 1)

            @block.tensor
            def _(pe):
                def turn(i, par):
                    pe.wait_ge(s["xn"], i + 1)
                    for k in range(DC):
                        for t in range(TPB):
                            ins = pe.transpose(ps[:, TURN_BANK + DC * par + k, P * t:P * t + P],
                                               tmp[par]["xn"][:, t, P * k:P * k + P], c["ident"][:, :])
                    ins.then_inc(s["turned"], 1)

                def map_gates(i, par):
                    pe.wait_ge(s["xT"], i + 1)
                    if not (isinstance(i, int) and i < 2):
                        pe.wait_ge(s["lg"], i - 1)
                    for t in range(TPB):
                        for k in range(DC):
                            ins = pe.matmul(ps[:, L_BANK + par, E * t:E * t + E], xT[:, par, k, P * t:P * t + P],
                                            gT[:, k, :], start=k == 0, stop=k == DC - 1)
                    ins.then_inc(s["l_ps"], 1)

                pe.wait_ge(s["gw"], 16)
                for k in range(DC):
                    ins = pe.transpose(ps[:, G_BANK, E * k:E * k + E], gw[:, P * k:P * k + P], c["ident"][0:E, 0:E])
                ins.then_inc(s["gT_ps"], 1)
                pe.wait_ge(s["gT"], 1)
                turn(0, 0)
                turn(1, 1)
                map_gates(0, 0)
                turn(2, 0)
                map_gates(1, 1)
                with pe.Fori(1, B // 2 - 1) as pair:
                    turn(pair * 2 + 1, 1)
                    map_gates(pair * 2, 0)
                    turn(pair * 2 + 2, 0)
                    map_gates(pair * 2 + 1, 1)
                turn(B - 1, 1)
                map_gates(B - 2, 0)
                map_gates(B - 1, 1)

            @block.scalar
            def _(act):
                def keep_turned(i, par):
                    act.wait_ge(s["turned"], i + 1)
                    for k in range(DC):
                        ins = act.copy(xT[:, par, k, :], ps[:, TURN_BANK + DC * par + k, :])
                    ins.then_inc(s["xT"], 1)

                def keep_logits(i, par):
                    act.wait_ge(s["l_ps"], i + 1)
                    act.copy(lg[:, ds(i * TPB, TPB), :],
                             ps[:, L_BANK + par, 0:TPB * E].rearrange("p (t e) -> p t e", e=E)).then_inc(s["lg"], 1)

                keep_turned(0, 0)
                with act.Fori(0, B // 2 - 1) as pair:
                    keep_turned(pair * 2 + 1, 1)
                    keep_logits(pair * 2, 0)
                    keep_turned(pair * 2 + 2, 0)
                    keep_logits(pair * 2 + 1, 1)
                keep_turned(B - 1, 1)
                keep_logits(B - 2, 0)
                keep_logits(B - 1, 1)


def router(nc, c, lg, rows, prob, final, chunk, slot):
    with ExitStack() as ctx:
        sb = allocator(ctx, nc, "ro")
        red = sb("red", [P, 3, NT], F32)
        pair_a = sb("pair_a", [P, NT, E, E], F32)
        before = sb("before", [P, NT, E], F32)
        rank = sb("rank", [P, NT, E], F32)
        sel = sb("sel", [P, NT, E], F32)
        key_e = sb("key", [P, E, NT], F32)
        key_rows = sb("key_rows", [P, 2, P], F32)
        below = sb("below", [P, 2, P], F32)
        T2 = sb("T2", [P, 2], F32)
        cand = sb("cand", [P, 2], F32)
        step = sb("step", [P, 2], F32)
        cnt2 = sb("cnt2", [P, 2], F32)
        T_diag = sb("T_diag", [P, E], F32)
        t1 = sb("t1", [P, NT, E], F32)
        t2 = sb("t2", [P, NT, E], F32)
        cnt = sb("cnt", [P, E], F32)
        cnt_b = sb("cnt_b", [P, E], BF16)
        T = sb("T", [P, E], F32)
        mask_b = sb("mask_b", [P, NT, E], BF16)
        tot = sb("tot", [P, E, NT], F32)
        offs = sb("offs", [P, E, NT + 1], F32)
        pos = sb("pos", [P, NT, E], F32)
        need = sb("need", [P, E], F32)
        ps = ctx.enter_context(nc.psum_tensor("ro_ps", [P, 4, 512], F32))
        s = sems(ctx, nc, "ro", "stored v key key_ps count found T_ps ones_mm pre_mm prob exp built")
        key = key_e[:, :, :].rearrange("p e t -> p t e")
        HALF = E // 2
        NE = NT * E

        def flat(a):
            return a[:, :, :].rearrange("p t e -> p (t e)")

        def over_e(a):
            return a.rearrange("p (t a) -> p t a", a=1).broadcast_to([P, NT, E])

        def over_t(a):
            return a.rearrange("p (a e) -> p a e", a=1).broadcast_to([P, NT, E])

        STEPS = list(range(2, -25, -1))
        with nc.Block() as block:
            @block.sync
            def _(sp):
                sp.wait_ge(s["prob"], 1)
                with nc.allow_non_contiguous_dma("8 probabilities per row"):
                    sp.dma_start(rows.rearrange("(t p) d -> p t d", p=P)[:, :, D:ROW], prob[:, :, :]).then_inc(s["stored"], 16)
                sp.wait_ge(s["stored"], 16)

            @block.scalar
            def _(act):
                act.wait_ge(s["v"], 2)
                act.activation(flat(lg), flat(lg), ACT.Exp).then_inc(s["exp"], 1)

            @block.tensor
            def _(pe):
                pe.wait_ge(s["key"], 1)
                for half in range(2):
                    ins = pe.transpose(ps[:, 2, P * half:P * half + P],
                                       key_e[:, HALF * half:HALF * half + HALF, :].rearrange("p e t -> p (e t)"),
                                       c["ident"][:, :])
                ins.then_inc(s["key_ps"], 1)
                for n in range(len(STEPS)):
                    pe.wait_ge(s["count"], n + 1)
                    pe.matmul(ps[:, 0, 0:2], c["group"][:, :], cnt2[:, :], start=True, stop=True
                              ).then_inc(s["found"], 1)
                pe.wait_ge(s["count"], len(STEPS) + 1)
                pe.matmul(ps[:, 2, 0:E], c["ones_row"][:, 0:P], T_diag[:, :], start=True, stop=True
                          ).then_inc(s["T_ps"], 1)
                pe.wait_ge(s["built"], 1)
                pe.matmul(ps[:, 0, 0:E], c["ones_bf"][:, :], cnt_b[:, :], start=True, stop=True).then_inc(s["ones_mm"], 1)
                for n in range(2):
                    pe.wait_ge(s["built"], 2 + n)
                    pe.matmul(ps[:, 1, 0:NE], c["lower_bf"][:, :], flat(mask_b), start=True, stop=True)
                    pe.matmul(ps[:, 3, 0:NE], c["ones_bf"][:, :], flat(mask_b), start=True, stop=True
                              ).then_inc(s["pre_mm"], 1)

            @block.vector
            def _(dve):
                n = [0]

                def v(ins):
                    n[0] += 1
                    ins.then_inc(s["v"], 1)
                    dve.wait_ge(s["v"], n[0])

                v(dve.tensor_reduce(red[:, 0, :], lg[:, :, :], AX.X, ALU.max))
                v(dve.tensor_tensor(lg[:, :, :], lg[:, :, :], over_e(red[:, 0, :]), ALU.subtract))
                dve.wait_ge(s["exp"], 1)
                v(dve.tensor_reduce(red[:, 1, :], lg[:, :, :], AX.X, ALU.add))
                v(dve.reciprocal(red[:, 2, :], red[:, 1, :]))
                dve.tensor_tensor(prob[:, :, :], lg[:, :, :], over_e(red[:, 2, :]), ALU.mult).then_inc(s["prob"], 1)
                dve.wait_ge(s["prob"], 1)
                pj = prob[:, :, :].rearrange("p t (a e) -> p t a e", a=1).broadcast_to([P, NT, E, E])
                for e in range(E):
                    own = prob[:, :, e:e + 1]
                    if e:
                        dve.tensor_tensor(pair_a[:, :, e, 0:e], prob[:, :, 0:e], own.broadcast_to([P, NT, e]), ALU.is_ge)
                    if e < E - 1:
                        ins = dve.tensor_tensor(pair_a[:, :, e, e + 1:E], prob[:, :, e + 1:E],
                                                own.broadcast_to([P, NT, E - 1 - e]), ALU.is_gt)
                    dve.memset(pair_a[:, :, e, e:e + 1], 0.0)
                v(dve.memset(T2[:, :], 0.0))
                v(dve.tensor_reduce(rank[:, :, :], pair_a[:, :, :, :], AX.X, ALU.add))
                v(dve.tensor_tensor(pair_a[:, :, :, :], pair_a[:, :, :, :], pj, ALU.mult))
                v(dve.tensor_reduce(before[:, :, :], pair_a[:, :, :, :], AX.X, ALU.add))
                v(dve.tensor_scalar(flat(sel), flat(before), 0.9, None, ALU.is_lt))
                v(dve.tensor_scalar(flat(rank), flat(rank), 1.0, None, ALU.add))
                v(dve.tensor_tensor(key, rank[:, :, :], prob[:, :, :], ALU.subtract))
                v(dve.tensor_tensor(key, key, sel[:, :, :], ALU.mult))
                v(dve.tensor_scalar(flat(t1), flat(sel), -FAR, FAR, ALU.mult, ALU.add))
                dve.tensor_tensor(key, key, t1[:, :, :], ALU.add).then_inc(s["key"], 1)
                dve.wait_ge(s["key"], 1)

                def count(which):
                    v(dve.tensor_tensor(t2[:, :, :], key, over_t(which), ALU.is_lt))
                    v(dve.tensor_reduce(cnt[:, :], t2[:, :, :].rearrange("p t e -> p e t"), AX.X, ALU.add))
                    dve.tensor_copy(cnt_b[:, :], cnt[:, :]).then_inc(s["built"], 1)

                dve.wait_ge(s["key_ps"], 1)
                v(dve.tensor_copy(key_rows[:, :, :], ps[:, 2, 0:2 * P].rearrange("p (a q) -> p a q", a=2)))
                for k, bit in enumerate(STEPS):
                    v(dve.tensor_scalar(cand[:, :], T2[:, :], 2.0 ** bit, None, ALU.add))
                    for half in range(2):
                        ins = dve.tensor_scalar(below[:, half, :], key_rows[:, half, :], cand[:, half:half + 1], 0.0,
                                                ALU.is_lt, ALU.add, accum_out=cnt2[:, half:half + 1])
                    ins.then_inc(s["count"], 1)
                    dve.wait_ge(s["found"], k + 1)
                    v(dve.tensor_scalar(step[:, :], ps[:, 0, 0:2], float(CAP), 2.0 ** bit, ALU.is_lt, ALU.mult))
                    v(dve.tensor_tensor(T2[:, :], T2[:, :], step[:, :], ALU.add))
                one = c["ident"][:, :].rearrange("p (g r) -> p g r", r=NT)[:, :, 0]
                for half in range(2):
                    ins = dve.tensor_scalar(T_diag[:, HALF * half:HALF * half + HALF], one, T2[:, half:half + 1], None,
                                            ALU.mult)
                ins.then_inc(s["count"], 1)
                dve.wait_ge(s["T_ps"], 1)
                v(dve.tensor_copy(T[:, :], ps[:, 2, 0:E]))
                count(T[:, :])
                dve.wait_ge(s["ones_mm"], 1)
                v(dve.tensor_scalar(need[:, :], ps[:, 0, 0:E], -1.0, float(CAP), ALU.mult, ALU.add))

                def ranks(k):
                    dve.wait_ge(s["pre_mm"], k + 1)
                    v(dve.tensor_copy(tot[:, :, :], ps[:, 3, 0:NE].rearrange("p (t e) -> p e t", e=E)))
                    for e in range(E):
                        ins = dve.tensor_tensor_scan(offs[:, e, 1:NT + 1], c["ones_row"][:, 0:NT], tot[:, e, :], 0.0,
                                                     ALU.mult, ALU.add)
                    v(ins)
                    v(dve.tensor_tensor(pos[:, :, :], ps[:, 1, 0:NE].rearrange("p (t e) -> p t e", e=E),
                                        offs[:, :, 0:NT].rearrange("p e t -> p t e"), ALU.add))

                v(dve.memset(offs[:, :, :], 0.0))
                v(dve.tensor_tensor(t1[:, :, :], key, over_t(T[:, :]), ALU.is_equal))
                dve.tensor_copy(flat(mask_b), flat(t1)).then_inc(s["built"], 1)
                ranks(0)
                v(dve.tensor_tensor(pos[:, :, :], pos[:, :, :], over_t(need[:, :]), ALU.is_lt))
                v(dve.tensor_tensor(t1[:, :, :], t1[:, :, :], pos[:, :, :], ALU.mult))
                v(dve.tensor_tensor(t1[:, :, :], t1[:, :, :], t2[:, :, :], ALU.add))
                v(dve.tensor_tensor(final[:, :, :], t1[:, :, :], sel[:, :, :], ALU.mult))
                dve.tensor_copy(flat(mask_b), flat(final)).then_inc(s["built"], 1)
                ranks(1)
                v(dve.tensor_scalar(flat(chunk), flat(pos), float(P), None, ALU.is_ge))
                for k in range(2, CT):
                    v(dve.tensor_scalar(flat(t1), flat(pos), float(P * k), None, ALU.is_ge))
                    v(dve.tensor_tensor(chunk[:, :, :], chunk[:, :, :], t1[:, :, :], ALU.add))
                v(dve.scalar_tensor_tensor(out=slot[:, :, :], in0=chunk[:, :, :], scalar=-float(P), in1=pos[:, :, :],
                                           op0=ALU.mult, op1=ALU.add))
                v(dve.tensor_scalar(flat(slot), flat(slot), 1.0, None, ALU.add))
                v(dve.tensor_tensor(slot[:, :, :], slot[:, :, :], final[:, :, :], ALU.mult))
                v(dve.tensor_scalar(flat(slot), flat(slot), -1.0, None, ALU.add))
                v(dve.tensor_scalar(c["spare"][:, :], c["part"][:, :], float(N), None, ALU.add))


def experts(nc, c, landed, rows, out, w1, w2, chunk, slot):
    EC = EF // P
    with ExitStack() as ctx:
        sb = allocator(ctx, nc, "ex")
        w1_in = sb("w1_in", [P, 2, EC, D], F32)
        w2_in = sb("w2_in", [P, 2, DC, EF], F32)
        w1T = sb("w1T", [P, 2, DC, EF], F32)
        w2T = sb("w2T", [P, 2, EC, D], F32)
        is_chunk = sb("is_chunk", [P, NT, CT], F32)
        onehot = sb("onehot", [P, 2, NT, P], BF16)
        number = sb("number", [P, 2, NT, 3, CT], BF16)
        sums = sb("sums", [P, 3, CT], F32)
        tok = sb("tok", [P, CT], F32)
        away = sb("away", [P, CT], F32)
        idx_get = sb("idx_get", [P, E, CT], I32)
        idx_put = sb("idx_put", [P, E, CT], I32)
        valid = sb("valid", [P, E, CT], F32)
        ix = sb("ix", [P, 2, 2, CT], I32)
        xg = sb("xg", [P, 2, CT, ROW], F32)
        sc = sb("sc", [P, CT], F32)
        xT = sb("xT", [P, 2, DC, CAP], F32)
        hT = sb("hT", [P, EC, CAP], F32)
        y = sb("y", [P, 2, CT, D], F32)
        ps = ctx.enter_context(nc.psum_tensor("ex_ps", [P, 8, 512], F32))
        W_BANK, SLOT_BANK, X_BANK, H_BANK, Y_BANK = 0, 1, 2, 4, 6
        s = sems(ctx, nc, "ex", "w0 w1 ix ix_put got0 got1 w_ps wT x_ps xT sc h_ps hT y_ps y put landed "
                 "chunk_of built slot_ps lists lists_v ids")

        def every_expert(eng, step):
            step(0, 0)
            with eng.Fori(0, E // 2 - 2) as pair:
                step(pair * 2 + 1, 1)
                step(pair * 2 + 2, 0)
            for e in range(E - 3, E):
                step(e, e % 2)

        def there(e):
            return not isinstance(e, int) or e < E

        def is_first(e):
            return isinstance(e, int) and e == 0

        def is_last(e):
            return isinstance(e, int) and e == E - 1

        with nc.Block() as block:
            @block.sync
            def _(sp):
                def load(e, par):
                    sp.dma_start(w1_in[:, par, :, :], w1[ds(e, 1)].rearrange("a (c p) d -> p (a c) d", p=P)
                                 ).then_inc(s[f"w{par}"], 16)
                    sp.dma_start(w2_in[:, par, :, :], w2[ds(e, 1)].rearrange("a (c p) f -> p (a c) f", p=P)
                                 ).then_inc(s[f"w{par}"], 16)

                load(0, 0)
                load(1, 1)
                with sp.Fori(1, E // 2) as pair:
                    for par in range(2):
                        e = pair * 2 + par
                        sp.wait_ge(s["w_ps"], 2 * (e - 1))
                        load(e, par)

            @block.gpsimd
            def _(pool):
                def gather(e, par):
                    if not (isinstance(e, int) and e < 2):
                        wait_apart(pool, s["x_ps"], e - 1)
                        wait_apart(pool, s["sc"], e - 1)
                    wait_apart(pool, s["ids"], e + 1)
                    pool.tensor_copy(ix[:, par, 0, :], idx_get[:, ds(e, 1), :].rearrange("p a t -> p (a t)")
                                     ).then_inc(s["ix"], 1)
                    wait_apart(pool, s["ix"], e + 1)
                    for t in range(CT):
                        pool.indirect_dma_start(
                            out=xg[:, par, t, :], out_offset=None, in_=rows,
                            in_offset=bass.IndirectOffsetOnAxis(ap=ix[:, par, 0, t:t + 1], axis=0)
                        ).then_inc(s[f"got{par}"], 16)

                def step(e, par):
                    if not is_last(e):
                        gather(e + 1, 1 - par)
                    if not is_first(e):
                        wait_apart(pool, s["put"], 16 * CT * e)
                    pool.sem_inc(s["landed"], 1)
                    pool.tensor_copy(ix[:, par, 1, :], idx_put[:, ds(e, 1), :].rearrange("p a t -> p (a t)")
                                     ).then_inc(s["ix_put"], 1)
                    wait_apart(pool, s["ix_put"], e + 1)
                    wait_apart(pool, s["y"], e + 1)
                    for t in range(CT):
                        pool.indirect_dma_start(
                            out=out, out_offset=bass.IndirectOffsetOnAxis(ap=ix[:, par, 1, t:t + 1], axis=0),
                            in_=y[:, par, t, :], in_offset=None, compute_op=ALU.add).then_inc(s["put"], 16)

                gather(0, 0)
                pool.wait_ge(landed, 32)
                every_expert(pool, step)
                pool.wait_ge(s["put"], 16 * CT * E)

            @block.tensor
            def _(pe):
                def turn_w1(e, par):
                    pe.wait_ge(s[f"w{par}"], 32 * (e // 2 + 1))
                    if not is_first(e):
                        pe.wait_ge(s["wT"], 2 * e)
                    for k in range(DC):
                        for f in range(EC):
                            ins = pe.transpose(ps[:, W_BANK, (k * EC + f) * P:(k * EC + f + 1) * P],
                                               w1_in[:, par, f, P * k:P * k + P], c["ident"][:, :])
                    ins.then_inc(s["w_ps"], 1)

                def turn_w2(e, par):
                    pe.wait_ge(s["wT"], 2 * e + 1)
                    for f in range(EC):
                        for k in range(DC):
                            ins = pe.transpose(ps[:, W_BANK, (f * DC + k) * P:(f * DC + k + 1) * P],
                                               w2_in[:, par, k, P * f:P * f + P], c["ident"][:, :])
                    ins.then_inc(s["w_ps"], 1)

                def sum_numbers(e, par):
                    pe.wait_ge(s["built"], e + 1)
                    if not is_first(e):
                        pe.wait_ge(s["lists"], e)
                    for t in range(NT):
                        ins = pe.matmul(ps[:, SLOT_BANK, 0:3 * CT], onehot[:, par, t, :],
                                        number[:, par, t, :, :].rearrange("p a c -> p (a c)"), start=t == 0,
                                        stop=t == NT - 1)
                    ins.then_inc(s["slot_ps"], 1)

                def turn_tokens(e, par):
                    pe.wait_ge(s[f"got{par}"], 16 * CT * (e // 2 + 1))
                    if not is_first(e):
                        pe.wait_ge(s["xT"], e)
                    for k in range(DC):
                        for t in range(CT):
                            ins = pe.transpose(ps[:, X_BANK + k, P * t:P * t + P], xg[:, par, t, P * k:P * k + P],
                                               c["ident"][:, :])
                    ins.then_inc(s["x_ps"], 1)

                def step(e, par):
                    if not is_last(e):
                        turn_w1(e + 1, 1 - par)
                    pe.wait_ge(s["wT"], 2 * e + 2)
                    pe.wait_ge(s["xT"], e + 1)
                    for f in range(EC):
                        for k in range(DC):
                            ins = pe.matmul(ps[:, H_BANK + f, :], w1T[:, par, k, P * f:P * f + P], xT[:, par, k, :],
                                            start=k == 0, stop=k == DC - 1)
                        ins.then_inc(s["h_ps"], 1)
                    if not is_last(e):
                        turn_w2(e + 1, 1 - par)
                    pe.wait_ge(s["hT"], EC * (e + 1))
                    if not is_first(e):
                        pe.wait_ge(s["y"], e)
                    for t in range(CT):
                        for f in range(EC):
                            ins = pe.matmul(ps[:, Y_BANK + t // 2, D * (t % 2):D * (t % 2) + D],
                                            hT[:, f, P * t:P * t + P], w2T[:, par, f, :], start=f == 0,
                                            stop=f == EC - 1)
                    ins.then_inc(s["y_ps"], 1)
                    if not is_last(e):
                        turn_tokens(e + 1, 1 - par)
                    if there(e + 2):
                        sum_numbers(e + 2, par)

                turn_w1(0, 0)
                turn_w2(0, 0)
                sum_numbers(0, 0)
                sum_numbers(1, 1)
                turn_tokens(0, 0)
                every_expert(pe, step)

            @block.scalar
            def _(act):
                def keep_w1(e, par):
                    act.wait_ge(s["w_ps"], 2 * e + 1)
                    act.copy(w1T[:, par, :, :], ps[:, W_BANK, :].rearrange("p (k f) -> p k f", k=DC)
                             ).then_inc(s["wT"], 1)

                def keep_w2(e, par):
                    act.wait_ge(s["w_ps"], 2 * e + 2)
                    act.copy(w2T[:, par, :, :], ps[:, W_BANK, :].rearrange("p (f d) -> p f d", f=EC)
                             ).then_inc(s["wT"], 1)

                def keep_tokens(e, par):
                    act.wait_ge(s["x_ps"], e + 1)
                    for k in range(DC):
                        ins = act.copy(xT[:, par, k, :], ps[:, X_BANK + k, :])
                    ins.then_inc(s["xT"], 1)

                def step(e, par):
                    if not is_last(e):
                        keep_w1(e + 1, 1 - par)
                    if not is_first(e):
                        act.wait_ge(s["y_ps"], e)
                    for f in range(EC):
                        act.wait_ge(s["h_ps"], EC * e + f + 1)
                        act.activation(hT[:, f, :], ps[:, H_BANK + f, :], ACT.Gelu).then_inc(s["hT"], 1)
                    if not is_last(e):
                        keep_w2(e + 1, 1 - par)
                        keep_tokens(e + 1, 1 - par)

                keep_w1(0, 0)
                keep_w2(0, 0)
                keep_tokens(0, 0)
                every_expert(act, step)

            @block.vector
            def _(dve):
                def build(e, par):
                    if not is_first(e):
                        dve.wait_ge(s["built"], e)
                    dve.tensor_tensor(is_chunk[:, :, :],
                                      c["slot"][:, 0:CT].rearrange("p (a q) -> p a q", a=1).broadcast_to([P, NT, CT]),
                                      chunk[:, :, ds(e, 1)].broadcast_to([P, NT, CT]), ALU.is_equal
                                      ).then_inc(s["chunk_of"], 1)
                    if not (isinstance(e, int) and e < 2):
                        dve.wait_ge(s["slot_ps"], e - 1)
                    dve.tensor_tensor(onehot[:, par, :, :],
                                      c["slot"][:, :].rearrange("p (a q) -> p a q", a=1).broadcast_to([P, NT, P]),
                                      slot[:, :, ds(e, 1)].broadcast_to([P, NT, P]), ALU.is_equal)
                    dve.wait_ge(s["chunk_of"], e + 1)
                    dve.tensor_tensor(number[:, par, :, 0, :], is_chunk[:, :, :],
                                      c["tile_no"][:, :].rearrange("p (t a) -> p t a", a=1).broadcast_to([P, NT, CT]),
                                      ALU.mult)
                    dve.tensor_scalar(number[:, par, :, 1, :], is_chunk[:, :, :], c["part"][:, 0:1], None, ALU.mult)
                    dve.tensor_copy(number[:, par, :, 2, :], is_chunk[:, :, :]).then_inc(s["built"], 1)

                def read(e):
                    LIST_STEPS = 4

                    def v(ins, k):
                        ins.then_inc(s["lists_v"], 1)
                        dve.wait_ge(s["lists_v"], LIST_STEPS * e + k)

                    def of_e(a):
                        return a[:, ds(e, 1), :].rearrange("p a t -> p (a t)")

                    dve.wait_ge(s["slot_ps"], e + 1)
                    dve.tensor_copy(sums[:, :, :], ps[:, SLOT_BANK, 0:3 * CT].rearrange("p (a k) -> p a k", a=3)
                                    ).then_inc(s["lists"], 1)
                    dve.wait_ge(s["lists"], e + 1)
                    v(dve.scalar_tensor_tensor(out=tok[:, :], in0=sums[:, 0, :], scalar=float(P), in1=sums[:, 1, :],
                                               op0=ALU.mult, op1=ALU.add), 1)
                    v(dve.tensor_copy(of_e(valid), sums[:, 2, :]), 2)
                    v(dve.tensor_scalar(away[:, :], sums[:, 2, :], -1.0, 1.0, ALU.mult, ALU.add), 3)
                    v(dve.tensor_copy(of_e(idx_get), tok[:, :]), 4)
                    dve.scalar_tensor_tensor(out=of_e(idx_put), in0=away[:, :], scalar=c["spare"][:, 0:1],
                                             in1=tok[:, :], op0=ALU.mult, op1=ALU.add).then_inc(s["ids"], 1)
                    dve.wait_ge(s["ids"], e + 1)

                def step(e, par):
                    if not is_first(e):
                        dve.wait_ge(s["y"], e)
                    dve.wait_ge(s[f"got{par}"], 16 * CT * (e // 2 + 1))
                    dve.tensor_tensor(sc[:, :], xg[:, par, :, ds(e + D, 1)].rearrange("p t a -> p (t a)"),
                                      valid[:, ds(e, 1), :].rearrange("p a t -> p (a t)"), ALU.mult
                                      ).then_inc(s["sc"], 1)
                    dve.wait_ge(s["sc"], e + 1)
                    dve.wait_ge(s["y_ps"], e + 1)
                    if not is_first(e):
                        dve.wait_ge(s["landed"], e)
                    for t in range(CT):
                        ins = dve.tensor_scalar(y[:, par, t, :],
                                                ps[:, Y_BANK + t // 2, D * (t % 2):D * (t % 2) + D],
                                                sc[:, t:t + 1], None, ALU.mult)
                    ins.then_inc(s["y"], 1)
                    if there(e + 2):
                        read(e + 2)
                    if there(e + 3):
                        build(e + 3, 1 - par)

                build(0, 0)
                read(0)
                build(1, 1)
                read(1)
                build(2, 0)
                every_expert(dve, step)


def build(nc, a, rows, gate_rows, max_rows, out):
    with ExitStack() as ctx:
        sb = allocator(ctx, nc, "k")
        x_all = sb("x", [P, NT, D], F32)
        c = {"ident": sb("ident", [P, P], F32), "sel": sb("sel", [MH, MH, P], F32), "lower": sb("lower", [P, P], F32),
             "lower_bf": sb("lower_bf", [P, P], BF16), "ones_row": sb("ones_row", [P, S], F32),
             "ones_bf": sb("ones_bf", [P, P], BF16), "minus_half": sb("minus_half", [P, 16], F32),
             "earlier": sb("earlier", [P, E, E], F32), "slot": sb("slot", [P, P], F32), "part": sb("part", [P, 1], F32),
             "tile_no": sb("tile_no", [P, NT], F32), "spare": sb("spare", [P, 1], F32), "group": sb("group", [P, P], F32),
             "zeros": sb("zeros", [P, D], F32)}
        landed = ctx.enter_context(nc.semaphore("k_landed"))
        setup(nc, c)
        with ExitStack() as mid:
            sbm = allocator(mid, nc, "m")
            ctxT_all = sbm("ctxT", [P, DC, N], F32)
            xnT_all = sbm("xnT", [P, DC, N], F32)
            with ExitStack() as mix:
                sbx = allocator(mix, nc, "mx")
                cols = sbx("cols", [P, 2, TPB, MH * B], F32)
                m = {"cols": cols, "w_row": sbx("w_row", [P, D], F32), "hs": sbx("hs", [P, 2, MH, TPB, MD + 1], F32),
                     "nrm": sbx("nrm", [P, 8, MH * TPB], F32), "hw": sbx("hw", [P, 2, MH * TPB, MD], F32),
                     "sq": sbx("sq", [P, MH * TPB, MD], F32)}
                s_fin = sems(mix, nc, "mf", "w hs fin fin_pow out")
                mlstm_gates(nc, c, a["x"], x_all, xnT_all, ctxT_all, cols, gate_rows, max_rows, a["ctx_1024"],
                            a["L0_xattn_ig_kernel"], a["L0_xattn_ig_bias"], a["L0_xattn_fg_kernel"],
                            a["L0_xattn_fg_bias"])
                mlstm_mix(nc, c, s_fin, m, x_all, xnT_all, ctxT_all, max_rows, a["ctx_1024"],
                          a["L0_xattn_outnorm_weight"])
                mlp(nc, c, s_fin, m, x_all, xnT_all, a["L0_ffn_w1"], a["L0_ffn_b1"], a["L0_ffn_w2"], a["L0_ffn_b2"],
                    a["L1_xattn_B_Output"])
            attention(nc, c, x_all, xnT_all, ctxT_all, a["L1_xattn_W_Query"], a["L1_xattn_W_Key"],
                      a["L1_xattn_W_Value"], a["L1_xattn_W_Output"], a["L1_xattn_B_Query"], a["L1_xattn_B_Key"],
                      a["L1_xattn_B_Value"])
        prob = sb("prob", [P, NT, E], F32)
        final = sb("final", [P, NT, E], F32)
        chunk = sb("token_chunk", [P, NT, E], F32)
        slot = sb("token_slot", [P, NT, E], F32)
        with ExitStack() as mid:
            lg = allocator(mid, nc, "r")("lg", [P, NT, E], F32)
            logits(nc, c, landed, x_all, a["L1_ffn_gate_w"], rows, lg, out)
            router(nc, c, lg, rows, prob, final, chunk, slot)
        experts(nc, c, landed, rows, out, a["L1_ffn_w1"], a["L1_ffn_w2"], chunk, slot)


_INS = ["x", "ctx_1024", "L0_xattn_ig_kernel", "L0_xattn_ig_bias", "L0_xattn_fg_kernel", "L0_xattn_fg_bias",
        "L0_xattn_outnorm_weight", "L0_ffn_w1", "L0_ffn_b1", "L0_ffn_w2", "L0_ffn_b2", "L1_xattn_W_Query",
        "L1_xattn_W_Key", "L1_xattn_W_Value", "L1_xattn_W_Output", "L1_xattn_B_Query", "L1_xattn_B_Key",
        "L1_xattn_B_Value", "L1_xattn_B_Output", "L1_ffn_gate_w", "L1_ffn_w1", "L1_ffn_w2"]


def kernel(**inputs):
    import numpy as np
    import concourse.bacc as bacc
    from concourse.bass_utils import run_bass_kernel_spmd as run

    nc = bacc.Bacc("TRN2", target_bir_lowering=False, num_devices=1)
    arrays, aps = {}, {}
    for name in _INS:
        arr = np.ascontiguousarray(inputs[name])
        arrays[f"in_{name}"] = arr
        aps[name] = nc.dram_tensor(f"in_{name}", arr.shape, mybir.dt.from_np(arr.dtype), kind="ExternalInput").ap()
    rows = nc.dram_tensor("rows", (N, ROW), F32, kind="Internal").ap()
    out = nc.dram_tensor("out_0", (N + SPARE, D), F32, kind="ExternalOutput").ap()
    gate_rows = nc.dram_tensor("gate_rows", (2, B, MH, S), F32, kind="Internal").ap()
    max_rows = nc.dram_tensor("max_rows", (B, MH, S), F32, kind="Internal").ap()
    build(nc, aps, rows, gate_rows, max_rows, out)
    r = run(nc, [arrays], core_ids=[0])
    return r.results[0]["out_0"][:N].reshape(B, S, D)
```
